# Optimizing a Trainium2 kernel written in Bass

```python
import numpy as np
import jax
import jax.numpy as jnp

def _softmax(x, axis=-1):
    return jax.nn.softmax(x, axis=axis)

def _gelu(x):
    return jax.nn.gelu(x, approximate=True)

def _silu(x):
    return jax.nn.silu(x)

def _sigmoid(x):
    return jax.nn.sigmoid(x)

def _layernorm(x, axis=-1, eps=1e-05):
    m = jnp.mean(x, axis=axis, keepdims=True)
    v = jnp.var(x, axis=axis, keepdims=True)
    return (x - m) / jnp.sqrt(v + eps)

def _scatter_add(tgt, idx, src, axis=0):
    return tgt.at[idx].add(src)

def _segment_sum(src, seg, n):
    return jax.ops.segment_sum(src, seg, n)
kernel_name = 'mk_macaron_d2_jaxref_r8_efad7d'

def setup_inputs(seed: int=0):
    np.random.seed(seed)
    _w = jnp.asarray

    def _L0_attn_setup():
        import jax, jax.numpy as jnp
        import numpy as np
        B, L, D = (4, 512, 256)
        EPS = 1e-05
        W_SCALE = 0.02

        def _hgrn_forward(x, Wi, Wf, Wg, g_norm_weight, Wo):
            i = jnp.einsum('bld,ed->ble', x, Wi)
            f = jnp.einsum('bld,ed->ble', x, Wf)
            gate = jax.nn.sigmoid(f)
            i_in = jax.nn.silu(i) * (1.0 - gate)

            def combine(c1, c2):
                a1, b1 = c1
                a2, b2 = c2
                return (a1 * a2, a2 * b1 + b2)
            _, o = jax.lax.associative_scan(combine, (gate, i_in), axis=1)
            g = jnp.einsum('bld,ed->ble', x, Wg)
            rms = jax.lax.rsqrt(jnp.mean(jnp.square(g), axis=-1, keepdims=True) + EPS)
            out = g * rms * g_norm_weight * (o * jax.nn.sigmoid(o))
            return jnp.einsum('ble,de->bld', out, Wo)
        key = jax.random.key(seed)
        kx, ki, kf, kg, ko = jax.random.split(key, 5)
        return {'hidden_states': jax.random.normal(kx, (B, L, D), dtype=jnp.float32), 'Wi': jax.random.normal(ki, (D, D), dtype=jnp.float32) * W_SCALE, 'Wf': jax.random.normal(kf, (D, D), dtype=jnp.float32) * W_SCALE, 'Wg': jax.random.normal(kg, (D, D), dtype=jnp.float32) * W_SCALE, 'g_norm_weight': jnp.ones((D,), dtype=jnp.float32), 'Wo': jax.random.normal(ko, (D, D), dtype=jnp.float32) * W_SCALE}
    _L0_attn_in = _L0_attn_setup()

    def _L0_ffn_setup():
        import jax, jax.numpy as jnp
        import numpy as np
        E = 8
        K = 2
        DIM = 256
        INTER = 176
        N_SHARED = 2
        STD = 0.02
        key = jax.random.key(seed)
        ks = jax.random.split(key, 9)
        B, S = (2, 256)
        return {'x': jax.random.normal(ks[0], (B, S, DIM), dtype=jnp.float32), 'gate_w': jax.random.normal(ks[1], (E, DIM), dtype=jnp.float32) * STD, 'router_bias': jnp.zeros((E,), dtype=jnp.float32), 'W1': jax.random.normal(ks[2], (E, DIM, INTER), dtype=jnp.float32) * STD, 'W3': jax.random.normal(ks[3], (E, DIM, INTER), dtype=jnp.float32) * STD, 'W2': jax.random.normal(ks[4], (E, INTER, DIM), dtype=jnp.float32) * STD, 'sw1': jax.random.normal(ks[5], (N_SHARED * INTER, DIM), dtype=jnp.float32) * STD, 'sw3': jax.random.normal(ks[6], (N_SHARED * INTER, DIM), dtype=jnp.float32) * STD, 'sw2': jax.random.normal(ks[7], (DIM, N_SHARED * INTER), dtype=jnp.float32) * STD}
    _L0_ffn_in = _L0_ffn_setup()

    def _L1_attn_setup():
        import jax, jax.numpy as jnp
        import numpy as np
        IN_FEATURES = 256
        HEAD_NUM = 64
        D = IN_FEATURES // HEAD_NUM
        SCALE = float(np.sqrt(D))
        key = jax.random.key(seed)
        ks = jax.random.split(key, 9)
        F = IN_FEATURES
        x = jax.random.normal(ks[0], (4, 128, F), dtype=jnp.float32)
        w = lambda k: jax.random.normal(k, (F, F), dtype=jnp.float32) * 0.02
        b = lambda k: jax.random.normal(k, (F,), dtype=jnp.float32) * 0.01
        return {'x': x, 'Wq': w(ks[1]), 'bq': b(ks[2]), 'Wk': w(ks[3]), 'bk': b(ks[4]), 'Wv': w(ks[5]), 'bv': b(ks[6]), 'Wo': w(ks[7]), 'bo': b(ks[8])}
    _L1_attn_in = _L1_attn_setup()

    def _L1_ffn_setup():
        import jax, jax.numpy as jnp
        import numpy as np
        B, S, H = (1, 128, 256)
        F = 128
        E = 16
        K = 2
        NS = 1
        ROUTE_SCALE = 1.0
        key = jax.random.key(seed)
        ks = jax.random.split(key, 8)

        def w(k, shape, fan_in):
            return jax.random.normal(k, shape, jnp.float32) * fan_in ** (-0.5)
        return {'hidden_states': jax.random.normal(ks[0], (B, S, H), jnp.float32), 'gate_w': w(ks[1], (H, E), H), 'expert_bias': jnp.zeros((E,), jnp.float32), 'shared_gate_w': w(ks[2], (H, F * NS), H), 'shared_up_w': w(ks[3], (H, F * NS), H), 'shared_down_w': w(ks[4], (F * NS, H), F * NS), 'experts_gate_up': w(ks[5], (E, H, 2 * F), H), 'experts_down': w(ks[6], (E, F, H), F)}
    _L1_ffn_in = _L1_ffn_setup()
    _d = {'L0_attn_hidden_states': _L0_attn_in['hidden_states'], 'L0_attn_Wi': _L0_attn_in['Wi'], 'L0_attn_Wf': _L0_attn_in['Wf'], 'L0_attn_Wg': _L0_attn_in['Wg'], 'L0_attn_g_norm_weight': _L0_attn_in['g_norm_weight'], 'L0_attn_Wo': _L0_attn_in['Wo'], 'L0_ffn_gate_w': _L0_ffn_in['gate_w'], 'L0_ffn_router_bias': _L0_ffn_in['router_bias'], 'L0_ffn_W1': _L0_ffn_in['W1'], 'L0_ffn_W3': _L0_ffn_in['W3'], 'L0_ffn_W2': _L0_ffn_in['W2'], 'L0_ffn_sw1': _L0_ffn_in['sw1'], 'L0_ffn_sw3': _L0_ffn_in['sw3'], 'L0_ffn_sw2': _L0_ffn_in['sw2'], 'L1_attn_Wq': _L1_attn_in['Wq'], 'L1_attn_bq': _L1_attn_in['bq'], 'L1_attn_Wk': _L1_attn_in['Wk'], 'L1_attn_bk': _L1_attn_in['bk'], 'L1_attn_Wv': _L1_attn_in['Wv'], 'L1_attn_bv': _L1_attn_in['bv'], 'L1_attn_Wo': _L1_attn_in['Wo'], 'L1_attn_bo': _L1_attn_in['bo'], 'L1_ffn_gate_w': _L1_ffn_in['gate_w'], 'L1_ffn_expert_bias': _L1_ffn_in['expert_bias'], 'L1_ffn_shared_gate_w': _L1_ffn_in['shared_gate_w'], 'L1_ffn_shared_up_w': _L1_ffn_in['shared_up_w'], 'L1_ffn_shared_down_w': _L1_ffn_in['shared_down_w'], 'L1_ffn_experts_gate_up': _L1_ffn_in['experts_gate_up'], 'L1_ffn_experts_down': _L1_ffn_in['experts_down']}
    _x0 = _d['L0_attn_hidden_states']
    _d['L0_attn_hidden_states'] = jax.random.normal(jax.random.fold_in(jax.random.key(seed), 1), (8, 256, 256), dtype=_x0.dtype)
    del _x0
    return _d

def reference(L0_attn_hidden_states, L0_attn_Wi, L0_attn_Wf, L0_attn_Wg, L0_attn_g_norm_weight, L0_attn_Wo, L0_ffn_gate_w, L0_ffn_router_bias, L0_ffn_W1, L0_ffn_W3, L0_ffn_W2, L0_ffn_sw1, L0_ffn_sw3, L0_ffn_sw2, L1_attn_Wq, L1_attn_bq, L1_attn_Wk, L1_attn_bk, L1_attn_Wv, L1_attn_bv, L1_attn_Wo, L1_attn_bo, L1_ffn_gate_w, L1_ffn_expert_bias, L1_ffn_shared_gate_w, L1_ffn_shared_up_w, L1_ffn_shared_down_w, L1_ffn_experts_gate_up, L1_ffn_experts_down):

    def _L0_attn_ref(hidden_states, Wi, Wf, Wg, g_norm_weight, Wo):
        import jax, jax.numpy as jnp
        import numpy as np
        B, L, D = (4, 512, 256)
        EPS = 1e-05
        W_SCALE = 0.02

        def _hgrn_forward(x, Wi, Wf, Wg, g_norm_weight, Wo):
            i = jnp.einsum('bld,ed->ble', x, Wi)
            f = jnp.einsum('bld,ed->ble', x, Wf)
            gate = jax.nn.sigmoid(f)
            i_in = jax.nn.silu(i) * (1.0 - gate)

            def combine(c1, c2):
                a1, b1 = c1
                a2, b2 = c2
                return (a1 * a2, a2 * b1 + b2)
            _, o = jax.lax.associative_scan(combine, (gate, i_in), axis=1)
            g = jnp.einsum('bld,ed->ble', x, Wg)
            rms = jax.lax.rsqrt(jnp.mean(jnp.square(g), axis=-1, keepdims=True) + EPS)
            out = g * rms * g_norm_weight * (o * jax.nn.sigmoid(o))
            return jnp.einsum('ble,de->bld', out, Wo)
        return _hgrn_forward(hidden_states, Wi, Wf, Wg, g_norm_weight, Wo)

    def _L0_ffn_ref(x, gate_w, router_bias, W1, W3, W2, sw1, sw3, sw2):
        import jax, jax.numpy as jnp
        import numpy as np
        E = 8
        K = 2
        DIM = 256
        INTER = 176
        N_SHARED = 2
        STD = 0.02
        B, S, D = x.shape
        X = x.reshape(-1, D)
        T = X.shape[0]
        logits = jnp.einsum('td,ed->te', X, gate_w)
        scores = jax.nn.sigmoid(logits)
        sel = scores + router_bias[None, :]
        _, idx = jax.lax.top_k(sel, K)
        w = jnp.take_along_axis(scores, idx, axis=1)
        w = w / jnp.clip(jnp.sum(w, axis=-1, keepdims=True), 1e-12)
        gate_full = jnp.zeros((T, E), dtype=w.dtype).at[jnp.arange(T)[:, None], idx].set(w)
        h1 = jnp.einsum('td,edh->eth', X, W1)
        h3 = jnp.einsum('td,edh->eth', X, W3)
        y = jnp.einsum('eth,ehd->etd', jax.nn.silu(h1) * h3, W2)
        out = jnp.einsum('etd,te->td', y, gate_full)
        shared = jnp.einsum('th,dh->td', jax.nn.silu(jnp.einsum('td,hd->th', X, sw1)) * jnp.einsum('td,hd->th', X, sw3), sw2)
        out = out + shared
        return out.reshape(B, S, D)

    def _L1_attn_ref(x, Wq, bq, Wk, bk, Wv, bv, Wo, bo):
        import jax, jax.numpy as jnp
        import numpy as np
        IN_FEATURES = 256
        HEAD_NUM = 64
        D = IN_FEATURES // HEAD_NUM
        SCALE = float(np.sqrt(D))
        B, S, F = x.shape
        d = D
        h = F // d
        q = x @ Wq + bq
        k = x @ Wk + bk
        v = x @ Wv + bv

        def to_heads(t):
            return t.reshape(B, S, d, h).transpose(0, 2, 1, 3)
        q, k, v = (to_heads(q), to_heads(k), to_heads(v))
        scores = jnp.einsum('bdsh,bdth->bdst', q, k) / SCALE
        weights = jax.nn.softmax(scores, axis=-1)
        feats = jnp.einsum('bdst,bdth->bdsh', weights, v)
        feats = feats.transpose(0, 2, 1, 3).reshape(B, S, F)
        return feats @ Wo + bo

    def _L1_ffn_ref(hidden_states, gate_w, expert_bias, shared_gate_w, shared_up_w, shared_down_w, experts_gate_up, experts_down):
        import jax, jax.numpy as jnp
        import numpy as np
        B, S, H = (1, 128, 256)
        F = 128
        E = 16
        K = 2
        NS = 1
        ROUTE_SCALE = 1.0
        b, s, h = hidden_states.shape
        x = hidden_states.reshape(-1, h)
        T = x.shape[0]
        router_logits = (x @ gate_w).astype(jnp.float32)
        scores = jax.nn.sigmoid(router_logits)
        _, selected = jax.lax.top_k(scores + expert_bias[None, :], K)
        top_scores = jnp.take_along_axis(scores, selected, axis=1)
        top_scores = top_scores / (top_scores.sum(-1, keepdims=True) + 1e-20)
        top_scores = top_scores * ROUTE_SCALE
        shared = jax.nn.silu(x @ shared_gate_w) * (x @ shared_up_w) @ shared_down_w
        comb = jnp.zeros((T, E), jnp.float32).at[jnp.arange(T)[:, None], selected].add(top_scores)
        routed = jnp.zeros_like(x)
        for e in range(E):
            gu = x @ experts_gate_up[e]
            g, u = jnp.split(gu, 2, axis=-1)
            routed = routed + comb[:, e:e + 1] * (jax.nn.silu(g) * u @ experts_down[e])
        return (shared + routed).reshape(b, s, h)
    x = L0_attn_hidden_states
    x = x + 0.5 * _L0_ffn_ref(_layernorm(x, axis=-1), L0_ffn_gate_w, L0_ffn_router_bias, L0_ffn_W1, L0_ffn_W3, L0_ffn_W2, L0_ffn_sw1, L0_ffn_sw3, L0_ffn_sw2)
    x = x + _L0_attn_ref(_layernorm(x, axis=-1), L0_attn_Wi, L0_attn_Wf, L0_attn_Wg, L0_attn_g_norm_weight, L0_attn_Wo)
    x = x + 0.5 * _L0_ffn_ref(_layernorm(x, axis=-1), L0_ffn_gate_w, L0_ffn_router_bias, L0_ffn_W1, L0_ffn_W3, L0_ffn_W2, L0_ffn_sw1, L0_ffn_sw3, L0_ffn_sw2)
    x = x + 0.5 * _L1_ffn_ref(_layernorm(x, axis=-1), L1_ffn_gate_w, L1_ffn_expert_bias, L1_ffn_shared_gate_w, L1_ffn_shared_up_w, L1_ffn_shared_down_w, L1_ffn_experts_gate_up, L1_ffn_experts_down)
    x = x + _L1_attn_ref(_layernorm(x, axis=-1), L1_attn_Wq, L1_attn_bq, L1_attn_Wk, L1_attn_bk, L1_attn_Wv, L1_attn_bv, L1_attn_Wo, L1_attn_bo)
    x = x + 0.5 * _L1_ffn_ref(_layernorm(x, axis=-1), L1_ffn_gate_w, L1_ffn_expert_bias, L1_ffn_shared_gate_w, L1_ffn_shared_up_w, L1_ffn_shared_down_w, L1_ffn_experts_gate_up, L1_ffn_experts_down)
    return x

_drawn_inputs = setup_inputs


def setup_inputs(seed=0):
    import zlib

    import numpy as np

    out = dict(_drawn_inputs(seed))
    spreads = {'L0_attn_g_norm_weight': (1.0, 0.6),
     'L0_ffn_router_bias': (0.0, 0.29),
     'L1_ffn_expert_bias': (0.0, 0.1)}
    factors = {'L0_attn_Wf': 2.974,
     'L1_attn_Wq': 4.654,
     'L1_attn_bq': 8.0,
     'L1_attn_Wk': 5.284,
     'L1_attn_bk': 8.0,
     'L1_attn_Wv': 3.592,
     'L1_attn_bv': 4.338,
     'L1_attn_Wo': 3.722,
     'L1_attn_bo': 2.69}
    for name, (base, spread) in spreads.items():
        noise = np.random.default_rng([zlib.crc32(name.encode()), seed]).standard_normal(out[name].shape)
        drawn = base * np.exp(spread * noise) if base else spread * noise
        out[name] = jnp.asarray(drawn.astype(out[name].dtype))
    for name, factor in factors.items():
        out[name] = (out[name] * factor).astype(out[name].dtype)
    return out
```

```python
import numpy as np
import concourse.bass as bass
from concourse import mybir
from contextlib import ExitStack

F32 = mybir.dt.float32
F16 = mybir.dt.float16
I32 = mybir.dt.int32
ALU = mybir.AluOpType
ACT = mybir.ActivationFunctionType
AX = mybir.AxisListType

P = 128
D = 256
KD = D // P
B, S = 8, 256
T = B * S
NTT = T // P
GT = 4
NG = NTT // GT
GW = GT * P
EPS = 1e-5
HEADS = 4
HD = D // HEADS
SCORE_SCALE = 0.5
BIG = 1.0e30


class Moe:

    def __init__(self, experts, hidden, shared):
        self.E, self.H, self.SH = experts, hidden, shared
        self.TILES = -(-(2 * T // P + experts - 1) // 4) * 4
        self.KH = [min(P, hidden - k) for k in range(0, hidden, P)]
        self.KS = [min(P, shared - k) for k in range(0, shared, P)]


MOE0 = Moe(8, 176, 352)
MOE1 = Moe(16, 128, 128)
MAXE = 16


def macaron_kernel(nc, a, out):
    ctx = ExitStack()
    with ctx:
        def sb(name, shape, dt=F32):
            return ctx.enter_context(nc.sbuf_tensor(name, shape, dt))

        def sem(name):
            return ctx.enter_context(nc.semaphore(name))

        X = sb("X", [P, NTT, D])
        XT = sb("XT", [P, KD, T])
        XN = sb("XN", [P, GT, D])
        ident = sb("ident", [P, P])
        ones = sb("ones", [P, P])
        ones16 = sb("ones16", [P, P], F16)
        before16 = sb("before16", [P, P], F16)
        iota = sb("iota", [P, P])
        tokens16 = sb("tokens16", [P, NTT], F16)
        epsc = sb("epsc", [P, 1])
        LAYERS = {}
        for n, m in (("f0", MOE0), ("f1", MOE1)):
            LAYERS[n] = dict(
                m=m,
                router=sb(n + "_router", [P, KD, m.E]),
                bias=sb(n + "_bias", [P, m.E]),
                w13=sb(n + "_w13", [P, KD, m.E, 2 * m.H]),
                w2=[sb(f"{n}_w2_{k}", [kp, m.E, D]) for k, kp in enumerate(m.KH)],
                s1=sb(n + "_s1", [P, KD, m.SH]),
                s3=sb(n + "_s3", [P, KD, m.SH]),
                s2=sb(n + "_s2", [P, len(m.KS), D]),
            )
        hw = {n: sb("h_" + n, [P, KD, D]) for n in ("wf", "wi", "wg", "wo")}
        hnorm = sb("h_norm", [P, KD])
        aw = {n: sb("a_" + n, [P, KD, D]) for n in ("wq", "wk", "wv", "wo")}
        abq = sb("a_bq", [P, KD])
        abk = sb("a_bk", [P, KD])
        abv = sb("a_bv", [P, D])
        abo = sb("a_bo", [P, D])

        st = sb("st", [P, GT, 6])
        mv = sb("mv", [P, GT, 2])
        sd = sb("sd", [P, GT])
        rs = sb("rs", [P, GT])
        ya = [sb(f"ya{q}", [P, D]) for q in range(4)]
        yb = [sb(f"yb{q}", [P, D]) for q in range(4)]
        wts = sb("wts", [P, 2, NTT])
        slots = sb("slots", [P, 2, NTT], I32)
        ARENA = 11072
        arena = sb("arena", [P, ARENA])

        class Carve:
            def __init__(self):
                self.at = 0

            def __call__(self, *shape, dt=F32, parts=P):
                size = 1
                for s in shape:
                    size *= s
                cols = -(-size * (2 if dt == F16 else 4) // 4)
                ap = arena[0:parts, self.at:self.at + cols]
                self.at += cols
                assert self.at <= ARENA, self.at
                if dt != F32:
                    ap = ap.bitcast(dt)
                if len(shape) == 1:
                    return ap
                names = "abcd"[:len(shape)]
                return ap.rearrange(f"p ({' '.join(names)}) -> p {' '.join(names)}",
                                    **{n: s for n, s in zip(names[1:], shape[1:])})

        c = Carve()
        lgT = c(GW)
        f_score = c(NTT * MAXE)
        f_sel = c(NTT * MAXE)
        f_tmp = c(NTT * MAXE)
        f_oh = [c(NTT * MAXE), c(NTT * MAXE)]
        f_m16 = c((NTT + 1) * MAXE, dt=F16)
        f_pos = c(NTT * MAXE)
        f_top = c(2, NTT)
        f_sum = c(NTT)
        f_slotf = c(2, NTT)
        f_hi = c(2, NTT, dt=I32)
        f_lo = c(2, NTT, dt=I32)
        f_hif = c(2, NTT)
        f_lof = c(2, NTT)
        f_cnt = c(MAXE, dt=I32)
        f_til = c(MAXE, dt=I32)
        f_tilf = c(MAXE)
        f_cum = c(MAXE)
        f_base = c(MAXE)
        shared_at = c.at
        f_lo16 = [c(NTT, P, dt=F16) for _ in range(2)]
        f_hi16 = [c(NTT, 48, dt=F16) for _ in range(2)]
        f_tok16 = [c(NTT, 48, dt=F16) for _ in range(2)]
        f_ge = c(48, MAXE, parts=1)
        marks_end, c.at = c.at, shared_at
        xs = [c(D) for _ in range(4)]
        xsT = [c(KD, P) for _ in range(2)]
        sg = [c(176) for _ in range(2)]
        hh = [c(176) for _ in range(2)]
        hT = [c(2, P) for _ in range(2)]
        ys = [c(D) for _ in range(4)]
        c.at = max(c.at, marks_end)
        f_rows = c(48, dt=I32)
        f_eidf = c(48, parts=1)
        f_eid = c(48, dt=I32, parts=1)
        f_sg = [c(GW) for _ in range(2)]
        f_HT = [c(3, GW) for _ in range(2)]
        c = Carve()
        g_keep = [c(GW) for _ in range(KD)]
        g_in = [c(GW) for _ in range(KD)]
        g_si = [c(GW) for _ in range(KD)]
        g_t1 = [c(GW) for _ in range(KD)]
        g_o = [c(GW) for _ in range(KD)]
        g_so = [c(GW) for _ in range(KD)]
        g_sq = [c(GW) for _ in range(KD)]
        g_gw = [c(GW) for _ in range(KD)]
        g_ms = c(GW)
        g_rms = c(GW)
        g_t = c(KD, GW)
        c = Carve()
        qz = c(HEADS, GW)
        kT = c(KD, GW)
        vz = c(GT, KD, 2 * P)
        pm = [c(2, S) for _ in range(2)]
        pT = [c(2, S) for _ in range(2)]
        fT = c(KD, GW)
        xTg = c(KD, GW)
        mx = [c(2) for _ in range(2)]
        nm = [c(2) for _ in range(2)]
        sm = [c(2) for _ in range(2)]
        ri = [c(2) for _ in range(2)]

        bank = [ctx.enter_context(nc.psum_tensor(f"bank{i}", [P, 512], F32)) for i in range(8)]

        xn_dram = nc.dram_tensor("xn_rows", (T, D), F32, kind="Internal").ap()
        y_drams = {n: nc.dram_tensor(n + "_expert_rows", (L["m"].TILES * P, D), F32, kind="Internal").ap()
                   for n, L in LAYERS.items()}

        x_in = [sem(f"x_in{g}") for g in range(NG)]
        loads = {}
        order = [("const", [(ident, a["ident"]), (ones, a["ones"]), (ones16, a["ones16"]),
                            (before16, a["before16"]), (iota, a["iota"]),
                            (tokens16, a["tokens16"])])]
        for n in ("f0", "h", "f1", "a"):
            if n in LAYERS:
                L = LAYERS[n]
                order.append((n + "_router", [(L["router"], a[n + "_router"]), (L["bias"], a[n + "_bias"])]))
                order.append((n + "_shared", [(L["s1"], a[n + "_s1"]), (L["s3"], a[n + "_s3"]), (L["s2"], a[n + "_s2"])]))
                k0 = 0
                w2 = []
                for k, kp in enumerate(L["m"].KH):
                    w2.append((L["w2"][k], a[n + "_w2"][k0:k0 + kp]))
                    k0 += kp
                order.append((n + "_experts", [(L["w13"], a[n + "_w13"])] + w2))
            elif n == "h":
                order.append(("h", [(hw[k], a["h_" + k]) for k in hw] + [(hnorm, a["h_norm"])]))
            else:
                order.append(("a", [(aw[k], a["a_" + k]) for k in aw]
                              + [(abq, a["a_bq"]), (abk, a["a_bk"]), (abv, a["a_bv"]), (abo, a["a_bo"])]))
        for name, parts in order:
            loads[name] = (sem("in_" + name), 16 * len(parts))

        def load_now(eng, k):
            name, parts = order[k]
            for dst, src in parts:
                full = dst[tuple(slice(None) for _ in dst.shape)]
                eng.dma_start(full, src).then_inc(loads[name][0], 16)

        def loaded(eng, name):
            eng.wait_ge(*loads[name])

        zero_q = sem("zero_q")
        eps_set = sem("eps_set")

        class Count:

            def __init__(self, of, start):
                self.sem, self.start = of, start

            def __call__(self, n):
                return self.sem, self.start + n

        made, left_at = {}, {}

        def count(name, total):
            if name not in made:
                made[name], left_at[name] = sem(name), 0
            got = Count(made[name], left_at[name])
            left_at[name] += total
            return got

        ROUTE_STEPS = 46

        def stage(number, kind, prev):
            totals = dict(stats=NTT, aggr=NG, stdev=NG, rstd=NG, xn=NTT, xT_psum=NTT, xT=NTT)
            mixes = kind in LAYERS
            lists = {}
            if mixes:
                m = LAYERS[kind]["m"]
                nk, tiles = len(m.KS), m.TILES
                totals |= dict(combined1=NTT, xn_stored=16 * NG, rl_psum=NG, rl_copied=NG, lg_psum=NG, scored=1,
                               route=ROUTE_STEPS, both=1, pos_psum=1, marks=2, map_psum=1, rows=1, experts=1,
                               up=NG * nk, silu=NG * nk, hid=NG * nk, down=NTT, shared_added=NTT)
                totals |= {k: tiles for k in ("r_xT_psum", "r_xT", "r_up", "r_silu", "r_hid", "r_hT_psum",
                                              "r_hT", "r_down", "r_y")}
                lists = dict(row_in=4 * tiles, y_out=4 * tiles, y_in=32 * NG)
            elif kind == "h":
                totals |= {k: KD * NG for k in ("f_psum", "i_psum", "g_psum", "keep", "in_", "si", "sq", "t1",
                                                "t2", "scan", "gw", "so", "t3", "t4", "t")}
                totals |= dict(ms_psum=NG, ms=NG, rms=NG, o_psum=NTT)
            else:
                totals |= dict(q_psum=KD * NG, q=4 * NG, k_psum=KD * NG, k=KD * NG, v_psum=2 * NG, v=4 * NG,
                               f_psum=8 * NG, fT=4 * NG, o_psum=NTT, bo=NTT, exp=16 * NG, pm=16 * NG)
                totals |= {k: 8 * NG for k in ("s_psum", "mx", "nm", "ri", "pT_psum", "pT")}
            got = {k: count(k, n) for k, n in totals.items()}
            got |= {k: [count(f"{k}{q}", n) for q in range(4)] for k, n in lists.items()}
            got |= dict(kind=kind, prev=prev, mixes=mixes, before_attention=False, x_new=count(f"x_new{number % 2}", NTT))
            return got

        stages, prev = [], None
        for number, kind in enumerate(["f0", "h", "f0", "f1", "a", "f1"]):
            if prev is not None:
                prev["before_attention"] = kind == "a"
            prev = stage(number, kind, prev)
            stages.append(prev)
        out_stored = sem("out_stored")

        def known(j):
            return isinstance(j, int)

        def after(j, n):
            return not known(j) or j >= n

        def rounds(eng, tiles, body):
            for j in range(6):
                body(j, j % 4, j // 4)
            with eng.Fori(0, (tiles - 8) // 4) as i:
                for u in range(6, 10):
                    body(4 * i + u, u % 4, i + u // 4)

        def groups(eng, body):
            body(0)
            with eng.Fori(1, NG) as g:
                body(g)

        block = ctx.enter_context(nc.Block())

        @block.sync
        def _(sp):
            x_dram = a["x"].rearrange("(g t p) d -> g p t d", g=NG, p=P)
            for g in range(NG):
                sp.dma_start(X[:, g * GT:(g + 1) * GT, :], x_dram[g]).then_inc(x_in[g], 16)
                if g == 0:
                    load_now(sp, 0)
            for k in range(1, len(order)):
                load_now(sp, k)

            for s in stages:
                if not s["mixes"]:
                    continue
                for g in range(NG):
                    sp.wait_ge(*s["xn"](GT * (g + 1)))
                    sp.dma_start(xn_dram[g * GW:(g + 1) * GW, :].rearrange("(t p) d -> p t d", p=P),
                                 XN[:, :, :]).then_inc(s["xn_stored"].sem, 16)

                def store_y(j, q, r):
                    sp.wait_ge(*s["r_y"](j + 1))
                    sp.dma_start(y_drams[s["kind"]][bass.ds(j * P, P), :], ys[q]).then_inc(s["y_out"][q].sem, 16)

                tiles = LAYERS[s["kind"]]["m"].TILES
                rounds(sp, tiles, store_y)
                for j in (tiles - 2, tiles - 1):
                    store_y(j, j % 4, j // 4)

            last = stages[-1]
            out_t = out.rearrange("(g t p) d -> g p t d", g=NG, p=P)
            for g in range(NG):
                sp.wait_ge(*last["x_new"](GT * (g + 1)))
                sp.dma_start(out_t[g], X[:, g * GT:(g + 1) * GT, :]).then_inc(out_stored, 16)
            sp.wait_ge(out_stored, 16 * NG)

        @block.gpsimd
        def _(pool):
            pool.memset(epsc[:, :], EPS).then_inc(eps_set, 1)

            def gather(dst, src, idx, done):
                pool.indirect_dma_start(out=dst, out_offset=None, in_=src,
                                        in_offset=bass.IndirectOffsetOnAxis(ap=idx, axis=0)).then_inc(done.sem, 16)

            for s in stages:
                if not s["mixes"]:
                    continue
                tiles = LAYERS[s["kind"]]["m"].TILES
                pool.wait_ge(*s["xn_stored"](16 * NG))
                pool.wait_ge(*s["rows"](1))
                for j in range(tiles):
                    if j >= 4:
                        pool.wait_ge(*s["r_xT_psum"](j - 3))
                    gather(xs[j % 4], xn_dram, f_rows[:, j:j + 1], s["row_in"][j % 4])
                for q in range(4):
                    pool.wait_ge(*s["y_out"][q](16 * tiles // 4))
                for i in range(NTT):
                    if i == 4 and s["before_attention"]:
                        pool.memset(qz, 0.0).then_inc(zero_q, 1)
                        pool.memset(vz, 0.0).then_inc(zero_q, 1)
                    if i >= 4:
                        pool.wait_ge(*s["x_new"](i - 3))
                    gather(ya[i % 4][:, :], y_drams[s["kind"]], slots[:, 0, i:i + 1], s["y_in"][i % 4])
                    gather(yb[i % 4][:, :], y_drams[s["kind"]], slots[:, 1, i:i + 1], s["y_in"][i % 4])

        @block.scalar
        def _(act):
            act.wait_ge(eps_set, 1)

            def stdev(s, g):
                act.wait_ge(*s["aggr"](g + 1))
                act.activation(sd[:, :], mv[:, :, 1], ACT.Sqrt, bias=epsc[:, :]).then_inc(s["stdev"].sem, 1)

            def copy_xT(s, g, t):
                act.wait_ge(*s["xT_psum"](GT * g + t + 1))
                to = xTg[:, :, t * P:(t + 1) * P] if s["kind"] == "a" else XT[:, :, bass.ds((GT * g + t) * P, P)]
                act.activation(to,
                               bank[t % 2][:, 0:D].rearrange("p (k n) -> p k n", k=KD),
                               ACT.Copy).then_inc(s["xT"].sem, 1)

            def mixture(s):
                L = LAYERS[s["kind"]]
                m = L["m"]
                nk = len(m.KS)
                for g in range(NG):
                    stdev(s, g)
                    for t in range(GT):
                        copy_xT(s, g, t)
                    act.wait_ge(*s["rl_psum"](g + 1))
                    act.activation(lgT[0:m.E, :], bank[5][0:m.E, :], ACT.Copy).then_inc(s["rl_copied"].sem, 1)
                act.wait_ge(*s["lg_psum"](NG))
                act.activation(f_score[:, 0:NTT * m.E], bank[4][:, 0:NTT * m.E], ACT.Sigmoid).then_inc(s["scored"].sem, 1)
                for n in range(NG * nk):
                    kp = m.KS[n % nk]
                    act.wait_ge(*s["up"](n + 1))
                    if n >= 2:
                        act.wait_ge(*s["hid"](n - 1))
                    act.activation(f_sg[n % 2][0:kp, :], bank[2 + n % 2][0:kp, :], ACT.Silu).then_inc(s["silu"].sem, 1)

                def xT(j, q, r):
                    act.wait_ge(*s["r_xT_psum"](j + 1))
                    if after(j, 2):
                        act.wait_ge(*s["r_up"](j - 1))
                    act.activation(xsT[q % 2], bank[q % 2][:, 0:D].rearrange("p (k n) -> p k n", k=KD),
                                   ACT.Copy).then_inc(s["r_xT"].sem, 1)

                def silu(j, q, r):
                    act.wait_ge(*s["r_up"](j + 1))
                    if after(j, 2):
                        act.wait_ge(*s["r_hid"](j - 1))
                    act.activation(sg[q % 2][:, 0:m.H], bank[2 + q % 2][:, 0:m.H], ACT.Silu).then_inc(s["r_silu"].sem, 1)

                def y(j, q, r):
                    act.wait_ge(*s["r_down"](j + 1))
                    if after(j, 4):
                        act.wait_ge(*s["y_out"][q](16 * r))
                    act.activation(ys[q], bank[6 + q % 2][:, 0:D], ACT.Copy).then_inc(s["r_y"].sem, 1)

                def step(j, q, r):
                    if not known(j) or j < m.TILES:
                        silu(j, q, r)
                    if after(j, 2):
                        y(j - 2, (q + 2) % 4, r if q >= 2 else r - 1)
                    if not known(j) or j + 1 < m.TILES:
                        xT(j + 1, (q + 1) % 4, r if q < 3 else r + 1)

                xT(0, 0, 0)
                rounds(act, m.TILES, step)
                for j in range(m.TILES - 2, m.TILES + 2):
                    step(j, j % 4, j // 4)

            def recurrence(s):
                def first(g):
                    for c in range(KD):
                        n = KD * g + c
                        act.wait_ge(*s["f_psum"](n + 1))
                        if after(g, 1):
                            act.wait_ge(*s["scan"](n - KD + 1))
                        act.activation(g_keep[c], bank[2][:, :], ACT.Sigmoid).then_inc(s["keep"].sem, 1)
                        act.activation(g_in[c], bank[2][:, :], ACT.Sigmoid, scale=-1.0).then_inc(s["in_"].sem, 1)
                        act.wait_ge(*s["i_psum"](n + 1))
                        act.activation(g_si[c], bank[3][:, :], ACT.Sigmoid).then_inc(s["si"].sem, 1)
                        act.wait_ge(*s["g_psum"](n + 1))
                        if after(g, 1):
                            act.wait_ge(*s["ms_psum"](g))
                        act.activation(g_sq[c], bank[4][:, :], ACT.Square).then_inc(s["sq"].sem, 1)
                    act.wait_ge(*s["ms_psum"](g + 1))
                    if after(g, 1):
                        act.wait_ge(*s["rms"](g))
                    act.activation(g_ms, bank[5][:, :], ACT.Sqrt, scale=1.0 / D, bias=epsc[:, :]).then_inc(s["ms"].sem, 1)

                def second(g):
                    for c in range(KD):
                        n = KD * g + c
                        act.wait_ge(*s["scan"](n + 1))
                        if after(g, 1):
                            act.wait_ge(*s["t"](n - KD + 1))
                        act.activation(g_so[c], g_o[c], ACT.Sigmoid).then_inc(s["so"].sem, 1)

                def group(g):
                    stdev(s, g + 1)
                    first(g)
                    for t in range(GT):
                        copy_xT(s, g + 1, t)
                    second(g)

                stdev(s, 0)
                for t in range(GT):
                    copy_xT(s, 0, t)
                group(0)
                with act.Fori(1, NG - 1) as g:
                    group(g)
                first(NG - 1)
                second(NG - 1)

            def attention(s):
                def group(g):
                    stdev(s, g)
                    for t in range(GT):
                        copy_xT(s, g, t)
                    if known(g):
                        act.wait_ge(zero_q, 2)
                    for c in range(KD):
                        act.wait_ge(*s["q_psum"](KD * g + c + 1))
                        if after(g, 1):
                            act.wait_ge(*s["s_psum"](8 * g))
                        for p in range(2):
                            r = slice(p * HD, (p + 1) * HD)
                            act.activation(qz[r, 2 * c + p, :], bank[2 + c][r, :], ACT.Identity,
                                           bias=abq[r, c:c + 1]).then_inc(s["q"].sem, 1)
                    for u in range(8 + 3):
                        if u < 8:
                            n = 8 * g + u
                            act.wait_ge(*s["nm"](n + 1))
                            if after(g, 1) or u >= 2:
                                act.wait_ge(*s["pT_psum"](n - 1))
                            for h in range(2):
                                act.activation(pm[u % 2][:, h, :], bank[2 + u % 2][:, h * S:(h + 1) * S], ACT.Exp,
                                               scale=SCORE_SCALE, bias=nm[u % 2][:, h:h + 1],
                                               accum_out=sm[u % 2][:, h:h + 1]).then_inc(s["exp"].sem, 1)
                        if u >= 2 and u - 2 < 8:
                            n = 8 * g + u - 2
                            act.wait_ge(*s["pT_psum"](n + 1))
                            if after(g, 1) or u - 2 >= 2:
                                act.wait_ge(*s["f_psum"](n - 1))
                            act.activation(pT[u % 2], bank[4 + u % 2][:, :].rearrange("p (k n) -> p k n", k=2),
                                           ACT.Copy).then_inc(s["pT"].sem, 1)
                        if u >= 3 and (u - 3) % 2 == 1:
                            v = u - 3
                            c = (v // 2) % 2
                            act.wait_ge(*s["f_psum"](8 * g + v + 1))
                            if after(g, 1):
                                act.wait_ge(*s["o_psum"](GT * g))
                            act.activation(fT[:, c, (v // 4) * S:(v // 4 + 1) * S], bank[6 + c][:, 0:S],
                                           ACT.Copy).then_inc(s["fT"].sem, 1)

                groups(act, group)

            for s in stages:
                if s["mixes"]:
                    mixture(s)
                elif s["kind"] == "h":
                    recurrence(s)
                else:
                    attention(s)

        @block.tensor
        def _(pe):
            loaded(pe, "const")

            def transpose_x(s, g, t):
                i = GT * g + t
                pe.wait_ge(*s["xn"](i + 1))
                if after(g, 1) or t >= 2:
                    pe.wait_ge(*s["xT"](i - 1))
                for k in range(KD):
                    last = pe.transpose(bank[t % 2][:, k * P:(k + 1) * P], XN[:, t, k * P:(k + 1) * P], ident[:, :])
                last.then_inc(s["xT_psum"].sem, 1)

            def mixture(s):
                L = LAYERS[s["kind"]]
                m = L["m"]
                E, nk = m.E, len(m.KS)

                def logits_back(g):
                    pe.wait_ge(*s["rl_copied"](g + 1))
                    for t in range(GT):
                        i = GT * g + t
                        last = pe.transpose(bank[4][:, i * E:(i + 1) * E], lgT[0:E, t * P:(t + 1) * P], ident[0:E, 0:E])
                    last.then_inc(s["lg_psum"].sem, 1)

                loaded(pe, s["kind"] + "_router")
                for g in range(NG):
                    for t in range(GT):
                        transpose_x(s, g, t)
                    if g:
                        logits_back(g - 1)
                    pe.wait_ge(*s["xT"](GT * (g + 1)))
                    for k in range(KD):
                        last = pe.matmul(bank[5][0:E, :], L["router"][:, k, :], XT[:, k, g * GW:(g + 1) * GW],
                                         start=(k == 0), stop=(k == KD - 1))
                    last.then_inc(s["rl_psum"].sem, 1)
                logits_back(NG - 1)

                loaded(pe, s["kind"] + "_shared")
                pe.wait_ge(*s["scored"](1))

                def shared_up(g):
                    for c, kp in enumerate(m.KS):
                        n = nk * g + c
                        if n >= 2:
                            pe.wait_ge(*s["hid"](n - 1))
                        for w, b in ((L["s1"], 2), (L["s3"], 4)):
                            for k in range(KD):
                                last = pe.matmul(bank[b + n % 2][0:kp, :], w[:, k, c * P:c * P + kp],
                                                 XT[:, k, g * GW:(g + 1) * GW], start=(k == 0), stop=(k == KD - 1))
                        last.then_inc(s["up"].sem, 1)

                def shared_down(g):
                    pe.wait_ge(*s["hid"](nk * (g + 1)))
                    for t in range(GT):
                        i = GT * g + t
                        if i >= 2:
                            pe.wait_ge(*s["shared_added"](i - 1))
                        for c, kp in enumerate(m.KS):
                            last = pe.matmul(bank[6 + i % 2][:, 0:D], f_HT[g % 2][0:kp, c, t * P:(t + 1) * P],
                                             L["s2"][0:kp, c, :], start=(c == 0), stop=(c == nk - 1))
                        last.then_inc(s["down"].sem, 1)

                def positions():
                    pe.wait_ge(*s["both"](1))
                    pos = bank[0][:, 0:(NTT + 1) * E]
                    marks = f_m16[:, 0:(NTT + 1) * E]
                    pe.matmul(pos, before16[:, :], marks, start=True, stop=False, skip_group_check=True)
                    for i in range(NTT):
                        n = NTT - i
                        last = pe.matmul(pos[:, (i + 1) * E:].rearrange("p (t e) -> p t e", e=E), ones16[:, :],
                                         marks[:, i * E:(i + 1) * E].unsqueeze(1).broadcast_to((P, n, E)),
                                         start=False, stop=(i == NTT - 1), skip_group_check=True)
                    last.then_inc(s["pos_psum"].sem, 1)

                def slot_tokens():
                    pe.wait_ge(*s["marks"](2))
                    for n in range(2 * NTT):
                        k, i = n // NTT, n % NTT
                        last = pe.matmul(bank[1][:, 0:m.TILES], f_lo16[k][:, i, :], f_tok16[k][:, i, 0:m.TILES],
                                         start=(n == 0), stop=(n == 2 * NTT - 1))
                    last.then_inc(s["map_psum"].sem, 1)

                shared_up(0)
                positions()
                shared_up(1)
                shared_down(0)
                slot_tokens()
                shared_up(2)
                shared_down(1)
                shared_up(3)
                shared_down(2)
                shared_down(3)

                def xT(j, q, r):
                    pe.wait_ge(*s["row_in"][q](16 * (r + 1)))
                    if after(j, 2):
                        pe.wait_ge(*s["r_xT"](j - 1))
                    for k in range(KD):
                        last = pe.transpose(bank[q % 2][:, k * P:(k + 1) * P], xs[q][:, k * P:(k + 1) * P], ident[:, :])
                    last.then_inc(s["r_xT_psum"].sem, 1)

                def expert(j):
                    return pe.value_load(f_eid[0:1, bass.ds(j, 1)], min_val=0, max_val=E - 1)

                def up(j, q, r):
                    e = expert(j)
                    pe.wait_ge(*s["r_xT"](j + 1))
                    if after(j, 2):
                        pe.wait_ge(*s["r_hid"](j - 1))
                    for k in range(KD):
                        last = pe.matmul(bank[2 + q % 2][:, 0:2 * m.H], xsT[q % 2][:, k, :],
                                         L["w13"][:, k, bass.ds(e, 1), :], start=(k == 0), stop=(k == KD - 1))
                    last.then_inc(s["r_up"].sem, 1)

                def hid(j, q, r):
                    pe.wait_ge(*s["r_hid"](j + 1))
                    if after(j, 2):
                        pe.wait_ge(*s["r_hT"](j - 1))
                    for k, kp in enumerate(m.KH):
                        last = pe.transpose(bank[4 + q % 2][0:kp, k * P:(k + 1) * P],
                                            hh[q % 2][:, k * P:k * P + kp], ident[:, :])
                    last.then_inc(s["r_hT_psum"].sem, 1)

                def down(j, q, r):
                    e = expert(j)
                    pe.wait_ge(*s["r_hT"](j + 1))
                    if after(j, 2):
                        pe.wait_ge(*s["r_y"](j - 1))
                    for k, kp in enumerate(m.KH):
                        last = pe.matmul(bank[6 + q % 2][:, 0:D], hT[q % 2][0:kp, k, :],
                                         L["w2"][k][:, bass.ds(e, 1), :], start=(k == 0), stop=(k == len(m.KH) - 1))
                    last.then_inc(s["r_down"].sem, 1)

                def step(j, q, r):
                    if not known(j) or j < m.TILES:
                        up(j, q, r)
                    if after(j, 1) and (not known(j) or j - 1 < m.TILES):
                        hid(j - 1, (q + 3) % 4, None)
                    if after(j, 2):
                        down(j - 2, (q + 2) % 4, None)
                    if not known(j) or j + 1 < m.TILES:
                        xT(j + 1, (q + 1) % 4, r if q < 3 else r + 1)

                loaded(pe, s["kind"] + "_experts")
                pe.wait_ge(*s["experts"](1))
                xT(0, 0, 0)
                rounds(pe, m.TILES, step)
                for j in range(m.TILES - 2, m.TILES + 2):
                    step(j, j % 4, j // 4)

            def recurrence(s):
                loaded(pe, "h")

                def project(g):
                    pe.wait_ge(*s["xT"](GT * (g + 1)))
                    for c in range(KD):
                        n = KD * g + c
                        for w, b, psum, used in (("wf", 2, s["f_psum"], s["in_"]), ("wi", 3, s["i_psum"], s["t1"]),
                                                 ("wg", 4, s["g_psum"], s["gw"])):
                            if after(g, 1) or c:
                                pe.wait_ge(*used(n))
                            for k in range(KD):
                                last = pe.matmul(bank[b][:, :], hw[w][:, k, c * P:(c + 1) * P],
                                                 XT[:, k, bass.ds(g * GW, GW)], start=(k == 0), stop=(k == KD - 1))
                            last.then_inc(psum.sem, 1)

                def squares(g):
                    if after(g, 1):
                        pe.wait_ge(*s["ms"](g))
                    for c in range(KD):
                        pe.wait_ge(*s["sq"](KD * g + c + 1))
                        last = pe.matmul(bank[5][:, :], ones[:, :], g_sq[c], start=(c == 0), stop=(c == KD - 1))
                    last.then_inc(s["ms_psum"].sem, 1)

                def project_out(g):
                    pe.wait_ge(*s["t"](KD * (g + 1)))
                    for t in range(GT):
                        i = GT * g + t
                        if after(g, 1) or t >= 2:
                            pe.wait_ge(*s["x_new"](i - 1))
                        for c in range(KD):
                            last = pe.matmul(bank[6 + t % 2][:, 0:D], g_t[:, c, t * P:(t + 1) * P], hw["wo"][:, c, :],
                                             start=(c == 0), stop=(c == KD - 1))
                        last.then_inc(s["o_psum"].sem, 1)

                def group(g):
                    for t in range(GT):
                        transpose_x(s, g, t)
                    project(g)
                    squares(g)

                group(0)
                for t in range(GT):
                    transpose_x(s, 1, t)
                project(1)
                squares(1)
                project_out(0)
                with pe.Fori(2, NG) as g:
                    group(g)
                    project_out(g - 1)
                project_out(NG - 1)

            def attention(s):
                loaded(pe, "a")

                def group(g):
                    for t in range(GT):
                        transpose_x(s, g, t)
                    pe.wait_ge(*s["xT"](GT * (g + 1)))
                    if after(g, 1):
                        pe.wait_ge(*s["fT"](4 * g))
                        pe.wait_ge(*s["exp"](16 * g))
                        pe.wait_ge(*s["pT"](8 * g))
                    for w, b, psum in (("wq", 2, s["q_psum"]), ("wk", 4, s["k_psum"])):
                        for c in range(KD):
                            for k in range(KD):
                                last = pe.matmul(bank[b + c][:, :], aw[w][:, k, c * P:(c + 1) * P],
                                                 xTg[:, k, :], start=(k == 0), stop=(k == KD - 1))
                            last.then_inc(psum.sem, 1)
                    for t in range(GT):
                        for k in range(KD):
                            last = pe.matmul(bank[6 + t // 2][:, (t % 2) * D:(t % 2 + 1) * D], xTg[:, k, t * P:(t + 1) * P],
                                             aw["wv"][:, k, :], start=(k == 0), stop=(k == KD - 1))
                        if t % 2:
                            last.then_inc(s["v_psum"].sem, 1)
                    pe.wait_ge(*s["q"](4 * (g + 1)))
                    pe.wait_ge(*s["k"](KD * (g + 1)))
                    for u in range(8 + 3):
                        if u < 8:
                            b, h = u // 4, u % 4
                            n = 8 * g + u
                            if u >= 2:
                                pe.wait_ge(*s["exp"](2 * (n - 1)))
                            for q in range(2):
                                last = pe.matmul(bank[2 + u % 2][:, q * S:(q + 1) * S],
                                                 qz[:, h, b * S + q * P:b * S + (q + 1) * P],
                                                 kT[:, h // 2, b * S:(b + 1) * S], start=True, stop=True)
                            last.then_inc(s["s_psum"].sem, 1)
                        if 2 <= u < 10:
                            v = u - 2
                            n = 8 * g + v
                            pe.wait_ge(*s["pm"](2 * (n + 1)))
                            if v >= 2:
                                pe.wait_ge(*s["pT"](n - 1))
                            for k in range(2):
                                for q in range(2):
                                    last = pe.transpose(bank[4 + v % 2][:, k * S + q * P:k * S + (q + 1) * P],
                                                        pm[v % 2][:, q, k * P:(k + 1) * P], ident[:, :])
                            last.then_inc(s["pT_psum"].sem, 1)
                        if u >= 3:
                            v = u - 3
                            b, h = v // 4, v % 4
                            n = 8 * g + v
                            pe.wait_ge(*s["pT"](n + 1))
                            if v == 0:
                                pe.wait_ge(*s["v"](4 * (g + 1)))
                            if v >= 4 and v % 2 == 0:
                                pe.wait_ge(*s["fT"](4 * g + v // 2 - 1))
                            for k in range(2):
                                last = pe.matmul(bank[6 + h // 2][:, 0:S],
                                                 vz[:, 2 * b + k, h // 2, (h % 2) * P:(h % 2 + 1) * P], pT[v % 2][:, k, :],
                                                 start=(h % 2 == 0 and k == 0), stop=(h % 2 == 1 and k == 1))
                            last.then_inc(s["f_psum"].sem, 1)
                    pe.wait_ge(*s["fT"](4 * (g + 1)))
                    for t in range(GT):
                        i = GT * g + t
                        if after(g, 1) or t >= 2:
                            pe.wait_ge(*s["x_new"](i - 1))
                        for c in range(KD):
                            last = pe.matmul(bank[4 + t % 2][:, 0:D], fT[:, c, t * P:(t + 1) * P], aw["wo"][:, c, :],
                                             start=(c == 0), stop=(c == KD - 1))
                        last.then_inc(s["o_psum"].sem, 1)

                groups(pe, group)

            for s in stages:
                if s["mixes"]:
                    mixture(s)
                elif s["kind"] == "h":
                    recurrence(s)
                else:
                    attention(s)

        @block.vector
        def _(dve):
            def x_tile(g, t):
                return X[:, bass.ds(GT * g + t, 1), :].rearrange("p a d -> p (a d)")

            def combine(s, g):
                for t in range(GT):
                    dve.wait_ge(*s["y_in"][t](32 * (g + 1)))
                    dve.scalar_tensor_tensor(x_tile(g, t), ya[t][:, :], wts[:, 0, bass.ds(GT * g + t, 1)], x_tile(g, t),
                                             ALU.mult, ALU.add).then_inc(s["combined1"].sem, 1)
                for t in range(GT):
                    dve.wait_ge(*s["combined1"](GT * g + t + 1))
                    dve.scalar_tensor_tensor(x_tile(g, t), yb[t][:, :], wts[:, 1, bass.ds(GT * g + t, 1)], x_tile(g, t),
                                             ALU.mult, ALU.add).then_inc(s["x_new"].sem, 1)

            def norm(s, g):
                if s["prev"] is None:
                    dve.wait_ge(x_in[g], 16)
                else:
                    if s["prev"]["mixes"]:
                        combine(s["prev"], g)
                    dve.wait_ge(*s["prev"]["x_new"](GT * (g + 1)))
                for t in range(GT):
                    dve.bn_stats(st[:, t, :], x_tile(g, t)).then_inc(s["stats"].sem, 1)
                for t in range(GT):
                    dve.wait_ge(*s["stats"](GT * g + t + 1))
                    last = dve.bn_aggr(mv[:, t, :], st[:, t, :])
                last.then_inc(s["aggr"].sem, 1)
                dve.wait_ge(*s["stdev"](g + 1))
                dve.reciprocal(rs[:, :], sd[:, :]).then_inc(s["rstd"].sem, 1)
                dve.wait_ge(*s["rstd"](g + 1))
                dve.wait_ge(*s["aggr"](g + 1))
                if after(g, 1) and s["mixes"]:
                    dve.wait_ge(*s["xn_stored"](16 * g))
                for t in range(GT):
                    if after(g, 1):
                        dve.wait_ge(*s["xT_psum"](GT * (g - 1) + t + 1))
                    dve.tensor_scalar(XN[:, t, :], x_tile(g, t), mv[:, t, 0:1], rs[:, t:t + 1],
                                      ALU.subtract, ALU.mult).then_inc(s["xn"].sem, 1)

            def mixture(s):
                L = LAYERS[s["kind"]]
                m = L["m"]
                E, nk, NT = m.E, len(m.KS), m.TILES
                steps = [0]

                def chain(ins):
                    steps[0] += 1
                    ins.then_inc(s["route"].sem, 1)
                    dve.wait_ge(*s["route"](steps[0]))

                def by_expert(ap):
                    return ap[:, 0:NTT * E].rearrange("p (t e) -> p t e", e=E)

                for g in range(NG):
                    norm(s, g)

                score, sel, tmp, pos = (by_expert(x) for x in (f_score, f_sel, f_tmp, f_pos))
                oh = [by_expert(x) for x in f_oh]
                numbers = iota[:, 0:E]

                def over_experts(ap):
                    return ap.unsqueeze(2).broadcast_to((P, NTT, E))

                def choices():
                    dve.wait_ge(*s["scored"](1))
                    loaded(dve, s["kind"] + "_router")
                    chain(dve.tensor_tensor(sel, score, L["bias"][:, :].unsqueeze(1).broadcast_to((P, NTT, E)), ALU.add))
                    number = numbers.unsqueeze(1).broadcast_to((P, NTT, E))
                    for k in range(2):
                        top = f_top[:, k, :]
                        chain(dve.tensor_reduce(top, sel, AX.X, ALU.max))
                        chain(dve.tensor_tensor(tmp, sel, over_experts(top), ALU.is_equal))
                        chain(dve.scalar_tensor_tensor(tmp, number, float(E), tmp, ALU.subtract, ALU.mult))
                        chain(dve.tensor_reduce(f_sum, tmp, AX.X, ALU.min))
                        chain(dve.tensor_scalar(f_sum, f_sum, float(E), None, ALU.add))
                        chain(dve.tensor_tensor(oh[k], number, over_experts(f_sum), ALU.is_equal))
                        if k == 0:
                            chain(dve.scalar_tensor_tensor(sel, oh[0], -BIG, sel, ALU.mult, ALU.add))
                    chain(dve.memset(f_m16[:, NTT * E:(NTT + 1) * E], 0.0))
                    dve.tensor_tensor(f_m16[:, 0:NTT * E].rearrange("p (t e) -> p t e", e=E), oh[0], oh[1],
                                      ALU.add).then_inc(s["both"].sem, 1)
                    for k in range(2):
                        chain(dve.tensor_tensor(tmp, oh[k], score, ALU.mult))
                        chain(dve.tensor_reduce(f_top[:, k, :], tmp, AX.X, ALU.add))
                    chain(dve.tensor_tensor(f_sum, f_top[:, 0, :], f_top[:, 1, :], ALU.add))
                    if s["kind"] == "f0":
                        chain(dve.tensor_scalar(f_sum, f_sum, 1e-12, None, ALU.max))
                    else:
                        chain(dve.tensor_scalar(f_sum, f_sum, 1e-20, None, ALU.add))
                    chain(dve.reciprocal(f_sum, f_sum))
                    for k in range(2):
                        chain(dve.scalar_tensor_tensor(wts[:, k, :], f_top[:, k, :], 0.5, f_sum, ALU.mult, ALU.mult))

                def places():
                    dve.wait_ge(*s["pos_psum"](1))
                    p0 = bank[0][:, 0:NTT * E].rearrange("p (t e) -> p t e", e=E)
                    total = bank[0][:, NTT * E:(NTT + 1) * E]
                    tiles_i, tiles_f, cum, base = f_til[:, 0:E], f_tilf[:, 0:E], f_cum[:, 0:E], f_base[:, 0:E]
                    chain(dve.tensor_scalar(f_cnt[:, 0:E], total, float(P - 1), None, ALU.add))
                    chain(dve.tensor_scalar(tiles_i, f_cnt[:, 0:E], 7, None, ALU.arith_shift_right))
                    chain(dve.tensor_copy(tiles_f, tiles_i))
                    chain(dve.tensor_tensor_scan(cum, ones[:, 0:E], tiles_f, 0.0, ALU.mult, ALU.add))
                    chain(dve.tensor_tensor(base, cum, tiles_f, ALU.subtract))
                    chain(dve.tensor_scalar(base, base, float(P), None, ALU.mult))
                    chain(dve.tensor_tensor(pos, p0, base.unsqueeze(1).broadcast_to((P, NTT, E)), ALU.add))
                    for k in range(2):
                        chain(dve.tensor_tensor(tmp, oh[k], pos, ALU.mult))
                        chain(dve.tensor_reduce(f_slotf[:, k, :], tmp, AX.X, ALU.add))
                    flat = "p a b -> p (a b)"
                    si, sf = slots[:, :, :].rearrange(flat), f_slotf.rearrange(flat)
                    chain(dve.tensor_copy(si, sf))
                    chain(dve.tensor_scalar(f_hi.rearrange(flat), si, 7, None, ALU.arith_shift_right))
                    chain(dve.tensor_scalar(f_lo.rearrange(flat), si, P - 1, None, ALU.bitwise_and))
                    chain(dve.tensor_copy(f_hif.rearrange(flat), f_hi.rearrange(flat)))
                    chain(dve.tensor_copy(f_lof.rearrange(flat), f_lo.rearrange(flat)))
                    for k in range(2):
                        chain(dve.tensor_tensor(f_hi16[k][:, :, 0:NT], iota[:, 0:NT].unsqueeze(1).broadcast_to((P, NTT, NT)),
                                                f_hif[:, k, :].unsqueeze(2).broadcast_to((P, NTT, NT)), ALU.is_equal))
                        chain(dve.tensor_tensor(f_tok16[k][:, :, 0:NT], f_hi16[k][:, :, 0:NT],
                                                tokens16[:, :].unsqueeze(2).broadcast_to((P, NTT, NT)), ALU.mult))
                        dve.tensor_tensor(f_lo16[k], iota[:, :].unsqueeze(1).broadcast_to((P, NTT, P)),
                                          f_lof[:, k, :].unsqueeze(2).broadcast_to((P, NTT, P)),
                                          ALU.is_equal).then_inc(s["marks"].sem, 1)
                    ge = f_ge[:, 0:NT, 0:E]
                    chain(dve.tensor_tensor(ge, iota[0:1, 0:NT].unsqueeze(2).broadcast_to((1, NT, E)),
                                            f_cum[0:1, 0:E].unsqueeze(1).broadcast_to((1, NT, E)), ALU.is_ge))
                    chain(dve.tensor_reduce(f_eidf[:, 0:NT], ge, AX.X, ALU.add))
                    dve.tensor_scalar(f_eid[:, 0:NT], f_eidf[:, 0:NT], float(E - 1), None, ALU.min).then_inc(s["experts"].sem, 1)

                def rows():
                    dve.wait_ge(*s["map_psum"](1))
                    dve.tensor_copy(f_rows[:, 0:NT], bank[1][:, 0:NT]).then_inc(s["rows"].sem, 1)

                def shared_hidden(g):
                    for c, kp in enumerate(m.KS):
                        n = nk * g + c
                        dve.wait_ge(*s["silu"](n + 1))
                        if g >= 2:
                            dve.wait_ge(*s["down"](GT * (g - 1)))
                        dve.tensor_tensor(f_HT[g % 2][0:kp, c, :], f_sg[n % 2][0:kp, :], bank[4 + n % 2][0:kp, :],
                                          ALU.mult).then_inc(s["hid"].sem, 1)

                def shared_add(g):
                    for t in range(GT):
                        i = GT * g + t
                        dve.wait_ge(*s["down"](i + 1))
                        dve.scalar_tensor_tensor(X[:, i, :], bank[6 + i % 2][:, 0:D], 0.5, X[:, i, :],
                                                 ALU.mult, ALU.add).then_inc(s["shared_added"].sem, 1)

                choices()
                shared_hidden(0)
                places()
                shared_hidden(1)
                shared_add(0)
                rows()
                shared_hidden(2)
                shared_add(1)
                shared_hidden(3)
                shared_add(2)
                shared_add(3)
                dve.wait_ge(*s["shared_added"](NTT))
                assert steps[0] == ROUTE_STEPS, steps

                def hid(j, q, r):
                    dve.wait_ge(*s["r_silu"](j + 1))
                    if after(j, 2):
                        dve.wait_ge(*s["r_hT_psum"](j - 1))
                    dve.tensor_tensor(hh[q % 2][:, 0:m.H], sg[q % 2][:, 0:m.H], bank[2 + q % 2][:, m.H:2 * m.H],
                                      ALU.mult).then_inc(s["r_hid"].sem, 1)

                def hidT(j, q, r):
                    dve.wait_ge(*s["r_hT_psum"](j + 1))
                    if after(j, 2):
                        dve.wait_ge(*s["r_down"](j - 1))
                    for k, kp in enumerate(m.KH):
                        last = dve.tensor_copy(hT[q % 2][0:kp, k, :], bank[4 + q % 2][0:kp, k * P:(k + 1) * P])
                    last.then_inc(s["r_hT"].sem, 1)

                def step(j, q, r):
                    if after(j, 1):
                        hidT(j - 1, (q + 3) % 4, None)
                    if not known(j) or j < NT:
                        hid(j, q, r)

                rounds(dve, NT, step)
                for j in range(NT - 2, NT + 1):
                    step(j, j % 4, j // 4)

            def add_out(s, g, first_bank):
                for t in range(GT):
                    dve.wait_ge(*s["o_psum"](GT * g + t + 1))
                    dve.tensor_tensor(x_tile(g, t), bank[first_bank + t % 2][:, 0:D], x_tile(g, t), ALU.add).then_inc(s["x_new"].sem, 1)

            def recurrence(s):
                loaded(dve, "h")

                def front(g):
                    for c in range(KD):
                        n = KD * g + c
                        dve.wait_ge(*s["si"](n + 1))
                        dve.tensor_tensor(g_t1[c], g_si[c], bank[3][:, :], ALU.mult).then_inc(s["t1"].sem, 1)
                        dve.wait_ge(*s["sq"](n + 1))
                        dve.tensor_scalar(g_gw[c], bank[4][:, :], hnorm[:, c:c + 1], None, ALU.mult).then_inc(s["gw"].sem, 1)
                        dve.wait_ge(*s["t1"](n + 1))
                        dve.tensor_tensor(g_t1[c], g_t1[c], g_in[c], ALU.mult).then_inc(s["t2"].sem, 1)
                        dve.wait_ge(*s["t2"](n + 1))
                        for b in range(GW // S):
                            seq = slice(b * S, (b + 1) * S)
                            last = dve.tensor_tensor_scan(g_o[c][:, seq], g_keep[c][:, seq], g_t1[c][:, seq], 0.0,
                                                          ALU.mult, ALU.add)
                        last.then_inc(s["scan"].sem, 1)

                def back(g):
                    dve.wait_ge(*s["ms"](g + 1))
                    dve.reciprocal(g_rms, g_ms).then_inc(s["rms"].sem, 1)
                    dve.wait_ge(*s["rms"](g + 1))
                    for c in range(KD):
                        n = KD * g + c
                        dve.wait_ge(*s["so"](n + 1))
                        dve.tensor_tensor(g_so[c], g_o[c], g_so[c], ALU.mult).then_inc(s["t3"].sem, 1)
                        dve.tensor_tensor(g_gw[c], g_gw[c], g_rms, ALU.mult).then_inc(s["t4"].sem, 1)
                        dve.wait_ge(*s["t3"](n + 1))
                        dve.wait_ge(*s["t4"](n + 1))
                        if after(g, 1):
                            dve.wait_ge(*s["o_psum"](GT * g))
                        dve.tensor_tensor(g_t[:, c, :], g_so[c], g_gw[c], ALU.mult).then_inc(s["t"].sem, 1)

                norm(s, 0)
                norm(s, 1)
                front(0)
                back(0)
                for g in range(1, NG):
                    if g + 1 < NG:
                        norm(s, g + 1)
                    front(g)
                    add_out(s, g - 1, 6)
                    back(g)
                add_out(s, NG - 1, 6)

            def attention(s):
                loaded(dve, "a")
                def group(g):
                    norm(s, g)
                    for c in range(KD):
                        dve.wait_ge(*s["k_psum"](KD * g + c + 1))
                        dve.tensor_scalar(kT[:, c, :], bank[4 + c][:, :], abk[:, c:c + 1], None, ALU.add).then_inc(s["k"].sem, 1)
                    if known(g):
                        dve.wait_ge(zero_q, 2)
                    for b in range(2):
                        dve.wait_ge(*s["v_psum"](2 * g + b + 1))
                        if after(g, 1):
                            dve.wait_ge(*s["f_psum"](8 * g))
                        for p in range(2):
                            dve.tensor_tensor(
                                vz[:, 2 * b:2 * b + 2, :, p * (P + HD):p * (P + HD) + HD],
                                bank[6 + b][:, :].rearrange("p (t c h d) -> p t c h d", t=2, c=KD, h=2)[:, :, :, p, :],
                                abv[:, :].rearrange("p (c h d) -> p c h d", c=KD, h=2)[:, :, p, :]
                                .unsqueeze(1).broadcast_to((P, 2, KD, HD)), ALU.add).then_inc(s["v"].sem, 1)
                    for t in range(GT):
                        dve.tensor_tensor(x_tile(g, t), x_tile(g, t), abo[:, :], ALU.add).then_inc(s["bo"].sem, 1)

                    def weights(u):
                        n = 8 * g + u
                        dve.wait_ge(*s["exp"](2 * (n + 1)))
                        dve.reciprocal(ri[u % 2], sm[u % 2]).then_inc(s["ri"].sem, 1)
                        dve.wait_ge(*s["ri"](n + 1))
                        for h in range(2):
                            dve.tensor_scalar(pm[u % 2][:, h, :], pm[u % 2][:, h, :], ri[u % 2][:, h:h + 1], None,
                                              ALU.mult).then_inc(s["pm"].sem, 1)

                    for u in range(8):
                        n = 8 * g + u
                        dve.wait_ge(*s["s_psum"](n + 1))
                        dve.tensor_reduce(mx[u % 2], bank[2 + u % 2][:, :].rearrange("p (h n) -> p h n", h=2),
                                          AX.X, ALU.max).then_inc(s["mx"].sem, 1)
                        dve.wait_ge(*s["mx"](n + 1))
                        if after(g, 1) or u >= 2:
                            dve.wait_ge(*s["exp"](2 * (n - 1)))
                        dve.tensor_scalar(nm[u % 2], mx[u % 2], -SCORE_SCALE, None, ALU.mult).then_inc(s["nm"].sem, 1)
                        if u >= 1:
                            weights(u - 1)
                    weights(7)
                    dve.wait_ge(*s["bo"](GT * (g + 1)))
                    add_out(s, g, 4)

                for g in range(NG):
                    group(g)

            for s in stages:
                if s["mixes"]:
                    mixture(s)
                elif s["kind"] == "h":
                    recurrence(s)
                else:
                    attention(s)
            for g in range(NG):
                combine(stages[-1], g)


def constants():
    k = np.arange(P)
    return {
        "ident": np.eye(P, dtype=np.float32),
        "ones": np.ones((P, P), np.float32),
        "ones16": np.ones((P, P), np.float16),
        "before16": (k[:, None] < k[None, :]).astype(np.float16),
        "iota": np.broadcast_to(k.astype(np.float32), (P, P)).copy(),
        "tokens16": (k[:, None] + P * np.arange(NTT)[None, :]).astype(np.float16),
    }


def kernel(**inputs):
    import concourse.bacc as _bacc
    from concourse.bass_utils import run_bass_kernel_spmd as _run

    v = {k: np.asarray(x) for k, x in inputs.items()}

    def on_partitions(w):
        return np.ascontiguousarray(np.moveaxis(w.reshape(-1, P, *w.shape[1:]), 0, 1))

    def rows(w):
        n = -(-w.shape[0] // P)
        full = np.zeros((n * P, w.shape[1]), w.dtype)
        full[:w.shape[0]] = w
        return on_partitions(full)

    arrays = dict(constants())
    arrays["x"] = np.ascontiguousarray(v["L0_attn_hidden_states"].reshape(T, D))
    f0, f1, h, at = "L0_ffn_", "L1_ffn_", "L0_attn_", "L1_attn_"
    arrays["f0_router"] = on_partitions(v[f0 + "gate_w"].T)
    arrays["f0_bias"] = np.broadcast_to(v[f0 + "router_bias"], (P, MOE0.E)).copy()
    arrays["f0_w13"] = on_partitions(np.concatenate([v[f0 + "W1"], v[f0 + "W3"]], axis=2).transpose(1, 0, 2))
    arrays["f0_w2"] = np.ascontiguousarray(v[f0 + "W2"].transpose(1, 0, 2))
    arrays["f0_s1"] = on_partitions(v[f0 + "sw1"].T)
    arrays["f0_s3"] = on_partitions(v[f0 + "sw3"].T)
    arrays["f0_s2"] = rows(v[f0 + "sw2"].T)
    arrays["f1_router"] = on_partitions(v[f1 + "gate_w"])
    arrays["f1_bias"] = np.broadcast_to(v[f1 + "expert_bias"], (P, MOE1.E)).copy()
    arrays["f1_w13"] = on_partitions(v[f1 + "experts_gate_up"].transpose(1, 0, 2))
    arrays["f1_w2"] = np.ascontiguousarray(v[f1 + "experts_down"].transpose(1, 0, 2))
    arrays["f1_s1"] = on_partitions(v[f1 + "shared_gate_w"])
    arrays["f1_s3"] = on_partitions(v[f1 + "shared_up_w"])
    arrays["f1_s2"] = rows(v[f1 + "shared_down_w"])
    for n, src in (("wf", "Wf"), ("wi", "Wi"), ("wg", "Wg"), ("wo", "Wo")):
        arrays["h_" + n] = on_partitions(v[h + src].T)
    arrays["h_norm"] = np.ascontiguousarray(v[h + "g_norm_weight"].reshape(KD, P).T)
    for n in ("q", "k", "v", "o"):
        arrays["a_w" + n] = on_partitions(v[at + "W" + n])
    arrays["a_bq"] = np.ascontiguousarray(v[at + "bq"].reshape(KD, P).T)
    arrays["a_bk"] = np.ascontiguousarray(v[at + "bk"].reshape(KD, P).T)
    arrays["a_bv"] = np.broadcast_to(v[at + "bv"], (P, D)).copy()
    arrays["a_bo"] = np.broadcast_to(v[at + "bo"], (P, D)).copy()

    nc = _bacc.Bacc("TRN2", target_bir_lowering=False, num_devices=1)
    args = {n: nc.dram_tensor("in_" + n, x.shape, mybir.dt.from_np(x.dtype), kind="ExternalInput").ap()
            for n, x in arrays.items()}
    out = nc.dram_tensor("out_x", (T, D), F32, kind="ExternalOutput").ap()
    macaron_kernel(nc, args, out)
    r = _run(nc, [{"in_" + n: x for n, x in arrays.items()}], core_ids=[0])
    return r.results[0]["out_x"].reshape(B, S, D)
```

```python
import numpy as np
import concourse.bass as bass
from concourse import mybir
from contextlib import ExitStack

F32 = mybir.dt.float32
F16 = mybir.dt.float16
I32 = mybir.dt.int32
ALU = mybir.AluOpType
ACT = mybir.ActivationFunctionType
AX = mybir.AxisListType

P = 128
D = 256
KD = D // P
R = 8
B, S = 8, 256
BT = S // P
T = B * S
NTT = T // P
GT = 4
NG = NTT // GT
GW = GT * P
EPS = 1e-5
HEADS = 4
HD = D // HEADS
SCORE_SCALE = 0.5
BIG = 1.0e30


class Moe:

    def __init__(self, experts, hidden, shared):
        self.E, self.H, self.SH = experts, hidden, shared
        self.TILES = -(-(2 * T // P + experts - 1) // R) * R
        self.KH = [min(P, hidden - k) for k in range(0, hidden, P)]
        self.KS = [min(P, shared - k) for k in range(0, shared, P)]


MOE0 = Moe(8, 176, 352)
MOE1 = Moe(16, 128, 128)
MAXE = 16


def macaron_kernel(nc, a, out):
    ctx = ExitStack()
    with ctx:
        def sb(name, shape, dt=F32):
            return ctx.enter_context(nc.sbuf_tensor(name, shape, dt))

        def sem(name):
            return ctx.enter_context(nc.semaphore(name))

        X = sb("X", [P, NTT, D])
        XT = sb("XT", [P, KD, T])
        XN = sb("XN", [P, NTT, D])
        ident = sb("ident", [P, P])
        ones = sb("ones", [P, P])
        ones16 = sb("ones16", [P, P], F16)
        before16 = sb("before16", [P, P], F16)
        iota = sb("iota", [P, P])
        tokens16 = sb("tokens16", [P, NTT], F16)
        spare = sb("spare", [P, MOE1.TILES])
        epsc = sb("epsc", [P, 1])
        w13_at = sb("w13", [P, KD * MOE1.E * 2 * MOE1.H])
        w2_at = sb("w2", [P, MOE1.E * D])
        LAYERS = {}
        for n, m in (("f0", MOE0), ("f1", MOE1)):
            w2 = w2_at[:, :].rearrange("p (k e d) -> p k e d", k=len(m.KH), e=m.E)
            LAYERS[n] = dict(
                m=m,
                router=sb(n + "_router", [P, KD, m.E]),
                bias=sb(n + "_bias", [P, m.E]),
                w13=w13_at[:, 0:KD * m.E * 2 * m.H].rearrange("p (k e h) -> p k e h", k=KD, e=m.E),
                w2=[w2[0:kp, k] for k, kp in enumerate(m.KH)],
                s1=sb(n + "_s1", [P, KD, m.SH]),
                s3=sb(n + "_s3", [P, KD, m.SH]),
                s2=sb(n + "_s2", [P, len(m.KS), D]),
            )
        hw = {n: sb("h_" + n, [P, KD, D]) for n in ("wf", "wi", "wg", "wo")}
        hnorm = sb("h_norm", [P, KD])
        aw = {n: sb("a_" + n, [P, KD, D]) for n in ("wq", "wk", "wv", "wo")}
        abq = sb("a_bq", [P, KD])
        abk = sb("a_bk", [P, KD])
        abv = sb("a_bv", [P, D])
        abo = sb("a_bo", [P, D])

        st = sb("st", [P, NTT, 6])
        mv = sb("mv", [P, NTT, 2])
        sd = sb("sd", [P, NTT])
        rs = sb("rs", [P, NTT])
        yab = [sb(f"yab{q}", [P, 2, D]) for q in range(4)]
        wts = sb("wts", [P, 2, NTT])
        slots = sb("slots", [P, 2, NTT], I32)
        ARENA = 14400
        arena = sb("arena", [P, ARENA])

        class Carve:
            def __init__(self):
                self.at = 0

            def __call__(self, *shape, dt=F32, parts=P):
                size = 1
                for s in shape:
                    size *= s
                cols = -(-size * (2 if dt == F16 else 4) // 4)
                ap = arena[0:parts, self.at:self.at + cols]
                self.at += cols
                assert self.at <= ARENA, self.at
                if dt != F32:
                    ap = ap.bitcast(dt)
                if len(shape) == 1:
                    return ap
                names = "abcd"[:len(shape)]
                return ap.rearrange(f"p ({' '.join(names)}) -> p {' '.join(names)}",
                                    **{n: s for n, s in zip(names[1:], shape[1:])})

        c = Carve()
        lgT = c(GW)
        f_score = c(NTT * MAXE)
        f_sel = c(NTT * MAXE)
        f_tmp = c(NTT * MAXE)
        f_oh = [c(NTT * MAXE), c(NTT * MAXE)]
        f_m16 = c((NTT + 1) * MAXE, dt=F16)
        f_pos = c(NTT * MAXE)
        f_top = c(2, NTT)
        f_sum = c(NTT)
        f_slotf = c(2, NTT)
        f_hi = c(2, NTT, dt=I32)
        f_lo = c(2, NTT, dt=I32)
        f_hif = c(2, NTT)
        f_lof = c(2, NTT)
        f_cnt = c(MAXE, dt=I32)
        f_til = c(MAXE, dt=I32)
        f_tilf = c(MAXE)
        f_cum = c(MAXE)
        f_base = c(MAXE)
        shared_at = c.at
        f_lo16 = [c(NTT, P, dt=F16) for _ in range(2)]
        f_hi16 = [c(NTT, 48, dt=F16) for _ in range(2)]
        f_tok16 = [c(NTT, 48, dt=F16) for _ in range(2)]
        f_ge = c(48, MAXE, parts=1)
        marks_end, c.at = c.at, shared_at
        xs = [c(D) for _ in range(R)]
        xsT = [c(KD, P) for _ in range(2)]
        sg = [c(176) for _ in range(2)]
        hh = [c(176) for _ in range(2)]
        hT = [c(2, P) for _ in range(2)]
        ys = [c(D) for _ in range(R)]
        c.at = max(c.at, marks_end)
        f_map = c(2, 48)
        f_full = c(48)
        f_empty = c(48)
        f_second = c(48)
        f_rows = c(48, dt=I32)
        f_eidf = c(48, parts=1)
        f_eid = c(48, dt=I32, parts=1)
        f_sg = [c(GW) for _ in range(2)]
        f_HT = [c(3, GW) for _ in range(3)]
        c = Carve()
        g_keep = [c(GW) for _ in range(KD)]
        g_in = [c(GW) for _ in range(KD)]
        g_si = [c(GW) for _ in range(KD)]
        g_t1 = [c(GW) for _ in range(KD)]
        g_o = [c(GW) for _ in range(KD)]
        g_so = [c(GW) for _ in range(KD)]
        g_sq = [c(GW) for _ in range(KD)]
        g_gw = [c(GW) for _ in range(KD)]
        g_ms = c(GT)
        g_rms = [c(GT) for _ in range(NG)]
        g_t = c(KD, GW)
        c = Carve()
        qz = c(2, HEADS, S)
        kT = c(2, KD, S)
        vz = c(2, BT, KD * 2 * P)
        pm = [c(2, S) for _ in range(2)]
        pT = [c(2, S) for _ in range(2)]
        fT = c(2, KD, S)
        xTb = c(2, KD, S)
        mx = [c(2) for _ in range(2)]
        nm = [c(2) for _ in range(2)]
        sm = [c(2) for _ in range(2)]
        ri = [c(2) for _ in range(2)]

        bank = [ctx.enter_context(nc.psum_tensor(f"bank{i}", [P, 512], F32)) for i in range(8)]

        x_rows = nc.dram_tensor("slot_rows", (MOE1.TILES * P, D), F32, kind="Internal").ap()
        y_rows = {n: nc.dram_tensor(n + "_result_rows", (2 * T + L["m"].TILES * P, D), F32, kind="Internal").ap()
                  for n, L in LAYERS.items()}

        x_in = [sem(f"x_in{g}") for g in range(NG)]
        loads = {}
        order = [("const", [(ident, a["ident"]), (ones, a["ones"]), (ones16, a["ones16"]),
                            (before16, a["before16"]), (iota, a["iota"]),
                            (tokens16, a["tokens16"]), (spare, a["spare"])])]
        for n in ("f0", "h", "f1", "a"):
            if n in LAYERS:
                L = LAYERS[n]
                order.append((n + "_router", [(L["router"], a[n + "_router"]), (L["bias"], a[n + "_bias"])]))
                order.append((n + "_shared", [(L["s1"], a[n + "_s1"]), (L["s3"], a[n + "_s3"]), (L["s2"], a[n + "_s2"])]))
                k0 = 0
                w2 = []
                for k, kp in enumerate(L["m"].KH):
                    w2.append((L["w2"][k], a[n + "_w2"][k0:k0 + kp]))
                    k0 += kp
                order.append((n + "_experts", [(L["w13"], a[n + "_w13"])] + w2))
            elif n == "h":
                order.append(("h", [(hw[k], a["h_" + k]) for k in hw] + [(hnorm, a["h_norm"])]))
            else:
                order.append(("a", [(aw[k], a["a_" + k]) for k in aw]
                              + [(abq, a["a_bq"]), (abk, a["a_bk"]), (abv, a["a_bv"]), (abo, a["a_bo"])]))
        for name, parts in order:
            loads[name] = (sem("in_" + name), 16 * len(parts))

        def load_now(eng, name):
            for dst, src in dict(order)[name]:
                full = dst[tuple(slice(None) for _ in dst.shape)]
                eng.dma_start(full, src).then_inc(loads[name][0], 16)

        def loaded(eng, name):
            eng.wait_ge(*loads[name])

        zero_q = sem("zero_q")
        eps_set = sem("eps_set")
        zeros_set = sem("zeros_set")
        rows_set = sem("rows_set")

        class Count:

            def __init__(self, of, start):
                self.sem, self.start = of, start

            def __call__(self, n):
                return self.sem, self.start + n

        made, left_at = {}, {}

        def count(name, total):
            if name not in made:
                made[name], left_at[name] = sem(name), 0
            got = Count(made[name], left_at[name])
            left_at[name] += total
            return got

        ROUTE_STEPS = 50

        def stage(number, kind, prev):
            totals = dict(stats=NTT, aggr=NG, stdev=NG, rstd=NG, xn=NTT, xT_psum=NTT, xT=NTT)
            mixes = kind in LAYERS
            lists = {}
            if mixes:
                m = LAYERS[kind]["m"]
                nk, tiles = len(m.KS), m.TILES
                totals |= dict(combined1=NTT, slotted=1, rows_out=16 * 2 * NTT, rl_psum=NG, rl_copied=NG, lg_psum=NG, scored=1,
                               route=ROUTE_STEPS, both=1, pos_psum=1, marks=2, map_psum=1, rows=1, experts=1,
                               up=NG * nk, silu=NG * nk, hid=NG * nk, down=NTT, shared_added=NTT)
                totals |= {k: tiles for k in ("r_xT_psum", "r_xT", "r_up", "r_silu", "r_hid", "r_hT_psum",
                                              "r_hT", "r_down", "r_y")}
                lists = dict(row_in=(R, 16 * tiles // R), y_out=(R, 16 * tiles // R), y_in=(4, 16 * NG))
            elif kind == "h":
                totals |= {k: KD * NG for k in ("f_psum", "i_psum", "g_psum", "keep", "in_", "si", "sq", "t1",
                                                "t2", "scan", "gw", "so", "t3", "t")}
                totals |= dict(ms_psum=NG, ms=NG, rms=NG, o_psum=NTT)
            else:
                totals |= dict(q_psum=B, q=B * HEADS, k_psum=B, k=B * KD, xTb=B, v_psum=B, v=2 * B,
                               f_psum=B * HEADS, fT=B * KD, o_psum=B, bo=NG, exp=B * 2 * HEADS, pm=B * 2 * HEADS)
                totals |= {k: B * HEADS for k in ("s_psum", "mx", "nm", "ri", "pT_psum", "pT")}
            got = {k: count(k, n) for k, n in totals.items()}
            got |= {k: [count(f"{k}{q}", n) for q in range(copies)] for k, (copies, n) in lists.items()}
            got |= dict(kind=kind, prev=prev, mixes=mixes, before_attention=False, x_new=count(f"x_new{number % 2}", NTT))
            return got

        stages, prev = [], None
        for number, kind in enumerate(["f0", "h", "f0", "f1", "a", "f1"]):
            if prev is not None:
                prev["before_attention"] = kind == "a"
            prev = stage(number, kind, prev)
            stages.append(prev)
        out_stored = sem("out_stored")

        def known(j):
            return isinstance(j, int)

        def after(j, n):
            return not known(j) or j >= n

        def rounds(eng, tiles, body, more=0):
            for j in range(2 * R - 2):
                body(j, j % R, j // R)
            with eng.Fori(1, tiles // R - 1) as i:
                for u in range(R - 2, 2 * R - 2):
                    body(R * i + u, u % R, i + u // R)
            for j in range(tiles - 2, tiles + more):
                body(j, j % R, j // R)

        def sequences(eng, body):
            body(0, 0)
            body(1, 1)
            with eng.Fori(1, B // 2 - 1) as i:
                body(2 * i, 0)
                body(2 * i + 1, 1)
            body(B - 2, 0)
            body(B - 1, 1)

        def back(b, h, n):
            return (b, h - n) if h >= n else (b - 1, h - n + HEADS)

        block = ctx.enter_context(nc.Block())

        @block.sync
        def _(sp):
            x_dram = a["x"].rearrange("(g t p) d -> g p t d", g=NG, p=P)

            def load_x(g):
                sp.dma_start(X[:, g * GT:(g + 1) * GT, :], x_dram[g]).then_inc(x_in[g], 16)

            load_x(0)
            load_now(sp, "const")
            load_x(1)
            load_now(sp, "f0_router")
            load_x(2)
            load_x(3)
            load_now(sp, "f0_shared")
            for g in range(NG):
                sp.wait_ge(x_in[g], 16)
            sp.wait_ge(zeros_set, 1)
            sp.dma_start(x_rows.rearrange("(n p) d -> p n d", p=P),
                         yab[0][:, 0:1, :].broadcast_to((P, MOE1.TILES, D))).then_inc(rows_set, 16)
            load_now(sp, "f0_experts")
            sp.wait_ge(*loads["f0_shared"])
            for name in ("h", "f1_router", "f1_shared", "a"):
                load_now(sp, name)

            for n, s in enumerate(stages):
                if not s["mixes"]:
                    continue
                tiles = LAYERS[s["kind"]]["m"].TILES
                sp.wait_ge(*s["rows_out"](16 * 2 * NTT))
                sp.wait_ge(*s["map_psum"](1))

                def load_rows(j, q, r):
                    if after(j, R):
                        sp.wait_ge(*s["r_xT_psum"](j - R + 1))
                    sp.dma_start(xs[q], x_rows[bass.ds(j * P, P), :]).then_inc(s["row_in"][q].sem, 16)

                rounds(sp, tiles, load_rows)
                for q in range(R):
                    sp.wait_ge(*s["y_out"][q](16 * tiles // R))
                results = y_rows[s["kind"]][0:2 * T, :].rearrange("(c t p) d -> t p c d", c=2, p=P)
                for i in range(NTT):
                    if i >= 4:
                        sp.wait_ge(*s["x_new"](i - 3))
                    sp.dma_start(yab[i % 4][:, :, :], results[i]).then_inc(s["y_in"][i % 4].sem, 16)
                if s["kind"] == "f0" and stages[n + 1]["kind"] == "f1":
                    load_now(sp, "f1_experts")

            last = stages[-1]
            out_t = out.rearrange("(g t p) d -> g p t d", g=NG, p=P)
            for g in range(NG):
                sp.wait_ge(*last["x_new"](GT * (g + 1)))
                sp.dma_start(out_t[g], X[:, g * GT:(g + 1) * GT, :]).then_inc(out_stored, 16)
            sp.wait_ge(out_stored, 16 * NG)

        @block.gpsimd
        def _(pool):
            pool.memset(epsc[:, :], EPS).then_inc(eps_set, 1)
            pool.memset(yab[0][:, 0, :], 0.0).then_inc(zeros_set, 1)
            pool.wait_ge(rows_set, 16)

            def scatter(dst, idx, src, done):
                pool.indirect_dma_start(out=dst, out_offset=bass.IndirectOffsetOnAxis(ap=idx, axis=0),
                                        in_=src, in_offset=None).then_inc(done.sem, 16)

            for s in stages:
                if s["kind"] == "a":
                    for b in range(B):
                        pool.wait_ge(*s["xT"](BT * (b + 1)))
                        if b >= 2:
                            pool.wait_ge(*s["v_psum"](b - 1))
                        pool.tensor_copy(xTb[:, b % 2], XT[:, :, b * S:(b + 1) * S]).then_inc(s["xTb"].sem, 1)
                if not s["mixes"]:
                    continue
                tiles = LAYERS[s["kind"]]["m"].TILES
                pool.wait_ge(*s["slotted"](1))
                for i in range(NTT):
                    for k in range(2):
                        scatter(x_rows, slots[:, k, i:i + 1], XN[:, i, :], s["rows_out"])
                pool.wait_ge(*s["rows"](1))
                for j in range(tiles):
                    pool.wait_ge(*s["r_y"](j + 1))
                    scatter(y_rows[s["kind"]], f_rows[:, j:j + 1], ys[j % R], s["y_out"][j % R])
                if s["before_attention"]:
                    for q in range(R):
                        pool.wait_ge(*s["y_out"][q](16 * tiles // R))
                    pool.memset(qz, 0.0).then_inc(zero_q, 1)
                    pool.memset(vz, 0.0).then_inc(zero_q, 1)

        @block.scalar
        def _(act):
            act.wait_ge(eps_set, 1)

            def stdev(s, g):
                act.wait_ge(*s["aggr"](g + 1))
                act.activation(sd[:, bass.ds(g * GT, GT)], mv[:, bass.ds(g * GT, GT), 1], ACT.Sqrt,
                               bias=epsc[:, :]).then_inc(s["stdev"].sem, 1)

            def copy_xT(s, g, t, banks=2):
                act.wait_ge(*s["xT_psum"](GT * g + t + 1))
                act.activation(XT[:, :, bass.ds((GT * g + t) * P, P)],
                               bank[t % banks][:, 0:D].rearrange("p (k n) -> p k n", k=KD),
                               ACT.Copy).then_inc(s["xT"].sem, 1)

            def mixture(s):
                L = LAYERS[s["kind"]]
                m = L["m"]
                nk = len(m.KS)
                def logits(g):
                    act.wait_ge(*s["rl_psum"](g + 1))
                    act.activation(lgT[0:m.E, :], bank[6][0:m.E, :], ACT.Copy).then_inc(s["rl_copied"].sem, 1)

                def shared_silu(first, end):
                    for n in range(first, end):
                        kp = m.KS[n % nk]
                        act.wait_ge(*s["up"](n + 1))
                        if n >= 2:
                            act.wait_ge(*s["hid"](n - 1))
                        act.activation(f_sg[n % 2][0:kp, :], bank[2 + n % 2][0:kp, :], ACT.Silu).then_inc(s["silu"].sem, 1)

                stdev(s, 0)
                stdev(s, 1)
                for g in range(NG):
                    for t in range(GT):
                        copy_xT(s, g, t)
                    logits(g)
                    if g + 2 < NG:
                        stdev(s, g + 2)
                    if g in (1, 2):
                        shared_silu((g - 1) * nk, g * nk)
                act.wait_ge(*s["lg_psum"](NG))
                act.activation(f_score[:, 0:NTT * m.E], bank[7][:, 0:NTT * m.E], ACT.Sigmoid).then_inc(s["scored"].sem, 1)
                shared_silu(2 * nk, NG * nk)

                def xT(j, q, r):
                    act.wait_ge(*s["r_xT_psum"](j + 1))
                    if after(j, 2):
                        act.wait_ge(*s["r_up"](j - 1))
                    act.activation(xsT[q % 2], bank[q % 2][:, 0:D].rearrange("p (k n) -> p k n", k=KD),
                                   ACT.Copy).then_inc(s["r_xT"].sem, 1)

                def silu(j, q, r):
                    act.wait_ge(*s["r_up"](j + 1))
                    if after(j, 2):
                        act.wait_ge(*s["r_hid"](j - 1))
                    act.activation(sg[q % 2][:, 0:m.H], bank[2 + q % 2][:, 0:m.H], ACT.Silu).then_inc(s["r_silu"].sem, 1)

                def y(j, q, r):
                    act.wait_ge(*s["r_down"](j + 1))
                    if after(j, R):
                        act.wait_ge(*s["y_out"][q](16 * r))
                    act.activation(ys[q], bank[6 + q % 2][:, 0:D], ACT.Copy).then_inc(s["r_y"].sem, 1)

                def step(j, q, r):
                    if not known(j) or j < m.TILES:
                        silu(j, q, r)
                    if not known(j) or j + 2 < m.TILES:
                        xT(j + 2, (q + 2) % R, None)
                    if after(j, 2):
                        y(j - 2, (q - 2) % R, r if q >= 2 else r - 1)

                xT(0, 0, 0)
                xT(1, 1, 0)
                rounds(act, m.TILES, step, more=2)

            def recurrence(s):
                def first(g):
                    for c in range(KD):
                        n = KD * g + c
                        act.wait_ge(*s["f_psum"](n + 1))
                        if after(g, 1):
                            act.wait_ge(*s["scan"](n - KD + 1))
                        act.activation(g_keep[c], bank[2][:, :], ACT.Sigmoid).then_inc(s["keep"].sem, 1)
                        act.activation(g_in[c], bank[2][:, :], ACT.Sigmoid, scale=-1.0).then_inc(s["in_"].sem, 1)
                        act.wait_ge(*s["i_psum"](n + 1))
                        act.activation(g_si[c], bank[3][:, :], ACT.Sigmoid).then_inc(s["si"].sem, 1)
                        act.wait_ge(*s["g_psum"](n + 1))
                        if after(g, 1):
                            act.wait_ge(*s["ms_psum"](g))
                        act.activation(g_sq[c], bank[4][:, :], ACT.Square).then_inc(s["sq"].sem, 1)

                def mean_square(g):
                    act.wait_ge(*s["ms_psum"](g + 1))
                    if g:
                        act.wait_ge(*s["rms"](g))
                    act.activation(g_ms, bank[5][:, 0:GT], ACT.Sqrt, scale=1.0 / D, bias=epsc[:, :]).then_inc(s["ms"].sem, 1)

                def second(g):
                    for c in range(KD):
                        n = KD * g + c
                        act.wait_ge(*s["scan"](n + 1))
                        if after(g, 1):
                            act.wait_ge(*s["t"](n - KD + 1))
                        act.activation(g_so[c], g_o[c], ACT.Sigmoid).then_inc(s["so"].sem, 1)

                stdev(s, 0)
                for t in range(GT):
                    copy_xT(s, 0, t)
                stdev(s, 1)
                for g in range(NG):
                    first(g)
                    if g + 1 < NG:
                        for t in range(GT):
                            copy_xT(s, g + 1, t)
                    mean_square(g)
                    if g + 2 < NG:
                        stdev(s, g + 2)
                    second(g)

            def attention(s):
                def copy_group(g):
                    for t in range(GT):
                        copy_xT(s, g, t, banks=1)

                def queries(b, side):
                    act.wait_ge(*s["q_psum"](b + 1))
                    for h in range(HEADS):
                        c, p = h // 2, h % 2
                        r = slice(p * HD, (p + 1) * HD)
                        act.activation(qz[r, side, h, :], bank[1][r, c * S:(c + 1) * S], ACT.Identity,
                                       bias=abq[r, c:c + 1]).then_inc(s["q"].sem, 1)

                def keys(b, side):
                    act.wait_ge(*s["k_psum"](b + 1))
                    for c in range(KD):
                        act.activation(kT[:, side, c, :], bank[1][:, c * S:(c + 1) * S], ACT.Identity,
                                       bias=abk[:, c:c + 1]).then_inc(s["k"].sem, 1)

                def exps(b, h):
                    n = HEADS * b + h
                    act.wait_ge(*s["nm"](n + 1))
                    if after(b, 1) or h >= 2:
                        act.wait_ge(*s["pT_psum"](n - 1))
                    for q in range(BT):
                        act.activation(pm[h % 2][:, q, :], bank[2 + h % 2][:, q * S:(q + 1) * S], ACT.Exp,
                                       scale=SCORE_SCALE, bias=nm[h % 2][:, q:q + 1],
                                       accum_out=sm[h % 2][:, q:q + 1]).then_inc(s["exp"].sem, 1)

                def copy_pT(b, h):
                    n = HEADS * b + h
                    act.wait_ge(*s["pT_psum"](n + 1))
                    if after(b, 1) or h >= 2:
                        act.wait_ge(*s["f_psum"](n - 1))
                    act.activation(pT[h % 2], bank[4 + h % 2][:, :].rearrange("p (k n) -> p k n", k=2),
                                   ACT.Copy).then_inc(s["pT"].sem, 1)

                def features(b, h, side):
                    act.wait_ge(*s["f_psum"](HEADS * b + h + 1))
                    act.activation(fT[:, side, h // 2, :], bank[6][:, (h // 2) * S:(h // 2 + 1) * S],
                                   ACT.Copy).then_inc(s["fT"].sem, 1)

                def step(b, side):
                    for h in range(HEADS):
                        if not known(b) or b < B:
                            exps(b, h)
                        if h == 0 and (not known(b) or b + 1 < B):
                            queries(b + 1, 1 - side)
                        if h == 1 and (not known(b) or b + 1 < B):
                            keys(b + 1, 1 - side)
                        pb, ph = back(b, h, 2)
                        if after(b, 1) or h >= 2:
                            if not known(b) or pb < B:
                                copy_pT(pb, ph)
                        pb, ph = back(b, h, 3)
                        if (after(b, 1) or h >= 3) and ph % 2 and (not known(b) or pb < B):
                            features(pb, ph, side if h >= 3 else 1 - side)
                        if known(b) and (b, h) == (0, 1):
                            stdev(s, 3)
                        if known(b) and b < 2:
                            copy_xT(s, 2 + b, h, banks=1)

                stdev(s, 0)
                stdev(s, 1)
                copy_group(0)
                act.wait_ge(zero_q, 2)
                queries(0, 0)
                keys(0, 0)
                stdev(s, 2)
                copy_group(1)
                sequences(act, step)
                step(B, 0)

            for s in stages:
                if s["mixes"]:
                    mixture(s)
                elif s["kind"] == "h":
                    recurrence(s)
                else:
                    attention(s)

        @block.tensor
        def _(pe):
            loaded(pe, "const")

            def transpose_x(s, g, t, banks=2):
                i = GT * g + t
                pe.wait_ge(*s["xn"](i + 1))
                if i >= banks:
                    pe.wait_ge(*s["xT"](i - banks + 1))
                for k in range(KD):
                    last = pe.transpose(bank[t % banks][:, k * P:(k + 1) * P], XN[:, i, k * P:(k + 1) * P], ident[:, :])
                last.then_inc(s["xT_psum"].sem, 1)

            def mixture(s):
                L = LAYERS[s["kind"]]
                m = L["m"]
                E, nk = m.E, len(m.KS)

                def logits_back(g):
                    pe.wait_ge(*s["rl_copied"](g + 1))
                    for t in range(GT):
                        i = GT * g + t
                        last = pe.transpose(bank[7][:, i * E:(i + 1) * E], lgT[0:E, t * P:(t + 1) * P], ident[0:E, 0:E])
                    last.then_inc(s["lg_psum"].sem, 1)

                def logits(g):
                    pe.wait_ge(*s["xT"](GT * (g + 1)))
                    for k in range(KD):
                        last = pe.matmul(bank[6][0:E, :], L["router"][:, k, :], XT[:, k, g * GW:(g + 1) * GW],
                                         start=(k == 0), stop=(k == KD - 1))
                    last.then_inc(s["rl_psum"].sem, 1)

                def shared_up(first, end):
                    for n in range(first, end):
                        g, c = n // nk, n % nk
                        kp = m.KS[c]
                        if n >= 2:
                            pe.wait_ge(*s["hid"](n - 1))
                        for w, b in ((L["s1"], 2), (L["s3"], 4)):
                            for k in range(KD):
                                last = pe.matmul(bank[b + n % 2][0:kp, :], w[:, k, c * P:c * P + kp],
                                                 XT[:, k, g * GW:(g + 1) * GW], start=(k == 0), stop=(k == KD - 1))
                        last.then_inc(s["up"].sem, 1)

                def shared_down(g):
                    pe.wait_ge(*s["hid"](nk * (g + 1)))
                    for t in range(GT):
                        i = GT * g + t
                        if i >= 2:
                            pe.wait_ge(*s["shared_added"](i - 1))
                        for c, kp in enumerate(m.KS):
                            last = pe.matmul(bank[6 + i % 2][:, 0:D], f_HT[g % 3][0:kp, c, t * P:(t + 1) * P],
                                             L["s2"][0:kp, c, :], start=(c == 0), stop=(c == nk - 1))
                        last.then_inc(s["down"].sem, 1)

                def positions():
                    pe.wait_ge(*s["both"](1))
                    pos = bank[0][:, 0:(NTT + 1) * E]
                    marks = f_m16[:, 0:(NTT + 1) * E]
                    pe.matmul(pos, before16[:, :], marks, start=True, stop=False, skip_group_check=True)
                    for i in range(NTT):
                        n = NTT - i
                        last = pe.matmul(pos[:, (i + 1) * E:].rearrange("p (t e) -> p t e", e=E), ones16[:, :],
                                         marks[:, i * E:(i + 1) * E].unsqueeze(1).broadcast_to((P, n, E)),
                                         start=False, stop=(i == NTT - 1), skip_group_check=True)
                    last.then_inc(s["pos_psum"].sem, 1)

                def slot_tokens():
                    pe.wait_ge(*s["marks"](2))
                    for k in range(2):
                        for i in range(NTT):
                            last = pe.matmul(bank[1][:, k * m.TILES:(k + 1) * m.TILES], f_lo16[k][:, i, :],
                                             f_tok16[k][:, i, 0:m.TILES], start=(i == 0), stop=(i == NTT - 1))
                    last.then_inc(s["map_psum"].sem, 1)

                loaded(pe, s["kind"] + "_router")
                for g in range(NG):
                    for t in range(GT):
                        transpose_x(s, g, t)
                    if g:
                        logits_back(g - 1)
                    logits(g)
                    if g == 1:
                        loaded(pe, s["kind"] + "_shared")
                    if g in (1, 2):
                        shared_up((g - 1) * nk, g * nk)
                logits_back(NG - 1)
                shared_up(2 * nk, 2 * nk + nk // 2)
                positions()
                shared_up(2 * nk + nk // 2, 3 * nk)
                pe.wait_ge(*s["scored"](1))
                shared_down(0)
                slot_tokens()
                shared_up(3 * nk, 4 * nk)
                for g in range(1, NG):
                    shared_down(g)

                def xT(j, q, r):
                    pe.wait_ge(*s["row_in"][q](16 * (r + 1)))
                    if after(j, 2):
                        pe.wait_ge(*s["r_xT"](j - 1))
                    for k in range(KD):
                        last = pe.transpose(bank[q % 2][:, k * P:(k + 1) * P], xs[q][:, k * P:(k + 1) * P], ident[:, :])
                    last.then_inc(s["r_xT_psum"].sem, 1)

                def expert(j):
                    return pe.value_load(f_eid[0:1, bass.ds(j, 1)], min_val=0, max_val=E - 1)

                def up(j, q, r):
                    e = expert(j)
                    pe.wait_ge(*s["r_xT"](j + 1))
                    if after(j, 2):
                        pe.wait_ge(*s["r_hid"](j - 1))
                    for k in range(KD):
                        last = pe.matmul(bank[2 + q % 2][:, 0:2 * m.H], xsT[q % 2][:, k, :],
                                         L["w13"][:, k, bass.ds(e, 1), :], start=(k == 0), stop=(k == KD - 1))
                    last.then_inc(s["r_up"].sem, 1)

                def hid(j, q, r):
                    pe.wait_ge(*s["r_hid"](j + 1))
                    if after(j, 2):
                        pe.wait_ge(*s["r_hT"](j - 1))
                    for k, kp in enumerate(m.KH):
                        last = pe.transpose(bank[4 + q % 2][0:kp, k * P:(k + 1) * P],
                                            hh[q % 2][:, k * P:k * P + kp], ident[:, :])
                    last.then_inc(s["r_hT_psum"].sem, 1)

                def down(j, q, r):
                    e = expert(j)
                    pe.wait_ge(*s["r_hT"](j + 1))
                    if after(j, 2):
                        pe.wait_ge(*s["r_y"](j - 1))
                    for k, kp in enumerate(m.KH):
                        last = pe.matmul(bank[6 + q % 2][:, 0:D], hT[q % 2][0:kp, k, :],
                                         L["w2"][k][:, bass.ds(e, 1), :], start=(k == 0), stop=(k == len(m.KH) - 1))
                    last.then_inc(s["r_down"].sem, 1)

                def step(j, q, r):
                    if not known(j) or j < m.TILES:
                        up(j, q, r)
                    if not known(j) or j + 2 < m.TILES:
                        xT(j + 2, (q + 2) % R, r if q < R - 2 else r + 1)
                    if after(j, 1) and (not known(j) or j - 1 < m.TILES):
                        hid(j - 1, (q - 1) % R, None)
                    if after(j, 2):
                        down(j - 2, (q - 2) % R, None)

                loaded(pe, s["kind"] + "_experts")
                pe.wait_ge(*s["experts"](1))
                xT(0, 0, 0)
                xT(1, 1, 0)
                rounds(pe, m.TILES, step, more=2)

            def recurrence(s):
                loaded(pe, "h")

                def project(g):
                    pe.wait_ge(*s["xT"](GT * (g + 1)))
                    for c in range(KD):
                        n = KD * g + c
                        for w, b, psum, used in (("wf", 2, s["f_psum"], s["in_"]), ("wi", 3, s["i_psum"], s["t1"]),
                                                 ("wg", 4, s["g_psum"], s["gw"])):
                            if after(g, 1) or c:
                                pe.wait_ge(*used(n))
                            for k in range(KD):
                                last = pe.matmul(bank[b][:, :], hw[w][:, k, c * P:(c + 1) * P],
                                                 XT[:, k, bass.ds(g * GW, GW)], start=(k == 0), stop=(k == KD - 1))
                            last.then_inc(psum.sem, 1)

                def squares(g):
                    if g:
                        pe.wait_ge(*s["ms"](g))
                    pe.wait_ge(*s["sq"](KD * (g + 1)))
                    for t in range(GT):
                        for c in range(KD):
                            last = pe.matmul(bank[5][:, t:t + 1], g_sq[c][:, t * P:(t + 1) * P], ones[:, 0:1],
                                             start=(c == 0), stop=(c == KD - 1))
                    last.then_inc(s["ms_psum"].sem, 1)

                def project_out(g):
                    pe.wait_ge(*s["t"](KD * (g + 1)))
                    for t in range(GT):
                        i = GT * g + t
                        if after(g, 1) or t >= 2:
                            pe.wait_ge(*s["x_new"](i - 1))
                        for c in range(KD):
                            last = pe.matmul(bank[6 + t % 2][:, 0:D], g_t[:, c, t * P:(t + 1) * P], hw["wo"][:, c, :],
                                             start=(c == 0), stop=(c == KD - 1))
                        last.then_inc(s["o_psum"].sem, 1)

                def group(g):
                    for t in range(GT):
                        transpose_x(s, g, t)
                    project(g)
                    squares(g)

                for t in range(GT):
                    transpose_x(s, 0, t)
                for g in range(NG):
                    project(g)
                    if g:
                        project_out(g - 1)
                    if g + 1 < NG:
                        for t in range(GT):
                            transpose_x(s, g + 1, t)
                    squares(g)
                project_out(NG - 1)

            def attention(s):
                loaded(pe, "a")

                def transpose_group(g):
                    for t in range(GT):
                        transpose_x(s, g, t, banks=1)

                def project(b, w, psum):
                    for c in range(KD):
                        for k in range(KD):
                            last = pe.matmul(bank[1][:, c * S:(c + 1) * S], aw[w][:, k, c * P:(c + 1) * P],
                                             XT[:, k, bass.ds(b * S, S)], start=(k == 0), stop=(k == KD - 1))
                    last.then_inc(psum.sem, 1)

                def queries(b):
                    pe.wait_ge(*s["xT"](BT * (b + 1)))
                    if after(b, 1):
                        pe.wait_ge(*s["k"](KD * b))
                    project(b, "wq", s["q_psum"])

                def keys(b):
                    pe.wait_ge(*s["q"](HEADS * (b + 1)))
                    project(b, "wk", s["k_psum"])

                def values(b, side):
                    pe.wait_ge(*s["xTb"](b + 1))
                    if after(b, 3):
                        pe.wait_ge(*s["x_new"](BT * (b - 2)))
                    for t in range(BT):
                        for k in range(KD):
                            last = pe.matmul(bank[7][:, t * D:(t + 1) * D], xTb[:, side, k, t * P:(t + 1) * P],
                                             aw["wv"][:, k, :], start=(k == 0), stop=(k == KD - 1))
                    last.then_inc(s["v_psum"].sem, 1)

                def scores(b, h, side):
                    n = HEADS * b + h
                    if h == 0:
                        pe.wait_ge(*s["k"](KD * (b + 1)))
                    if after(b, 1) or h >= 2:
                        pe.wait_ge(*s["exp"](BT * (n - 1)))
                    for q in range(BT):
                        last = pe.matmul(bank[2 + h % 2][:, q * S:(q + 1) * S], qz[:, side, h, q * P:(q + 1) * P],
                                         kT[:, side, h // 2, :], start=True, stop=True)
                    last.then_inc(s["s_psum"].sem, 1)

                def transpose_weights(b, h):
                    n = HEADS * b + h
                    pe.wait_ge(*s["pm"](BT * (n + 1)))
                    if after(b, 1) or h >= 2:
                        pe.wait_ge(*s["pT"](n - 1))
                    for k in range(BT):
                        for q in range(BT):
                            last = pe.transpose(bank[4 + h % 2][:, k * S + q * P:k * S + (q + 1) * P],
                                                pm[h % 2][:, q, k * P:(k + 1) * P], ident[:, :])
                    last.then_inc(s["pT_psum"].sem, 1)

                def features(b, h, side):
                    n = HEADS * b + h
                    pe.wait_ge(*s["pT"](n + 1))
                    if h == 0:
                        pe.wait_ge(*s["v"](2 * (b + 1)))
                    if h % 2 == 0 and (after(b, 1) or h):
                        pe.wait_ge(*s["fT"](KD * b + h // 2))
                    for k in range(BT):
                        last = pe.matmul(bank[6][:, (h // 2) * S:(h // 2 + 1) * S],
                                         vz[:, side, k, h * P:(h + 1) * P], pT[h % 2][:, k, :],
                                         start=(h % 2 == 0 and k == 0), stop=(h % 2 == 1 and k == BT - 1))
                    last.then_inc(s["f_psum"].sem, 1)

                def project_out(b, side):
                    pe.wait_ge(*s["fT"](KD * (b + 1)))
                    if not known(b) or b + 2 < B:
                        pe.wait_ge(*s["v"](2 * (b + 3)))
                    for t in range(BT):
                        for c in range(KD):
                            last = pe.matmul(bank[7][:, t * D:(t + 1) * D], fT[:, side, c, t * P:(t + 1) * P],
                                             aw["wo"][:, c, :], start=(c == 0), stop=(c == KD - 1))
                    last.then_inc(s["o_psum"].sem, 1)

                def step(b, side):
                    for h in range(HEADS):
                        here = not known(b) or b < B
                        ahead = not known(b) or b + 1 < B
                        if here:
                            scores(b, h, side)
                        if ahead and h == 0:
                            queries(b + 1)
                        if ahead and h == 1:
                            keys(b + 1)
                        if ahead and h == 2:
                            values(b + 1, 1 - side)
                        pb, ph = back(b, h, 2)
                        if (after(b, 1) or h >= 2) and (not known(b) or pb < B):
                            transpose_weights(pb, ph)
                        pb, ph = back(b, h, 3)
                        if (after(b, 1) or h >= 3) and (not known(b) or pb < B):
                            features(pb, ph, side if h >= 3 else 1 - side)
                        if h == 3 and after(b, 1):
                            project_out(b - 1, 1 - side)
                        if known(b) and b < 2:
                            transpose_x(s, 2 + b, h, banks=1)

                transpose_group(0)
                queries(0)
                keys(0)
                transpose_group(1)
                values(0, 0)
                sequences(pe, step)
                step(B, 0)

            for s in stages:
                if s["mixes"]:
                    mixture(s)
                elif s["kind"] == "h":
                    recurrence(s)
                else:
                    attention(s)

        @block.vector
        def _(dve):
            def x_tile(g, t):
                return X[:, bass.ds(GT * g + t, 1), :].rearrange("p a d -> p (a d)")

            def combine(s, g):
                for t in range(GT):
                    dve.wait_ge(*s["y_in"][t](16 * (g + 1)))
                    dve.scalar_tensor_tensor(x_tile(g, t), yab[t][:, 0, :], wts[:, 0, bass.ds(GT * g + t, 1)], x_tile(g, t),
                                             ALU.mult, ALU.add).then_inc(s["combined1"].sem, 1)
                for t in range(GT):
                    dve.wait_ge(*s["combined1"](GT * g + t + 1))
                    dve.scalar_tensor_tensor(x_tile(g, t), yab[t][:, 1, :], wts[:, 1, bass.ds(GT * g + t, 1)], x_tile(g, t),
                                             ALU.mult, ALU.add).then_inc(s["x_new"].sem, 1)

            def moments(s, g):
                if s["prev"] is None:
                    dve.wait_ge(x_in[g], 16)
                else:
                    if s["prev"]["mixes"]:
                        combine(s["prev"], g)
                    dve.wait_ge(*s["prev"]["x_new"](GT * (g + 1)))
                for i in range(GT * g, GT * (g + 1)):
                    dve.bn_stats(st[:, i, :], X[:, i, :]).then_inc(s["stats"].sem, 1)
                for i in range(GT * g, GT * (g + 1)):
                    dve.wait_ge(*s["stats"](i + 1))
                    last = dve.bn_aggr(mv[:, i, :], st[:, i, :])
                last.then_inc(s["aggr"].sem, 1)

            def normalise(s, g):
                span = slice(GT * g, GT * (g + 1))
                dve.wait_ge(*s["stdev"](g + 1))
                dve.reciprocal(rs[:, span], sd[:, span]).then_inc(s["rstd"].sem, 1)
                dve.wait_ge(*s["rstd"](g + 1))
                for i in range(GT * g, GT * (g + 1)):
                    dve.tensor_scalar(XN[:, i, :], X[:, i, :], mv[:, i, 0:1], rs[:, i:i + 1],
                                      ALU.subtract, ALU.mult).then_inc(s["xn"].sem, 1)

            def norm(s, g):
                moments(s, g)
                normalise(s, g)

            def mixture(s):
                L = LAYERS[s["kind"]]
                m = L["m"]
                E, nk, NT = m.E, len(m.KS), m.TILES
                steps = [0]

                def chain(ins):
                    steps[0] += 1
                    ins.then_inc(s["route"].sem, 1)
                    dve.wait_ge(*s["route"](steps[0]))

                def by_expert(ap):
                    return ap[:, 0:NTT * E].rearrange("p (t e) -> p t e", e=E)

                score, sel, tmp, pos = (by_expert(x) for x in (f_score, f_sel, f_tmp, f_pos))
                oh = [by_expert(x) for x in f_oh]
                numbers = iota[:, 0:E]

                def over_experts(ap):
                    return ap.unsqueeze(2).broadcast_to((P, NTT, E))

                def choices():
                    dve.wait_ge(*s["scored"](1))
                    loaded(dve, s["kind"] + "_router")
                    chain(dve.tensor_tensor(sel, score, L["bias"][:, :].unsqueeze(1).broadcast_to((P, NTT, E)), ALU.add))
                    number = numbers.unsqueeze(1).broadcast_to((P, NTT, E))
                    for k in range(2):
                        top = f_top[:, k, :]
                        chain(dve.tensor_reduce(top, sel, AX.X, ALU.max))
                        chain(dve.tensor_tensor(tmp, sel, over_experts(top), ALU.is_equal))
                        chain(dve.scalar_tensor_tensor(tmp, number, float(E), tmp, ALU.subtract, ALU.mult))
                        chain(dve.tensor_reduce(f_sum, tmp, AX.X, ALU.min))
                        chain(dve.tensor_scalar(f_sum, f_sum, float(E), None, ALU.add))
                        chain(dve.tensor_tensor(oh[k], number, over_experts(f_sum), ALU.is_equal))
                        if k == 0:
                            chain(dve.scalar_tensor_tensor(sel, oh[0], -BIG, sel, ALU.mult, ALU.add))
                    chain(dve.memset(f_m16[:, NTT * E:(NTT + 1) * E], 0.0))
                    dve.tensor_tensor(f_m16[:, 0:NTT * E].rearrange("p (t e) -> p t e", e=E), oh[0], oh[1],
                                      ALU.add).then_inc(s["both"].sem, 1)

                def weights():
                    for k in range(2):
                        chain(dve.tensor_tensor(tmp, oh[k], score, ALU.mult))
                        chain(dve.tensor_reduce(f_top[:, k, :], tmp, AX.X, ALU.add))
                    chain(dve.tensor_tensor(f_sum, f_top[:, 0, :], f_top[:, 1, :], ALU.add))
                    if s["kind"] == "f0":
                        chain(dve.tensor_scalar(f_sum, f_sum, 1e-12, None, ALU.max))
                    else:
                        chain(dve.tensor_scalar(f_sum, f_sum, 1e-20, None, ALU.add))
                    chain(dve.reciprocal(f_sum, f_sum))
                    for k in range(2):
                        chain(dve.scalar_tensor_tensor(wts[:, k, :], f_top[:, k, :], 0.5, f_sum, ALU.mult, ALU.mult))

                def places():
                    dve.wait_ge(*s["pos_psum"](1))
                    p0 = bank[0][:, 0:NTT * E].rearrange("p (t e) -> p t e", e=E)
                    total = bank[0][:, NTT * E:(NTT + 1) * E]
                    tiles_i, tiles_f, cum, base = f_til[:, 0:E], f_tilf[:, 0:E], f_cum[:, 0:E], f_base[:, 0:E]
                    chain(dve.tensor_scalar(f_cnt[:, 0:E], total, float(P - 1), None, ALU.add))
                    chain(dve.tensor_scalar(tiles_i, f_cnt[:, 0:E], 7, None, ALU.arith_shift_right))
                    chain(dve.tensor_copy(tiles_f, tiles_i))
                    chain(dve.tensor_tensor_scan(cum, ones[:, 0:E], tiles_f, 0.0, ALU.mult, ALU.add))
                    chain(dve.tensor_tensor(base, cum, tiles_f, ALU.subtract))
                    chain(dve.tensor_scalar(base, base, float(P), None, ALU.mult))
                    chain(dve.tensor_tensor(pos, p0, base.unsqueeze(1).broadcast_to((P, NTT, E)), ALU.add))
                    for k in range(2):
                        chain(dve.tensor_tensor(tmp, oh[k], pos, ALU.mult))
                        chain(dve.tensor_reduce(f_slotf[:, k, :], tmp, AX.X, ALU.add))
                    flat = "p a b -> p (a b)"
                    si, sf = slots[:, :, :].rearrange(flat), f_slotf.rearrange(flat)
                    dve.tensor_copy(si, sf).then_inc(s["slotted"].sem, 1)

                def marks():
                    flat = "p a b -> p (a b)"
                    si = slots[:, :, :].rearrange(flat)
                    dve.wait_ge(*s["slotted"](1))
                    chain(dve.tensor_scalar(f_hi.rearrange(flat), si, 7, None, ALU.arith_shift_right))
                    chain(dve.tensor_scalar(f_lo.rearrange(flat), si, P - 1, None, ALU.bitwise_and))
                    chain(dve.tensor_copy(f_hif.rearrange(flat), f_hi.rearrange(flat)))
                    chain(dve.tensor_copy(f_lof.rearrange(flat), f_lo.rearrange(flat)))
                    for k in range(2):
                        chain(dve.tensor_tensor(f_hi16[k][:, :, 0:NT], iota[:, 0:NT].unsqueeze(1).broadcast_to((P, NTT, NT)),
                                                f_hif[:, k, :].unsqueeze(2).broadcast_to((P, NTT, NT)), ALU.is_equal))
                        chain(dve.tensor_tensor(f_tok16[k][:, :, 0:NT], f_hi16[k][:, :, 0:NT],
                                                tokens16[:, :].unsqueeze(2).broadcast_to((P, NTT, NT)), ALU.mult))
                        dve.tensor_tensor(f_lo16[k], iota[:, :].unsqueeze(1).broadcast_to((P, NTT, P)),
                                          f_lof[:, k, :].unsqueeze(2).broadcast_to((P, NTT, P)),
                                          ALU.is_equal).then_inc(s["marks"].sem, 1)
                    ge = f_ge[:, 0:NT, 0:E]
                    chain(dve.tensor_tensor(ge, iota[0:1, 0:NT].unsqueeze(2).broadcast_to((1, NT, E)),
                                            f_cum[0:1, 0:E].unsqueeze(1).broadcast_to((1, NT, E)), ALU.is_ge))
                    chain(dve.tensor_reduce(f_eidf[:, 0:NT], ge, AX.X, ALU.add))
                    dve.tensor_scalar(f_eid[:, 0:NT], f_eidf[:, 0:NT], float(E - 1), None, ALU.min).then_inc(s["experts"].sem, 1)

                def rows():
                    dve.wait_ge(*s["map_psum"](1))
                    both = f_map[:, :, 0:NT]
                    full, empty, second = f_full[:, 0:NT], f_empty[:, 0:NT], f_second[:, 0:NT]
                    chain(dve.tensor_copy(both, bank[1][:, 0:2 * NT].rearrange("p (k j) -> p k j", k=2)))
                    chain(dve.tensor_tensor(full, both[:, 0, :], both[:, 1, :], ALU.add))
                    chain(dve.scalar_tensor_tensor(empty, full, 0.0, spare[:, 0:NT], ALU.is_equal, ALU.mult))
                    chain(dve.tensor_scalar(second, both[:, 1, :], 0.0, float(T), ALU.is_gt, ALU.mult))
                    chain(dve.scalar_tensor_tensor(full, full, -1.0, second, ALU.add, ALU.add))
                    dve.tensor_tensor(f_rows[:, 0:NT], full, empty, ALU.add).then_inc(s["rows"].sem, 1)

                def shared_hidden(first, end):
                    for n in range(first, end):
                        g, c = n // nk, n % nk
                        kp = m.KS[c]
                        dve.wait_ge(*s["silu"](n + 1))
                        if g >= 3:
                            dve.wait_ge(*s["down"](GT * (g - 2)))
                        dve.tensor_tensor(f_HT[g % 3][0:kp, c, :], f_sg[n % 2][0:kp, :], bank[4 + n % 2][0:kp, :],
                                          ALU.mult).then_inc(s["hid"].sem, 1)

                def shared_add(g):
                    for t in range(GT):
                        i = GT * g + t
                        dve.wait_ge(*s["down"](i + 1))
                        dve.scalar_tensor_tensor(X[:, i, :], bank[6 + i % 2][:, 0:D], 0.5, X[:, i, :],
                                                 ALU.mult, ALU.add).then_inc(s["shared_added"].sem, 1)

                moments(s, 0)
                moments(s, 1)
                for g in range(NG):
                    normalise(s, g)
                    if g + 2 < NG:
                        moments(s, g + 2)
                shared_hidden(0, 2 * nk)
                choices()
                shared_hidden(2 * nk, 2 * nk + nk // 2)
                places()
                shared_hidden(2 * nk + nk // 2, 3 * nk)
                marks()
                shared_add(0)
                shared_hidden(3 * nk, 4 * nk)
                rows()
                weights()
                for g in range(1, NG):
                    shared_add(g)
                dve.wait_ge(*s["shared_added"](NTT))
                assert steps[0] == ROUTE_STEPS, steps

                def hid(j, q, r):
                    dve.wait_ge(*s["r_silu"](j + 1))
                    if after(j, 2):
                        dve.wait_ge(*s["r_hT_psum"](j - 1))
                    dve.tensor_tensor(hh[q % 2][:, 0:m.H], sg[q % 2][:, 0:m.H], bank[2 + q % 2][:, m.H:2 * m.H],
                                      ALU.mult).then_inc(s["r_hid"].sem, 1)

                def hidT(j, q, r):
                    dve.wait_ge(*s["r_hT_psum"](j + 1))
                    if after(j, 2):
                        dve.wait_ge(*s["r_down"](j - 1))
                    for k, kp in enumerate(m.KH):
                        last = dve.tensor_copy(hT[q % 2][0:kp, k, :], bank[4 + q % 2][0:kp, k * P:(k + 1) * P])
                    last.then_inc(s["r_hT"].sem, 1)

                def step(j, q, r):
                    if after(j, 1):
                        hidT(j - 1, (q - 1) % R, None)
                    if not known(j) or j < NT:
                        hid(j, q, r)

                rounds(dve, NT, step, more=1)

            def add_out(s, g, first_bank, scale=None):
                for t in range(GT):
                    dve.wait_ge(*s["o_psum"](GT * g + t + 1))
                    psum = bank[first_bank + t % 2][:, 0:D]
                    if scale is None:
                        ins = dve.tensor_tensor(x_tile(g, t), psum, x_tile(g, t), ALU.add)
                    else:
                        ins = dve.scalar_tensor_tensor(x_tile(g, t), psum, scale[:, t:t + 1], x_tile(g, t),
                                                       ALU.mult, ALU.add)
                    ins.then_inc(s["x_new"].sem, 1)

            def recurrence(s):
                loaded(dve, "h")

                def front(g):
                    for c in range(KD):
                        n = KD * g + c
                        dve.wait_ge(*s["si"](n + 1))
                        dve.tensor_tensor(g_t1[c], g_si[c], bank[3][:, :], ALU.mult).then_inc(s["t1"].sem, 1)
                        dve.wait_ge(*s["sq"](n + 1))
                        dve.tensor_scalar(g_gw[c], bank[4][:, :], hnorm[:, c:c + 1], None, ALU.mult).then_inc(s["gw"].sem, 1)
                        dve.wait_ge(*s["t1"](n + 1))
                        dve.tensor_tensor(g_t1[c], g_t1[c], g_in[c], ALU.mult).then_inc(s["t2"].sem, 1)
                        dve.wait_ge(*s["t2"](n + 1))
                        for b in range(GW // S):
                            seq = slice(b * S, (b + 1) * S)
                            last = dve.tensor_tensor_scan(g_o[c][:, seq], g_keep[c][:, seq], g_t1[c][:, seq], 0.0,
                                                          ALU.mult, ALU.add)
                        last.then_inc(s["scan"].sem, 1)

                def back(g):
                    dve.wait_ge(*s["ms"](g + 1))
                    dve.reciprocal(g_rms[g], g_ms).then_inc(s["rms"].sem, 1)
                    dve.wait_ge(*s["rms"](g + 1))
                    for c in range(KD):
                        n = KD * g + c
                        dve.wait_ge(*s["so"](n + 1))
                        dve.tensor_tensor(g_so[c], g_o[c], g_so[c], ALU.mult).then_inc(s["t3"].sem, 1)
                        dve.wait_ge(*s["t3"](n + 1))
                        if after(g, 1):
                            dve.wait_ge(*s["o_psum"](GT * g))
                        dve.tensor_tensor(g_t[:, c, :], g_so[c], g_gw[c], ALU.mult).then_inc(s["t"].sem, 1)

                norm(s, 0)
                norm(s, 1)
                for g in range(NG):
                    front(g)
                    if g:
                        add_out(s, g - 1, 6, g_rms[g - 1])
                    if g + 2 < NG:
                        moments(s, g + 2)
                    back(g)
                    if g + 2 < NG:
                        normalise(s, g + 2)
                add_out(s, NG - 1, 6, g_rms[NG - 1])

            def attention(s):
                loaded(dve, "a")

                def rest(s, g):
                    normalise(s, g)
                    span = slice(GT * g, GT * (g + 1))
                    dve.wait_ge(*s["xn"](GT * (g + 1)))
                    dve.tensor_tensor(X[:, span, :], X[:, span, :], abo[:, :].unsqueeze(1).broadcast_to((P, GT, D)),
                                      ALU.add).then_inc(s["bo"].sem, 1)

                def values(b, side):
                    dve.wait_ge(*s["v_psum"](b + 1))
                    if after(b, 2):
                        dve.wait_ge(*s["f_psum"](HEADS * (b - 1)))
                    for p in range(2):
                        dve.tensor_tensor(
                            vz[:, side].rearrange("p t (c n) -> p t c n", c=KD)[:, :, :, p * (P + HD):p * (P + HD) + HD],
                            bank[7][:, :].rearrange("p (t c h d) -> p t c h d", t=BT, c=KD, h=2)[:, :, :, p, :],
                            abv[:, :].rearrange("p (c h d) -> p c h d", c=KD, h=2)[:, :, p, :]
                            .unsqueeze(1).broadcast_to((P, BT, KD, HD)), ALU.add).then_inc(s["v"].sem, 1)

                def maxima(b, h):
                    n = HEADS * b + h
                    dve.wait_ge(*s["s_psum"](n + 1))
                    dve.tensor_reduce(mx[h % 2], bank[2 + h % 2][:, :].rearrange("p (q n) -> p q n", q=BT),
                                      AX.X, ALU.max).then_inc(s["mx"].sem, 1)
                    dve.wait_ge(*s["mx"](n + 1))
                    if after(b, 1) or h >= 2:
                        dve.wait_ge(*s["exp"](BT * (n - 1)))
                    dve.tensor_scalar(nm[h % 2], mx[h % 2], -SCORE_SCALE, None, ALU.mult).then_inc(s["nm"].sem, 1)

                def weights(b, h):
                    n = HEADS * b + h
                    dve.wait_ge(*s["exp"](BT * (n + 1)))
                    dve.reciprocal(ri[h % 2], sm[h % 2]).then_inc(s["ri"].sem, 1)
                    dve.wait_ge(*s["ri"](n + 1))
                    for q in range(BT):
                        dve.tensor_scalar(pm[h % 2][:, q, :], pm[h % 2][:, q, :], ri[h % 2][:, q:q + 1], None,
                                          ALU.mult).then_inc(s["pm"].sem, 1)

                def add_out(b):
                    dve.wait_ge(*s["o_psum"](b + 1))
                    dve.wait_ge(*s["bo"](NG))
                    for t in range(BT):
                        x = X[:, bass.ds(BT * b + t, 1), :].rearrange("p a d -> p (a d)")
                        dve.tensor_tensor(x, bank[7][:, t * D:(t + 1) * D], x, ALU.add).then_inc(s["x_new"].sem, 1)

                def step(b, side):
                    for h in range(HEADS):
                        if h == 3 and (not known(b) or b + 1 < B):
                            values(b + 1, 1 - side)
                        if not known(b) or b < B:
                            maxima(b, h)
                        pb, ph = back(b, h, 1)
                        if (after(b, 1) or h >= 1) and (not known(b) or pb < B):
                            weights(pb, ph)
                        if known(b) and (b, h) == (0, 0):
                            moments(s, 3)
                        if known(b) and (b, h) == (0, 1):
                            rest(s, 3)
                    if after(b, 1):
                        add_out(b - 1)

                moments(s, 0)
                moments(s, 1)
                rest(s, 0)
                rest(s, 1)
                moments(s, 2)
                dve.wait_ge(zero_q, 2)
                values(0, 0)
                rest(s, 2)
                sequences(dve, step)
                step(B, 0)

            for s in stages:
                if s["mixes"]:
                    mixture(s)
                elif s["kind"] == "h":
                    recurrence(s)
                else:
                    attention(s)
            for g in range(NG):
                combine(stages[-1], g)


def constants():
    k = np.arange(P)
    return {
        "ident": np.eye(P, dtype=np.float32),
        "ones": np.ones((P, P), np.float32),
        "ones16": np.ones((P, P), np.float16),
        "before16": (k[:, None] < k[None, :]).astype(np.float16),
        "iota": np.broadcast_to(k.astype(np.float32), (P, P)).copy(),
        "tokens16": (1 + k[:, None] + P * np.arange(NTT)[None, :]).astype(np.float16),
        "spare": (2 * T + 1 + k[:, None] + P * np.arange(MOE1.TILES)[None, :]).astype(np.float32),
    }


def kernel(**inputs):
    import concourse.bacc as _bacc
    from concourse.bass_utils import run_bass_kernel_spmd as _run

    v = {k: np.asarray(x) for k, x in inputs.items()}

    def on_partitions(w):
        return np.ascontiguousarray(np.moveaxis(w.reshape(-1, P, *w.shape[1:]), 0, 1))

    def rows(w):
        n = -(-w.shape[0] // P)
        full = np.zeros((n * P, w.shape[1]), w.dtype)
        full[:w.shape[0]] = w
        return on_partitions(full)

    arrays = dict(constants())
    arrays["x"] = np.ascontiguousarray(v["L0_attn_hidden_states"].reshape(T, D))
    f0, f1, h, at = "L0_ffn_", "L1_ffn_", "L0_attn_", "L1_attn_"
    arrays["f0_router"] = on_partitions(v[f0 + "gate_w"].T)
    arrays["f0_bias"] = np.broadcast_to(v[f0 + "router_bias"], (P, MOE0.E)).copy()
    arrays["f0_w13"] = on_partitions(np.concatenate([v[f0 + "W1"], v[f0 + "W3"]], axis=2).transpose(1, 0, 2))
    arrays["f0_w2"] = np.ascontiguousarray(v[f0 + "W2"].transpose(1, 0, 2))
    arrays["f0_s1"] = on_partitions(v[f0 + "sw1"].T)
    arrays["f0_s3"] = on_partitions(v[f0 + "sw3"].T)
    arrays["f0_s2"] = rows(v[f0 + "sw2"].T)
    arrays["f1_router"] = on_partitions(v[f1 + "gate_w"])
    arrays["f1_bias"] = np.broadcast_to(v[f1 + "expert_bias"], (P, MOE1.E)).copy()
    arrays["f1_w13"] = on_partitions(v[f1 + "experts_gate_up"].transpose(1, 0, 2))
    arrays["f1_w2"] = np.ascontiguousarray(v[f1 + "experts_down"].transpose(1, 0, 2))
    arrays["f1_s1"] = on_partitions(v[f1 + "shared_gate_w"])
    arrays["f1_s3"] = on_partitions(v[f1 + "shared_up_w"])
    arrays["f1_s2"] = rows(v[f1 + "shared_down_w"])
    for n, src in (("wf", "Wf"), ("wi", "Wi"), ("wg", "Wg"), ("wo", "Wo")):
        arrays["h_" + n] = on_partitions(v[h + src].T)
    arrays["h_norm"] = np.ascontiguousarray(v[h + "g_norm_weight"].reshape(KD, P).T)
    for n in ("q", "k", "v", "o"):
        arrays["a_w" + n] = on_partitions(v[at + "W" + n])
    arrays["a_bq"] = np.ascontiguousarray(v[at + "bq"].reshape(KD, P).T)
    arrays["a_bk"] = np.ascontiguousarray(v[at + "bk"].reshape(KD, P).T)
    arrays["a_bv"] = np.broadcast_to(v[at + "bv"], (P, D)).copy()
    arrays["a_bo"] = np.broadcast_to(v[at + "bo"], (P, D)).copy()

    nc = _bacc.Bacc("TRN2", target_bir_lowering=False, num_devices=1)
    args = {n: nc.dram_tensor("in_" + n, x.shape, mybir.dt.from_np(x.dtype), kind="ExternalInput").ap()
            for n, x in arrays.items()}
    out = nc.dram_tensor("out_x", (T, D), F32, kind="ExternalOutput").ap()
    macaron_kernel(nc, args, out)
    r = _run(nc, [{"in_" + n: x for n, x in arrays.items()}], core_ids=[0])
    return r.results[0]["out_x"].reshape(B, S, D)
```

```python
import numpy as np
import concourse.bass as bass
from concourse import mybir
from contextlib import ExitStack

F32 = mybir.dt.float32
F16 = mybir.dt.float16
I32 = mybir.dt.int32
ALU = mybir.AluOpType
ACT = mybir.ActivationFunctionType
AX = mybir.AxisListType

P = 128
D = 256
KD = D // P
R = 8
B, S = 8, 256
BT = S // P
T = B * S
NTT = T // P
GT = 4
NG = NTT // GT
GW = GT * P
EPS = 1e-5
HEADS = 4
HD = D // HEADS
SCORE_SCALE = 0.5
BIG = 1.0e30


class Moe:

    def __init__(self, experts, hidden, shared):
        self.E, self.H, self.SH = experts, hidden, shared
        self.TILES = -(-(2 * T // P + experts - 1) // R) * R
        self.KH = [min(P, hidden - k) for k in range(0, hidden, P)]
        self.KS = [min(P, shared - k) for k in range(0, shared, P)]


MOE0 = Moe(8, 176, 352)
MOE1 = Moe(16, 128, 128)
MAXE = 16


def macaron_kernel(nc, a, out):
    ctx = ExitStack()
    with ctx:
        def sb(name, shape, dt=F32):
            return ctx.enter_context(nc.sbuf_tensor(name, shape, dt))

        def sem(name):
            return ctx.enter_context(nc.semaphore(name))

        X = sb("X", [P, NTT, D])
        XT = sb("XT", [P, KD, T])
        XN = sb("XN", [P, NTT, D])
        ident = sb("ident", [P, P])
        ones = sb("ones", [P, P])
        ones16 = sb("ones16", [P, P], F16)
        before16 = sb("before16", [P, P], F16)
        iota = sb("iota", [P, P])
        tokens16 = sb("tokens16", [P, NTT], F16)
        spare = sb("spare", [P, MOE1.TILES])
        epsc = sb("epsc", [P, 1])
        w13_at = sb("w13", [P, KD * MOE1.E * 2 * MOE1.H])
        w2_at = sb("w2", [P, MOE1.E * D])
        LAYERS = {}
        for n, m in (("f0", MOE0), ("f1", MOE1)):
            w2 = w2_at[:, :].rearrange("p (k e d) -> p k e d", k=len(m.KH), e=m.E)
            LAYERS[n] = dict(
                m=m,
                router=sb(n + "_router", [P, KD, m.E]),
                bias=sb(n + "_bias", [P, m.E]),
                w13=w13_at[:, 0:KD * m.E * 2 * m.H].rearrange("p (k e h) -> p k e h", k=KD, e=m.E),
                w2=[w2[0:kp, k] for k, kp in enumerate(m.KH)],
                s1=sb(n + "_s1", [P, KD, m.SH]),
                s3=sb(n + "_s3", [P, KD, m.SH]),
                s2=sb(n + "_s2", [P, len(m.KS), D]),
            )
        hw = {n: sb("h_" + n, [P, KD, D]) for n in ("wf", "wi", "wg", "wo")}
        hnorm = sb("h_norm", [P, KD])
        aw = {n: sb("a_" + n, [P, KD, D]) for n in ("wq", "wk", "wv", "wo")}
        abq = sb("a_bq", [P, KD])
        abk = sb("a_bk", [P, KD])
        abv = sb("a_bv", [P, D])
        abo = sb("a_bo", [P, D])

        st = sb("st", [P, NTT, 6])
        mv = sb("mv", [P, NTT, 2])
        sd = sb("sd", [P, NTT])
        rs = sb("rs", [P, NTT])
        zeros = sb("zeros", [P, D])
        wts = sb("wts", [P, 2, NTT])
        slots = sb("slots", [P, 2, NTT], I32)
        ARENA = 14400
        arena = sb("arena", [P, ARENA])

        class Carve:
            def __init__(self):
                self.at = 0

            def __call__(self, *shape, dt=F32, parts=P):
                size = 1
                for s in shape:
                    size *= s
                cols = -(-size * (2 if dt == F16 else 4) // 4)
                ap = arena[0:parts, self.at:self.at + cols]
                self.at += cols
                assert self.at <= ARENA, self.at
                if dt != F32:
                    ap = ap.bitcast(dt)
                if len(shape) == 1:
                    return ap
                names = "abcd"[:len(shape)]
                return ap.rearrange(f"p ({' '.join(names)}) -> p {' '.join(names)}",
                                    **{n: s for n, s in zip(names[1:], shape[1:])})

        c = Carve()
        lgT = c(GW)
        f_score = c(NTT * MAXE)
        f_sel = c(NTT * MAXE)
        f_tmp = c(NTT * MAXE)
        f_oh = [c(NTT * MAXE), c(NTT * MAXE)]
        f_m16 = c((NTT + 1) * MAXE, dt=F16)
        f_pos = c(NTT * MAXE)
        f_top = c(2, NTT)
        f_sum = c(NTT)
        f_slotf = c(2, NTT)
        f_hi = c(2, NTT, dt=I32)
        f_lo = c(2, NTT, dt=I32)
        f_hif = c(2, NTT)
        f_lof = c(2, NTT)
        f_cnt = c(MAXE, dt=I32)
        f_til = c(MAXE, dt=I32)
        f_tilf = c(MAXE)
        f_cum = c(MAXE)
        f_base = c(MAXE)
        shared_at = c.at
        f_lo16 = [c(NTT, P, dt=F16) for _ in range(2)]
        f_hi16 = [c(NTT, 48, dt=F16) for _ in range(2)]
        f_tok16 = [c(NTT, 48, dt=F16) for _ in range(2)]
        f_ge = c(48, MAXE, parts=1)
        marks_end, c.at = c.at, shared_at
        xs = [c(D) for _ in range(R)]
        xsT = [c(KD, P) for _ in range(2)]
        sg = [c(176) for _ in range(2)]
        hh = [c(176) for _ in range(2)]
        hT = [c(2, P) for _ in range(2)]
        ys = [c(D) for _ in range(R)]
        c.at = max(c.at, marks_end)
        f_map = c(2, 48)
        f_full = c(48)
        f_empty = c(48)
        f_second = c(48)
        f_rows = c(48, dt=I32)
        f_eidf = c(48, parts=1)
        f_eid = c(48, dt=I32, parts=1)
        f_sg = [c(GW) for _ in range(2)]
        f_HT = [c(3, GW) for _ in range(3)]
        c = Carve()
        g_keep = [c(GW) for _ in range(KD)]
        g_in = [c(GW) for _ in range(KD)]
        g_si = [c(GW) for _ in range(KD)]
        g_t1 = [c(GW) for _ in range(KD)]
        g_o = [c(GW) for _ in range(KD)]
        g_so = [c(GW) for _ in range(KD)]
        g_sq = c(2, KD, GW)
        g_gw = [c(GW) for _ in range(KD)]
        g_ms = c(NTT)
        g_rms = c(NTT)
        g_t = c(2, KD, GW)
        c = Carve()
        qz = c(2, HEADS, S)
        kT = c(2, KD, S)
        vz = c(2, BT, KD * 2 * P)
        pm = [c(2, S) for _ in range(2)]
        pT = [c(2, S) for _ in range(2)]
        fT = c(2, KD, S)
        xTb = c(2, KD, S)
        mx = [c(2) for _ in range(2)]
        nm = [c(2) for _ in range(2)]
        sm = [c(2) for _ in range(2)]
        ri = [c(2) for _ in range(2)]

        bank = [ctx.enter_context(nc.psum_tensor(f"bank{i}", [P, 512], F32)) for i in range(8)]

        x_rows = nc.dram_tensor("slot_rows", (MOE1.TILES * P, D), F32, kind="Internal").ap()
        y_rows = {n: nc.dram_tensor(n + "_result_rows", (2 * T + L["m"].TILES * P, D), F32, kind="Internal").ap()
                  for n, L in LAYERS.items()}

        x_in = [sem(f"x_in{g}") for g in range(NG)]
        loads = {}
        order = [("const", [(ident, a["ident"]), (ones, a["ones"]), (ones16, a["ones16"]),
                            (before16, a["before16"]), (iota, a["iota"]),
                            (tokens16, a["tokens16"]), (spare, a["spare"])])]
        for n in ("f0", "h", "f1", "a"):
            if n in LAYERS:
                L = LAYERS[n]
                order.append((n + "_router", [(L["router"], a[n + "_router"]), (L["bias"], a[n + "_bias"])]))
                order.append((n + "_shared", [(L["s1"], a[n + "_s1"]), (L["s3"], a[n + "_s3"]), (L["s2"], a[n + "_s2"])]))
                k0 = 0
                w2 = []
                for k, kp in enumerate(L["m"].KH):
                    w2.append((L["w2"][k], a[n + "_w2"][k0:k0 + kp]))
                    k0 += kp
                order.append((n + "_experts", [(L["w13"], a[n + "_w13"])] + w2))
            elif n == "h":
                order.append(("h", [(hw[k], a["h_" + k]) for k in hw] + [(hnorm, a["h_norm"])]))
            else:
                order.append(("a", [(aw[k], a["a_" + k]) for k in aw]
                              + [(abq, a["a_bq"]), (abk, a["a_bk"]), (abv, a["a_bv"]), (abo, a["a_bo"])]))
        for name, parts in order:
            loads[name] = (sem("in_" + name), 16 * len(parts))

        def load_now(eng, name):
            for dst, src in dict(order)[name]:
                full = dst[tuple(slice(None) for _ in dst.shape)]
                eng.dma_start(full, src).then_inc(loads[name][0], 16)

        def loaded(eng, name):
            eng.wait_ge(*loads[name])

        zero_q = sem("zero_q")
        eps_set = sem("eps_set")
        zeros_set = sem("zeros_set")
        rows_set = sem("rows_set")

        class Count:

            def __init__(self, of, start):
                self.sem, self.start = of, start

            def __call__(self, n):
                return self.sem, self.start + n

        made, left_at = {}, {}

        def count(name, total):
            if name not in made:
                made[name], left_at[name] = sem(name), 0
            got = Count(made[name], left_at[name])
            left_at[name] += total
            return got

        ROUTE_STEPS = 50

        def stage(number, kind, prev):
            totals = dict(stats=NTT, aggr=NG, stdev=NG, rstd=NG, xn=NTT, xT_psum=NTT, xT=NTT)
            mixes = kind in LAYERS
            lists = {}
            if mixes:
                m = LAYERS[kind]["m"]
                nk, tiles = len(m.KS), m.TILES
                totals |= dict(weighted1=NTT, combined1=NTT, slotted=1, rows_out=16 * 2 * NTT, rl_psum=NG, rl_copied=NG, lg_psum=NG, scored=1,
                               route=ROUTE_STEPS, both=1, pos_psum=1, marks=2, map_psum=1, rows=1, experts=1,
                               up=NG * nk, silu=NG * nk, hid=NG * nk, down=NTT, shared_added=NTT)
                totals |= {k: tiles for k in ("r_xT_psum", "r_xT", "r_up", "r_silu", "r_hid", "r_hT_psum",
                                              "r_hT", "r_down", "r_y")}
                lists = dict(row_in=(R, 16 * tiles // R), y_out=(R, 16 * tiles // R), y_in=(NG, 16 * (1 + KD)))
            elif kind == "h":
                totals |= {k: KD * NG for k in ("f_psum", "i_psum", "g_psum", "keep", "in_", "si", "sq", "t1",
                                                "t2", "scan", "gw", "so", "t3", "t")}
                totals |= dict(ms_psum=NG, ms=NG // 2, rms=NG // 2, o_psum=NTT)
            else:
                totals |= dict(q_psum=B, q=B * HEADS, k_psum=B, k=B * KD, xTb=B, v_psum=B, v=2 * B,
                               f_psum=B * HEADS, fT=B * KD, o_psum=B, bo=NG, exp=B * 2 * HEADS, pm=B * 2 * HEADS)
                totals |= {k: B * HEADS for k in ("s_psum", "mx", "nm", "ri", "pT_psum", "pT")}
            got = {k: count(k, n) for k, n in totals.items()}
            got |= {k: [count(f"{k}{q}", n) for q in range(copies)] for k, (copies, n) in lists.items()}
            got |= dict(kind=kind, prev=prev, mixes=mixes, before_attention=False, x_new=count(f"x_new{number % 2}", NTT))
            return got

        stages, prev = [], None
        for number, kind in enumerate(["f0", "h", "f0", "f1", "a", "f1"]):
            if prev is not None:
                prev["before_attention"] = kind == "a"
            prev = stage(number, kind, prev)
            stages.append(prev)
        out_stored = sem("out_stored")

        def known(j):
            return isinstance(j, int)

        def after(j, n):
            return not known(j) or j >= n

        def rounds(eng, tiles, body, more=0, ahead=None):
            ahead = ahead or (lambda j, n: None)
            ahead(0, 2 * R - 2)
            for j in range(2 * R - 2):
                body(j, j % R, j // R)
            with eng.Fori(1, tiles // R - 1) as i:
                ahead(R * i + R - 2, R)
                for u in range(R - 2, 2 * R - 2):
                    body(R * i + u, u % R, i + u // R)
            ahead(tiles - 2, 2)
            for j in range(tiles - 2, tiles + more):
                body(j, j % R, j // R)

        def sequences(eng, body):
            body(0, 0)
            body(1, 1)
            with eng.Fori(1, B // 2 - 1) as i:
                body(2 * i, 0)
                body(2 * i + 1, 1)
            body(B - 2, 0)
            body(B - 1, 1)

        def back(b, h, n):
            return (b, h - n) if h >= n else (b - 1, h - n + HEADS)

        block = ctx.enter_context(nc.Block())

        @block.sync
        def _(sp):
            x_dram = a["x"].rearrange("(g t p) d -> g p t d", g=NG, p=P)

            def load_x(g):
                sp.dma_start(X[:, g * GT:(g + 1) * GT, :], x_dram[g]).then_inc(x_in[g], 16)

            load_x(0)
            load_now(sp, "const")
            load_x(1)
            load_now(sp, "f0_router")
            load_x(2)
            load_x(3)
            load_now(sp, "f0_shared")
            for g in range(NG):
                sp.wait_ge(x_in[g], 16)
            sp.wait_ge(zeros_set, 1)
            sp.dma_start(x_rows.rearrange("(n p) d -> p n d", p=P),
                         zeros[:, :].unsqueeze(1).broadcast_to((P, MOE1.TILES, D))).then_inc(rows_set, 16)
            load_now(sp, "f0_experts")
            sp.wait_ge(*loads["f0_shared"])
            for name in ("h", "f1_router", "f1_shared", "a"):
                load_now(sp, name)

            for n, s in enumerate(stages):
                if not s["mixes"]:
                    continue
                tiles = LAYERS[s["kind"]]["m"].TILES
                sp.wait_ge(*s["rows_out"](16 * 2 * NTT))
                sp.wait_ge(*s["map_psum"](1))

                def load_rows(j, q, r):
                    if after(j, R):
                        sp.wait_ge(*s["r_xT_psum"](j - R + 1))
                    sp.dma_start(xs[q], x_rows[bass.ds(j * P, P), :]).then_inc(s["row_in"][q].sem, 16)

                rounds(sp, tiles, load_rows)
                for q in range(R):
                    sp.wait_ge(*s["y_out"][q](16 * tiles // R))
                sp.wait_ge(*s["up"](NG * len(LAYERS[s["kind"]]["m"].KS)))
                first = y_rows[s["kind"]][0:T, :].rearrange("(g t p) d -> g p t d", g=NG, p=P)
                second = y_rows[s["kind"]][T:2 * T, :].rearrange("(g t p) d -> g p t d", g=NG, p=P)
                for g in range(NG):
                    sp.dma_start(XN[:, g * GT:(g + 1) * GT, :], first[g]).then_inc(s["y_in"][g].sem, 16)
                    for k in range(KD):
                        sp.dma_start(XT[:, k, g * GW:(g + 1) * GW].rearrange("p (t d) -> p t d", t=GT),
                                     second[g][:, :, k * P:(k + 1) * P]).then_inc(s["y_in"][g].sem, 16)
                if s["kind"] == "f0" and stages[n + 1]["kind"] == "f1":
                    load_now(sp, "f1_experts")

            last = stages[-1]
            out_t = out.rearrange("(g t p) d -> g p t d", g=NG, p=P)
            for g in range(NG):
                sp.wait_ge(*last["x_new"](GT * (g + 1)))
                sp.dma_start(out_t[g], X[:, g * GT:(g + 1) * GT, :]).then_inc(out_stored, 16)
            sp.wait_ge(out_stored, 16 * NG)

        @block.gpsimd
        def _(pool):
            pool.memset(epsc[:, :], EPS).then_inc(eps_set, 1)
            pool.memset(zeros[:, :], 0.0).then_inc(zeros_set, 1)
            pool.wait_ge(rows_set, 16)

            def scatter(dst, idx, src, done):
                pool.indirect_dma_start(out=dst, out_offset=bass.IndirectOffsetOnAxis(ap=idx, axis=0),
                                        in_=src, in_offset=None).then_inc(done.sem, 16)

            def copy_sequence(s, b):
                pool.wait_ge(*s["xT"](BT * (b + 1)))
                if b >= 2:
                    pool.wait_ge(*s["v_psum"](b - 1))
                pool.tensor_copy(xTb[:, b % 2], XT[:, :, b * S:(b + 1) * S]).then_inc(s["xTb"].sem, 1)

            for n, s in enumerate(stages):
                if s["kind"] == "a":
                    for b in range(2, B):
                        copy_sequence(s, b)
                if not s["mixes"]:
                    continue
                tiles = LAYERS[s["kind"]]["m"].TILES
                pool.wait_ge(*s["slotted"](1))
                for i in range(NTT):
                    for k in range(2):
                        scatter(x_rows, slots[:, k, i:i + 1], XN[:, i, :], s["rows_out"])
                pool.wait_ge(*s["rows"](1))
                for j in range(tiles):
                    pool.wait_ge(*s["r_y"](j + 1))
                    scatter(y_rows[s["kind"]], f_rows[:, j:j + 1], ys[j % R], s["y_out"][j % R])
                pool.wait_ge(*s["shared_added"](NTT))
                for i in range(NTT):
                    if s["before_attention"] and i == 2 * GT:
                        for q in range(R):
                            pool.wait_ge(*s["y_out"][q](16 * tiles // R))
                        pool.memset(qz, 0.0).then_inc(zero_q, 1)
                        pool.memset(vz, 0.0).then_inc(zero_q, 1)
                    if s["before_attention"] and i == 3 * GT:
                        copy_sequence(stages[n + 1], 0)
                        copy_sequence(stages[n + 1], 1)
                    pool.wait_ge(*s["weighted1"](i + 1))
                    pool.tensor_tensor(X[:, i, :], XN[:, i, :], X[:, i, :], ALU.add).then_inc(s["combined1"].sem, 1)

        @block.scalar
        def _(act):
            act.wait_ge(eps_set, 1)

            def weight(s, g):
                if s is None or not s["mixes"]:
                    return
                act.wait_ge(*s["y_in"][g](16 * (1 + KD)))
                for i in range(GT * g, GT * (g + 1)):
                    act.activation(XN[:, i, :], XN[:, i, :], ACT.Copy,
                                   scale=wts[:, 0, i:i + 1]).then_inc(s["weighted1"].sem, 1)

            def stdev(s, g):
                act.wait_ge(*s["aggr"](g + 1))
                act.activation(sd[:, bass.ds(g * GT, GT)], mv[:, bass.ds(g * GT, GT), 1], ACT.Sqrt,
                               bias=epsc[:, :]).then_inc(s["stdev"].sem, 1)

            def copy_xT(s, g, t, banks=2):
                act.wait_ge(*s["xT_psum"](GT * g + t + 1))
                act.activation(XT[:, :, bass.ds((GT * g + t) * P, P)],
                               bank[t % banks][:, 0:D].rearrange("p (k n) -> p k n", k=KD),
                               ACT.Copy).then_inc(s["xT"].sem, 1)

            def mixture(s):
                L = LAYERS[s["kind"]]
                m = L["m"]
                nk = len(m.KS)
                def logits(g):
                    act.wait_ge(*s["rl_psum"](g + 1))
                    act.activation(lgT[0:m.E, :], bank[6][0:m.E, :], ACT.Copy).then_inc(s["rl_copied"].sem, 1)

                def shared_silu(first, end):
                    for n in range(first, end):
                        kp = m.KS[n % nk]
                        act.wait_ge(*s["up"](n + 1))
                        if n >= 2:
                            act.wait_ge(*s["hid"](n - 1))
                        act.activation(f_sg[n % 2][0:kp, :], bank[2 + n % 2][0:kp, :], ACT.Silu).then_inc(s["silu"].sem, 1)

                for g in range(NG):
                    weight(s["prev"], g)
                stdev(s, 0)
                stdev(s, 1)
                for g in range(NG):
                    for t in range(GT):
                        copy_xT(s, g, t)
                    if g + 2 < NG:
                        stdev(s, g + 2)
                    logits(g)
                act.wait_ge(*s["lg_psum"](NG))
                act.activation(f_score[:, 0:NTT * m.E], bank[7][:, 0:NTT * m.E], ACT.Sigmoid).then_inc(s["scored"].sem, 1)
                shared_silu(0, NG * nk)

                def xT(j, q, r):
                    act.wait_ge(*s["r_xT_psum"](j + 1))
                    if after(j, 2):
                        act.wait_ge(*s["r_up"](j - 1))
                    act.activation(xsT[q % 2], bank[q % 2][:, 0:D].rearrange("p (k n) -> p k n", k=KD),
                                   ACT.Copy).then_inc(s["r_xT"].sem, 1)

                def silu(j, q, r):
                    act.wait_ge(*s["r_up"](j + 1))
                    if after(j, 2):
                        act.wait_ge(*s["r_hid"](j - 1))
                    act.activation(sg[q % 2][:, 0:m.H], bank[2 + q % 2][:, 0:m.H], ACT.Silu).then_inc(s["r_silu"].sem, 1)

                def y(j, q, r):
                    act.wait_ge(*s["r_down"](j + 1))
                    if after(j, R):
                        act.wait_ge(*s["y_out"][q](16 * r))
                    act.activation(ys[q], bank[6 + q % 2][:, 0:D], ACT.Copy).then_inc(s["r_y"].sem, 1)

                def step(j, q, r):
                    if not known(j) or j < m.TILES:
                        silu(j, q, r)
                    if not known(j) or j + 2 < m.TILES:
                        xT(j + 2, (q + 2) % R, None)
                    if after(j, 2):
                        y(j - 2, (q - 2) % R, r if q >= 2 else r - 1)

                xT(0, 0, 0)
                xT(1, 1, 0)
                rounds(act, m.TILES, step, more=2)

            def recurrence(s):
                def first(g):
                    for c in range(KD):
                        n = KD * g + c
                        f, i, gate = (bank[2 + (3 * n + k) % 4][:, :] for k in range(3))
                        act.wait_ge(*s["f_psum"](n + 1))
                        if g:
                            act.wait_ge(*s["scan"](n - KD + 1))
                        act.activation(g_keep[c], f, ACT.Sigmoid).then_inc(s["keep"].sem, 1)
                        act.activation(g_in[c], f, ACT.Sigmoid, scale=-1.0).then_inc(s["in_"].sem, 1)
                        if g < 2:
                            copy_xT(s, g + 2, 2 * c, banks=1)
                        act.wait_ge(*s["i_psum"](n + 1))
                        act.activation(g_si[c], i, ACT.Sigmoid).then_inc(s["si"].sem, 1)
                        if g < 2:
                            copy_xT(s, g + 2, 2 * c + 1, banks=1)
                        act.wait_ge(*s["g_psum"](n + 1))
                        if g >= 2:
                            act.wait_ge(*s["ms_psum"](g - 1))
                        act.activation(g_sq[:, g % 2, c, :], gate, ACT.Square).then_inc(s["sq"].sem, 1)
                        if g:
                            act.wait_ge(*s["t"](n - KD + 1))
                        act.activation(g_gw[c], gate, ACT.Copy, scale=hnorm[:, c:c + 1]).then_inc(s["gw"].sem, 1)

                def mean_squares(half):
                    act.wait_ge(*s["ms_psum"](2 * half + 2))
                    act.activation(g_ms[:, 2 * GT * half:2 * GT * (half + 1)], bank[1][:, 2 * GT * half:2 * GT * (half + 1)],
                                   ACT.Sqrt, scale=1.0 / D, bias=epsc[:, :]).then_inc(s["ms"].sem, 1)

                def second(g):
                    for c in range(KD):
                        n = KD * g + c
                        act.wait_ge(*s["scan"](n + 1))
                        if g:
                            act.wait_ge(*s["t"](n - KD + 1))
                        act.activation(g_so[c], g_o[c], ACT.Sigmoid).then_inc(s["so"].sem, 1)

                loaded(act, "h")
                for g in range(NG):
                    weight(s["prev"], g)
                for g in range(NG):
                    stdev(s, g)
                    if g < 2:
                        for t in range(GT):
                            copy_xT(s, g, t, banks=1)
                for g in range(NG):
                    first(g)
                    if g == 2:
                        mean_squares(0)
                    second(g)
                mean_squares(1)

            def attention(s):
                def copy_group(g):
                    for t in range(GT):
                        copy_xT(s, g, t, banks=1)

                def queries(b, side):
                    act.wait_ge(*s["q_psum"](b + 1))
                    for h in range(HEADS):
                        c, p = h // 2, h % 2
                        r = slice(p * HD, (p + 1) * HD)
                        act.activation(qz[r, side, h, :], bank[1][r, c * S:(c + 1) * S], ACT.Identity,
                                       bias=abq[r, c:c + 1]).then_inc(s["q"].sem, 1)

                def keys(b, side):
                    act.wait_ge(*s["k_psum"](b + 1))
                    for c in range(KD):
                        act.activation(kT[:, side, c, :], bank[1][:, c * S:(c + 1) * S], ACT.Identity,
                                       bias=abk[:, c:c + 1]).then_inc(s["k"].sem, 1)

                def exps(b, h):
                    n = HEADS * b + h
                    act.wait_ge(*s["nm"](n + 1))
                    if after(b, 1) or h >= 2:
                        act.wait_ge(*s["pT_psum"](n - 1))
                    for q in range(BT):
                        act.activation(pm[h % 2][:, q, :], bank[2 + h % 2][:, q * S:(q + 1) * S], ACT.Exp,
                                       scale=SCORE_SCALE, bias=nm[h % 2][:, q:q + 1],
                                       accum_out=sm[h % 2][:, q:q + 1]).then_inc(s["exp"].sem, 1)

                def copy_pT(b, h):
                    n = HEADS * b + h
                    act.wait_ge(*s["pT_psum"](n + 1))
                    if after(b, 1) or h >= 2:
                        act.wait_ge(*s["f_psum"](n - 1))
                    act.activation(pT[h % 2], bank[4 + h % 2][:, :].rearrange("p (k n) -> p k n", k=2),
                                   ACT.Copy).then_inc(s["pT"].sem, 1)

                def features(b, h, side):
                    act.wait_ge(*s["f_psum"](HEADS * b + h + 1))
                    act.activation(fT[:, side, h // 2, :], bank[6][:, (h // 2) * S:(h // 2 + 1) * S],
                                   ACT.Copy).then_inc(s["fT"].sem, 1)

                def step(b, side):
                    for h in range(HEADS):
                        if not known(b) or b < B:
                            exps(b, h)
                        if h == 0 and (not known(b) or b + 1 < B):
                            queries(b + 1, 1 - side)
                        if h == 1 and (not known(b) or b + 1 < B):
                            keys(b + 1, 1 - side)
                        pb, ph = back(b, h, 2)
                        if after(b, 1) or h >= 2:
                            if not known(b) or pb < B:
                                copy_pT(pb, ph)
                        pb, ph = back(b, h, 3)
                        if (after(b, 1) or h >= 3) and ph % 2 and (not known(b) or pb < B):
                            features(pb, ph, side if h >= 3 else 1 - side)
                        if known(b) and (b, h) == (0, 0):
                            stdev(s, 3)
                        if known(b) and b < 2:
                            copy_xT(s, 2 + b, h, banks=1)

                for g in range(NG):
                    weight(s["prev"], g)
                stdev(s, 0)
                stdev(s, 1)
                copy_group(0)
                act.wait_ge(zero_q, 2)
                queries(0, 0)
                keys(0, 0)
                stdev(s, 2)
                copy_group(1)
                sequences(act, step)
                step(B, 0)

            for s in stages:
                if s["mixes"]:
                    mixture(s)
                elif s["kind"] == "h":
                    recurrence(s)
                else:
                    attention(s)
            for g in range(NG):
                weight(stages[-1], g)

        @block.tensor
        def _(pe):
            loaded(pe, "const")

            def transpose_x(s, g, t, banks=2):
                i = GT * g + t
                pe.wait_ge(*s["xn"](i + 1))
                if i >= banks:
                    pe.wait_ge(*s["xT"](i - banks + 1))
                for k in range(KD):
                    last = pe.transpose(bank[t % banks][:, k * P:(k + 1) * P], XN[:, i, k * P:(k + 1) * P], ident[:, :])
                last.then_inc(s["xT_psum"].sem, 1)

            def mixture(s):
                L = LAYERS[s["kind"]]
                m = L["m"]
                E, nk = m.E, len(m.KS)

                def logits_back(g):
                    pe.wait_ge(*s["rl_copied"](g + 1))
                    for t in range(GT):
                        i = GT * g + t
                        last = pe.transpose(bank[7][:, i * E:(i + 1) * E], lgT[0:E, t * P:(t + 1) * P], ident[0:E, 0:E])
                    last.then_inc(s["lg_psum"].sem, 1)

                def logits(g):
                    pe.wait_ge(*s["xT"](GT * (g + 1)))
                    for k in range(KD):
                        last = pe.matmul(bank[6][0:E, :], L["router"][:, k, :], XT[:, k, g * GW:(g + 1) * GW],
                                         start=(k == 0), stop=(k == KD - 1))
                    last.then_inc(s["rl_psum"].sem, 1)

                def shared_up(first, end):
                    for n in range(first, end):
                        g, c = n // nk, n % nk
                        kp = m.KS[c]
                        if n >= 2:
                            pe.wait_ge(*s["hid"](n - 1))
                        for w, b in ((L["s1"], 2), (L["s3"], 4)):
                            for k in range(KD):
                                last = pe.matmul(bank[b + n % 2][0:kp, :], w[:, k, c * P:c * P + kp],
                                                 XT[:, k, g * GW:(g + 1) * GW], start=(k == 0), stop=(k == KD - 1))
                        last.then_inc(s["up"].sem, 1)

                def shared_down(g):
                    pe.wait_ge(*s["hid"](nk * (g + 1)))
                    for t in range(GT):
                        i = GT * g + t
                        if i >= 2:
                            pe.wait_ge(*s["shared_added"](i - 1))
                        for c, kp in enumerate(m.KS):
                            last = pe.matmul(bank[6 + i % 2][:, 0:D], f_HT[g % 3][0:kp, c, t * P:(t + 1) * P],
                                             L["s2"][0:kp, c, :], start=(c == 0), stop=(c == nk - 1))
                        last.then_inc(s["down"].sem, 1)

                def positions():
                    pe.wait_ge(*s["both"](1))
                    pos = bank[0][:, 0:(NTT + 1) * E]
                    marks = f_m16[:, 0:(NTT + 1) * E]
                    pe.matmul(pos, before16[:, :], marks, start=True, stop=False, skip_group_check=True)
                    for i in range(NTT):
                        n = NTT - i
                        last = pe.matmul(pos[:, (i + 1) * E:].rearrange("p (t e) -> p t e", e=E), ones16[:, :],
                                         marks[:, i * E:(i + 1) * E].unsqueeze(1).broadcast_to((P, n, E)),
                                         start=False, stop=(i == NTT - 1), skip_group_check=True)
                    last.then_inc(s["pos_psum"].sem, 1)

                def slot_tokens():
                    pe.wait_ge(*s["marks"](2))
                    for k in range(2):
                        for i in range(NTT):
                            last = pe.matmul(bank[1][:, k * m.TILES:(k + 1) * m.TILES], f_lo16[k][:, i, :],
                                             f_tok16[k][:, i, 0:m.TILES], start=(i == 0), stop=(i == NTT - 1))
                    last.then_inc(s["map_psum"].sem, 1)

                loaded(pe, s["kind"] + "_router")
                for g in range(NG):
                    for t in range(GT):
                        transpose_x(s, g, t)
                    if g:
                        logits_back(g - 1)
                    logits(g)
                logits_back(NG - 1)
                loaded(pe, s["kind"] + "_shared")
                shared_up(0, 2)
                positions()
                shared_up(2, 3 * nk)
                pe.wait_ge(*s["scored"](1))
                shared_down(0)
                slot_tokens()
                shared_up(3 * nk, 4 * nk)
                for g in range(1, NG):
                    shared_down(g)

                def xT(j, q, r):
                    pe.wait_ge(*s["row_in"][q](16 * (r + 1)))
                    if after(j, 2):
                        pe.wait_ge(*s["r_xT"](j - 1))
                    for k in range(KD):
                        last = pe.transpose(bank[q % 2][:, k * P:(k + 1) * P], xs[q][:, k * P:(k + 1) * P], ident[:, :])
                    last.then_inc(s["r_xT_psum"].sem, 1)

                held = {}

                def experts(j, n):
                    back = 2 if after(j, 2) else 0
                    _, held["e"] = nc.values_load_multi_w_load_instructions(
                        f_eid[0:1, bass.ds(j - back, n + back)], engines=(mybir.EngineType.PE,), min_val=0, max_val=E - 1,
                        skip_runtime_bounds_check_because="the vector engine has limited them to the experts")
                    held["first"] = j if known(j) else R - 2
                    held["back"] = back

                def expert(j, q, ago):
                    at = j - held["first"] if known(j) else (q + ago - held["first"]) % R - ago
                    return held["e"][at + held["back"]]

                def up(j, q, r):
                    e = expert(j, q, 0)
                    pe.wait_ge(*s["r_xT"](j + 1))
                    if after(j, 2):
                        pe.wait_ge(*s["r_hid"](j - 1))
                    for k in range(KD):
                        last = pe.matmul(bank[2 + q % 2][:, 0:2 * m.H], xsT[q % 2][:, k, :],
                                         L["w13"][:, k, bass.ds(e, 1), :], start=(k == 0), stop=(k == KD - 1))
                    last.then_inc(s["r_up"].sem, 1)

                def hid(j, q, r):
                    pe.wait_ge(*s["r_hid"](j + 1))
                    if after(j, 2):
                        pe.wait_ge(*s["r_hT"](j - 1))
                    for k, kp in enumerate(m.KH):
                        last = pe.transpose(bank[4 + q % 2][0:kp, k * P:(k + 1) * P],
                                            hh[q % 2][:, k * P:k * P + kp], ident[:, :])
                    last.then_inc(s["r_hT_psum"].sem, 1)

                def down(j, q, r):
                    e = expert(j, q, 2)
                    pe.wait_ge(*s["r_hT"](j + 1))
                    if after(j, 2):
                        pe.wait_ge(*s["r_y"](j - 1))
                    for k, kp in enumerate(m.KH):
                        last = pe.matmul(bank[6 + q % 2][:, 0:D], hT[q % 2][0:kp, k, :],
                                         L["w2"][k][:, bass.ds(e, 1), :], start=(k == 0), stop=(k == len(m.KH) - 1))
                    last.then_inc(s["r_down"].sem, 1)

                def step(j, q, r):
                    if not known(j) or j < m.TILES:
                        up(j, q, r)
                    if not known(j) or j + 2 < m.TILES:
                        xT(j + 2, (q + 2) % R, r if q < R - 2 else r + 1)
                    if after(j, 1) and (not known(j) or j - 1 < m.TILES):
                        hid(j - 1, (q - 1) % R, None)
                    if after(j, 2):
                        down(j - 2, (q - 2) % R, None)

                loaded(pe, s["kind"] + "_experts")
                pe.wait_ge(*s["experts"](1))
                xT(0, 0, 0)
                xT(1, 1, 0)
                rounds(pe, m.TILES, step, more=2, ahead=experts)

            def recurrence(s):
                loaded(pe, "h")

                def transpose_group(g):
                    for t in range(GT):
                        transpose_x(s, g, t, banks=1)

                def project(g):
                    pe.wait_ge(*s["xT"](GT * (g + 1)))
                    for c in range(KD):
                        n = KD * g + c
                        for k, (w, psum) in enumerate((("wf", s["f_psum"]), ("wi", s["i_psum"]), ("wg", s["g_psum"]))):
                            m = 3 * n + k
                            if m >= 4:
                                pe.wait_ge(*(s["in_"], s["t1"], s["gw"])[(m - 4) % 3]((m - 4) // 3 + 1))
                            for kk in range(KD):
                                last = pe.matmul(bank[2 + m % 4][:, :], hw[w][:, kk, c * P:(c + 1) * P],
                                                 XT[:, kk, g * GW:(g + 1) * GW], start=(kk == 0), stop=(kk == KD - 1))
                            last.then_inc(psum.sem, 1)
                            if g < 2 and k < 2:
                                transpose_x(s, g + 2, 2 * c + k, banks=1)
                        if c == 0 and g:
                            squares(g - 1)

                def squares(g):
                    if g == 2:
                        pe.wait_ge(*s["ms"](1))
                    pe.wait_ge(*s["sq"](KD * (g + 1)))
                    for t in range(GT):
                        for c in range(KD):
                            last = pe.matmul(bank[1][:, GT * g + t:GT * g + t + 1], g_sq[:, g % 2, c, t * P:(t + 1) * P], ones[:, 0:1],
                                             start=(c == 0), stop=(c == KD - 1))
                    last.then_inc(s["ms_psum"].sem, 1)

                def project_out(g):
                    pe.wait_ge(*s["t"](KD * (g + 1)))
                    for t in range(GT):
                        i = GT * g + t
                        if i >= 2:
                            pe.wait_ge(*s["x_new"](i - 1))
                        for c in range(KD):
                            last = pe.matmul(bank[6 + t % 2][:, 0:D], g_t[:, g % 2, c, t * P:(t + 1) * P], hw["wo"][:, c, :],
                                             start=(c == 0), stop=(c == KD - 1))
                        last.then_inc(s["o_psum"].sem, 1)

                transpose_group(0)
                transpose_group(1)
                for g in range(NG):
                    project(g)
                    if g >= 2:
                        project_out(g - 2)
                squares(NG - 1)
                project_out(NG - 2)
                project_out(NG - 1)

            def attention(s):
                loaded(pe, "a")

                def transpose_group(g):
                    for t in range(GT):
                        transpose_x(s, g, t, banks=1)

                def project(b, w, psum):
                    for c in range(KD):
                        for k in range(KD):
                            last = pe.matmul(bank[1][:, c * S:(c + 1) * S], aw[w][:, k, c * P:(c + 1) * P],
                                             XT[:, k, bass.ds(b * S, S)], start=(k == 0), stop=(k == KD - 1))
                    last.then_inc(psum.sem, 1)

                def queries(b):
                    pe.wait_ge(*s["xT"](BT * (b + 1)))
                    if after(b, 1):
                        pe.wait_ge(*s["k"](KD * b))
                    project(b, "wq", s["q_psum"])

                def keys(b):
                    pe.wait_ge(*s["q"](HEADS * (b + 1)))
                    project(b, "wk", s["k_psum"])

                def values(b, side):
                    pe.wait_ge(*s["xTb"](b + 1))
                    if after(b, 3):
                        pe.wait_ge(*s["x_new"](BT * (b - 2)))
                    for t in range(BT):
                        for k in range(KD):
                            last = pe.matmul(bank[7][:, t * D:(t + 1) * D], xTb[:, side, k, t * P:(t + 1) * P],
                                             aw["wv"][:, k, :], start=(k == 0), stop=(k == KD - 1))
                    last.then_inc(s["v_psum"].sem, 1)

                def scores(b, h, side):
                    n = HEADS * b + h
                    if h == 0:
                        pe.wait_ge(*s["k"](KD * (b + 1)))
                    if after(b, 1) or h >= 2:
                        pe.wait_ge(*s["exp"](BT * (n - 1)))
                    for q in range(BT):
                        last = pe.matmul(bank[2 + h % 2][:, q * S:(q + 1) * S], qz[:, side, h, q * P:(q + 1) * P],
                                         kT[:, side, h // 2, :], start=True, stop=True)
                    last.then_inc(s["s_psum"].sem, 1)

                def transpose_weights(b, h):
                    n = HEADS * b + h
                    pe.wait_ge(*s["pm"](BT * (n + 1)))
                    if after(b, 1) or h >= 2:
                        pe.wait_ge(*s["pT"](n - 1))
                    for k in range(BT):
                        for q in range(BT):
                            last = pe.transpose(bank[4 + h % 2][:, k * S + q * P:k * S + (q + 1) * P],
                                                pm[h % 2][:, q, k * P:(k + 1) * P], ident[:, :])
                    last.then_inc(s["pT_psum"].sem, 1)

                def features(b, h, side):
                    n = HEADS * b + h
                    pe.wait_ge(*s["pT"](n + 1))
                    if h == 0:
                        pe.wait_ge(*s["v"](2 * (b + 1)))
                    if h % 2 == 0 and (after(b, 1) or h):
                        pe.wait_ge(*s["fT"](KD * b + h // 2))
                    for k in range(BT):
                        last = pe.matmul(bank[6][:, (h // 2) * S:(h // 2 + 1) * S],
                                         vz[:, side, k, h * P:(h + 1) * P], pT[h % 2][:, k, :],
                                         start=(h % 2 == 0 and k == 0), stop=(h % 2 == 1 and k == BT - 1))
                    last.then_inc(s["f_psum"].sem, 1)

                def project_out(b, side):
                    pe.wait_ge(*s["fT"](KD * (b + 1)))
                    if not known(b) or b + 2 < B:
                        pe.wait_ge(*s["v"](2 * (b + 3)))
                    for t in range(BT):
                        for c in range(KD):
                            last = pe.matmul(bank[7][:, t * D:(t + 1) * D], fT[:, side, c, t * P:(t + 1) * P],
                                             aw["wo"][:, c, :], start=(c == 0), stop=(c == KD - 1))
                    last.then_inc(s["o_psum"].sem, 1)

                def step(b, side):
                    for h in range(HEADS):
                        here = not known(b) or b < B
                        ahead = not known(b) or b + 1 < B
                        if here:
                            scores(b, h, side)
                        if ahead and h == 0:
                            queries(b + 1)
                        if ahead and h == 1:
                            keys(b + 1)
                        if ahead and h == 2:
                            values(b + 1, 1 - side)
                        pb, ph = back(b, h, 2)
                        if (after(b, 1) or h >= 2) and (not known(b) or pb < B):
                            transpose_weights(pb, ph)
                        pb, ph = back(b, h, 3)
                        if (after(b, 1) or h >= 3) and (not known(b) or pb < B):
                            features(pb, ph, side if h >= 3 else 1 - side)
                        if h == 3 and after(b, 1):
                            project_out(b - 1, 1 - side)
                        if known(b) and b < 2:
                            transpose_x(s, 2 + b, h, banks=1)

                transpose_group(0)
                queries(0)
                keys(0)
                transpose_group(1)
                values(0, 0)
                sequences(pe, step)
                step(B, 0)

            for s in stages:
                if s["mixes"]:
                    mixture(s)
                elif s["kind"] == "h":
                    recurrence(s)
                else:
                    attention(s)

        @block.vector
        def _(dve):
            def x_tile(g, t):
                return X[:, bass.ds(GT * g + t, 1), :].rearrange("p a d -> p (a d)")

            def combine(s, g):
                dve.wait_ge(*s["y_in"][g](16 * (1 + KD)))
                for i in range(GT * g, GT * (g + 1)):
                    dve.wait_ge(*s["combined1"](i + 1))
                    x = X[:, i, :].rearrange("p (k d) -> p k d", k=KD)
                    dve.scalar_tensor_tensor(x, XT[:, :, i * P:(i + 1) * P], wts[:, 1, i:i + 1], x,
                                             ALU.mult, ALU.add).then_inc(s["x_new"].sem, 1)

            def moments(s, g):
                if s["prev"] is None:
                    dve.wait_ge(x_in[g], 16)
                else:
                    if s["prev"]["mixes"]:
                        combine(s["prev"], g)
                    dve.wait_ge(*s["prev"]["x_new"](GT * (g + 1)))
                for i in range(GT * g, GT * (g + 1)):
                    dve.bn_stats(st[:, i, :], X[:, i, :]).then_inc(s["stats"].sem, 1)
                for i in range(GT * g, GT * (g + 1)):
                    dve.wait_ge(*s["stats"](i + 1))
                    last = dve.bn_aggr(mv[:, i, :], st[:, i, :])
                last.then_inc(s["aggr"].sem, 1)

            def normalise(s, g):
                span = slice(GT * g, GT * (g + 1))
                dve.wait_ge(*s["stdev"](g + 1))
                dve.reciprocal(rs[:, span], sd[:, span]).then_inc(s["rstd"].sem, 1)
                dve.wait_ge(*s["rstd"](g + 1))
                for i in range(GT * g, GT * (g + 1)):
                    dve.tensor_scalar(XN[:, i, :], X[:, i, :], mv[:, i, 0:1], rs[:, i:i + 1],
                                      ALU.subtract, ALU.mult).then_inc(s["xn"].sem, 1)

            def norm(s, g):
                moments(s, g)
                normalise(s, g)

            def mixture(s):
                L = LAYERS[s["kind"]]
                m = L["m"]
                E, nk, NT = m.E, len(m.KS), m.TILES
                steps = [0]

                def chain(ins):
                    steps[0] += 1
                    ins.then_inc(s["route"].sem, 1)
                    dve.wait_ge(*s["route"](steps[0]))

                def by_expert(ap):
                    return ap[:, 0:NTT * E].rearrange("p (t e) -> p t e", e=E)

                score, sel, tmp, pos = (by_expert(x) for x in (f_score, f_sel, f_tmp, f_pos))
                oh = [by_expert(x) for x in f_oh]
                numbers = iota[:, 0:E]

                def over_experts(ap):
                    return ap.unsqueeze(2).broadcast_to((P, NTT, E))

                def choices():
                    dve.wait_ge(*s["scored"](1))
                    loaded(dve, s["kind"] + "_router")
                    chain(dve.tensor_tensor(sel, score, L["bias"][:, :].unsqueeze(1).broadcast_to((P, NTT, E)), ALU.add))
                    number = numbers.unsqueeze(1).broadcast_to((P, NTT, E))
                    for k in range(2):
                        top = f_top[:, k, :]
                        chain(dve.tensor_reduce(top, sel, AX.X, ALU.max))
                        chain(dve.tensor_tensor(tmp, sel, over_experts(top), ALU.is_equal))
                        chain(dve.scalar_tensor_tensor(tmp, number, float(E), tmp, ALU.subtract, ALU.mult))
                        chain(dve.tensor_reduce(f_sum, tmp, AX.X, ALU.min))
                        chain(dve.tensor_scalar(f_sum, f_sum, float(E), None, ALU.add))
                        chain(dve.tensor_tensor(oh[k], number, over_experts(f_sum), ALU.is_equal))
                        if k == 0:
                            chain(dve.scalar_tensor_tensor(sel, oh[0], -BIG, sel, ALU.mult, ALU.add))
                    chain(dve.memset(f_m16[:, NTT * E:(NTT + 1) * E], 0.0))
                    dve.tensor_tensor(f_m16[:, 0:NTT * E].rearrange("p (t e) -> p t e", e=E), oh[0], oh[1],
                                      ALU.add).then_inc(s["both"].sem, 1)

                def weights():
                    for k in range(2):
                        chain(dve.tensor_tensor(tmp, oh[k], score, ALU.mult))
                        chain(dve.tensor_reduce(f_top[:, k, :], tmp, AX.X, ALU.add))
                    chain(dve.tensor_tensor(f_sum, f_top[:, 0, :], f_top[:, 1, :], ALU.add))
                    if s["kind"] == "f0":
                        chain(dve.tensor_scalar(f_sum, f_sum, 1e-12, None, ALU.max))
                    else:
                        chain(dve.tensor_scalar(f_sum, f_sum, 1e-20, None, ALU.add))
                    chain(dve.reciprocal(f_sum, f_sum))
                    for k in range(2):
                        chain(dve.scalar_tensor_tensor(wts[:, k, :], f_top[:, k, :], 0.5, f_sum, ALU.mult, ALU.mult))

                def places():
                    dve.wait_ge(*s["pos_psum"](1))
                    p0 = bank[0][:, 0:NTT * E].rearrange("p (t e) -> p t e", e=E)
                    total = bank[0][:, NTT * E:(NTT + 1) * E]
                    tiles_i, tiles_f, cum, base = f_til[:, 0:E], f_tilf[:, 0:E], f_cum[:, 0:E], f_base[:, 0:E]
                    chain(dve.tensor_scalar(f_cnt[:, 0:E], total, float(P - 1), None, ALU.add))
                    chain(dve.tensor_scalar(tiles_i, f_cnt[:, 0:E], 7, None, ALU.arith_shift_right))
                    chain(dve.tensor_copy(tiles_f, tiles_i))
                    chain(dve.tensor_tensor_scan(cum, ones[:, 0:E], tiles_f, 0.0, ALU.mult, ALU.add))
                    chain(dve.tensor_tensor(base, cum, tiles_f, ALU.subtract))
                    chain(dve.tensor_scalar(base, base, float(P), None, ALU.mult))
                    chain(dve.tensor_tensor(pos, p0, base.unsqueeze(1).broadcast_to((P, NTT, E)), ALU.add))
                    for k in range(2):
                        chain(dve.tensor_tensor(tmp, oh[k], pos, ALU.mult))
                        chain(dve.tensor_reduce(f_slotf[:, k, :], tmp, AX.X, ALU.add))
                    flat = "p a b -> p (a b)"
                    si, sf = slots[:, :, :].rearrange(flat), f_slotf.rearrange(flat)
                    dve.tensor_copy(si, sf).then_inc(s["slotted"].sem, 1)

                def split_slots():
                    flat = "p a b -> p (a b)"
                    si = slots[:, :, :].rearrange(flat)
                    dve.wait_ge(*s["slotted"](1))
                    chain(dve.tensor_scalar(f_hi.rearrange(flat), si, 7, None, ALU.arith_shift_right))
                    chain(dve.tensor_scalar(f_lo.rearrange(flat), si, P - 1, None, ALU.bitwise_and))
                    chain(dve.tensor_copy(f_hif.rearrange(flat), f_hi.rearrange(flat)))
                    chain(dve.tensor_copy(f_lof.rearrange(flat), f_lo.rearrange(flat)))

                def mark(k):
                    chain(dve.tensor_tensor(f_hi16[k][:, :, 0:NT], iota[:, 0:NT].unsqueeze(1).broadcast_to((P, NTT, NT)),
                                            f_hif[:, k, :].unsqueeze(2).broadcast_to((P, NTT, NT)), ALU.is_equal))
                    chain(dve.tensor_tensor(f_tok16[k][:, :, 0:NT], f_hi16[k][:, :, 0:NT],
                                            tokens16[:, :].unsqueeze(2).broadcast_to((P, NTT, NT)), ALU.mult))
                    dve.tensor_tensor(f_lo16[k], iota[:, :].unsqueeze(1).broadcast_to((P, NTT, P)),
                                      f_lof[:, k, :].unsqueeze(2).broadcast_to((P, NTT, P)),
                                      ALU.is_equal).then_inc(s["marks"].sem, 1)

                def tile_experts():
                    ge = f_ge[:, 0:NT, 0:E]
                    chain(dve.tensor_tensor(ge, iota[0:1, 0:NT].unsqueeze(2).broadcast_to((1, NT, E)),
                                            f_cum[0:1, 0:E].unsqueeze(1).broadcast_to((1, NT, E)), ALU.is_ge))
                    chain(dve.tensor_reduce(f_eidf[:, 0:NT], ge, AX.X, ALU.add))
                    dve.tensor_scalar(f_eid[:, 0:NT], f_eidf[:, 0:NT], float(E - 1), None, ALU.min).then_inc(s["experts"].sem, 1)

                def rows():
                    dve.wait_ge(*s["map_psum"](1))
                    both = f_map[:, :, 0:NT]
                    full, empty, second = f_full[:, 0:NT], f_empty[:, 0:NT], f_second[:, 0:NT]
                    chain(dve.tensor_copy(both, bank[1][:, 0:2 * NT].rearrange("p (k j) -> p k j", k=2)))
                    chain(dve.tensor_tensor(full, both[:, 0, :], both[:, 1, :], ALU.add))
                    chain(dve.scalar_tensor_tensor(empty, full, 0.0, spare[:, 0:NT], ALU.is_equal, ALU.mult))
                    chain(dve.tensor_scalar(second, both[:, 1, :], 0.0, float(T), ALU.is_gt, ALU.mult))
                    chain(dve.scalar_tensor_tensor(full, full, -1.0, second, ALU.add, ALU.add))
                    dve.tensor_tensor(f_rows[:, 0:NT], full, empty, ALU.add).then_inc(s["rows"].sem, 1)

                def shared_hidden(first, end):
                    for n in range(first, end):
                        g, c = n // nk, n % nk
                        kp = m.KS[c]
                        dve.wait_ge(*s["silu"](n + 1))
                        if g >= 3:
                            dve.wait_ge(*s["down"](GT * (g - 2)))
                        dve.tensor_tensor(f_HT[g % 3][0:kp, c, :], f_sg[n % 2][0:kp, :], bank[4 + n % 2][0:kp, :],
                                          ALU.mult).then_inc(s["hid"].sem, 1)

                def shared_add(g):
                    for t in range(GT):
                        i = GT * g + t
                        dve.wait_ge(*s["down"](i + 1))
                        dve.scalar_tensor_tensor(X[:, i, :], bank[6 + i % 2][:, 0:D], 0.5, X[:, i, :],
                                                 ALU.mult, ALU.add).then_inc(s["shared_added"].sem, 1)

                moments(s, 0)
                moments(s, 1)
                for g in range(NG):
                    normalise(s, g)
                    if g + 2 < NG:
                        moments(s, g + 2)
                choices()
                shared_hidden(0, 1)
                places()
                split_slots()
                shared_hidden(1, 3)
                for k in range(2):
                    mark(k)
                    if nk > 1:
                        shared_hidden(3 + k, 4 + k)
                tile_experts()
                if nk > 1:
                    shared_hidden(5, 3 * nk)
                shared_add(0)
                shared_hidden(3 * nk, 4 * nk)
                rows()
                weights()
                for g in range(1, NG):
                    shared_add(g)
                dve.wait_ge(*s["shared_added"](NTT))
                assert steps[0] == ROUTE_STEPS, steps

                def hid(j, q, r):
                    dve.wait_ge(*s["r_silu"](j + 1))
                    if after(j, 2):
                        dve.wait_ge(*s["r_hT_psum"](j - 1))
                    dve.tensor_tensor(hh[q % 2][:, 0:m.H], sg[q % 2][:, 0:m.H], bank[2 + q % 2][:, m.H:2 * m.H],
                                      ALU.mult).then_inc(s["r_hid"].sem, 1)

                def hidT(j, q, r):
                    dve.wait_ge(*s["r_hT_psum"](j + 1))
                    if after(j, 2):
                        dve.wait_ge(*s["r_down"](j - 1))
                    for k, kp in enumerate(m.KH):
                        last = dve.tensor_copy(hT[q % 2][0:kp, k, :], bank[4 + q % 2][0:kp, k * P:(k + 1) * P])
                    last.then_inc(s["r_hT"].sem, 1)

                def step(j, q, r):
                    if after(j, 1):
                        hidT(j - 1, (q - 1) % R, None)
                    if not known(j) or j < NT:
                        hid(j, q, r)

                rounds(dve, NT, step, more=1)

            def recurrence(s):
                def front(g):
                    for c in range(KD):
                        n = KD * g + c
                        dve.wait_ge(*s["si"](n + 1))
                        dve.tensor_tensor(g_t1[c], g_si[c], bank[2 + (3 * n + 1) % 4][:, :], ALU.mult).then_inc(s["t1"].sem, 1)
                        dve.wait_ge(*s["t1"](n + 1))
                        dve.tensor_tensor(g_t1[c], g_t1[c], g_in[c], ALU.mult).then_inc(s["t2"].sem, 1)
                        dve.wait_ge(*s["t2"](n + 1))
                        for b in range(GW // S):
                            seq = slice(b * S, (b + 1) * S)
                            last = dve.tensor_tensor_scan(g_o[c][:, seq], g_keep[c][:, seq], g_t1[c][:, seq], 0.0,
                                                          ALU.mult, ALU.add)
                        last.then_inc(s["scan"].sem, 1)

                def back(g):
                    for c in range(KD):
                        n = KD * g + c
                        dve.wait_ge(*s["so"](n + 1))
                        dve.tensor_tensor(g_so[c], g_o[c], g_so[c], ALU.mult).then_inc(s["t3"].sem, 1)
                        dve.wait_ge(*s["t3"](n + 1))
                        dve.wait_ge(*s["gw"](n + 1))
                        if g >= 2:
                            dve.wait_ge(*s["o_psum"](GT * (g - 1)))
                        dve.tensor_tensor(g_t[:, g % 2, c, :], g_so[c], g_gw[c], ALU.mult).then_inc(s["t"].sem, 1)

                def scales(half):
                    span = slice(2 * GT * half, 2 * GT * (half + 1))
                    dve.wait_ge(*s["ms"](half + 1))
                    dve.reciprocal(g_rms[:, span], g_ms[:, span]).then_inc(s["rms"].sem, 1)
                    dve.wait_ge(*s["rms"](half + 1))

                def add_out(s, g):
                    for i in range(GT * g, GT * (g + 1)):
                        dve.wait_ge(*s["o_psum"](i + 1))
                        dve.scalar_tensor_tensor(X[:, i, :], bank[6 + i % 2][:, 0:D], g_rms[:, i:i + 1], X[:, i, :],
                                                 ALU.mult, ALU.add).then_inc(s["x_new"].sem, 1)

                moments(s, 0)
                for g in range(NG):
                    if g + 1 < NG:
                        moments(s, g + 1)
                    normalise(s, g)
                for g in range(NG):
                    front(g)
                    if g == 2:
                        scales(0)
                    if g >= 2:
                        add_out(s, g - 2)
                    back(g)
                scales(1)
                add_out(s, NG - 2)
                add_out(s, NG - 1)

            def attention(s):
                loaded(dve, "a")

                def rest(s, g):
                    normalise(s, g)
                    span = slice(GT * g, GT * (g + 1))
                    dve.wait_ge(*s["xn"](GT * (g + 1)))
                    dve.tensor_tensor(X[:, span, :], X[:, span, :], abo[:, :].unsqueeze(1).broadcast_to((P, GT, D)),
                                      ALU.add).then_inc(s["bo"].sem, 1)

                def values(b, side):
                    dve.wait_ge(*s["v_psum"](b + 1))
                    if after(b, 2):
                        dve.wait_ge(*s["f_psum"](HEADS * (b - 1)))
                    for p in range(2):
                        dve.tensor_tensor(
                            vz[:, side].rearrange("p t (c n) -> p t c n", c=KD)[:, :, :, p * (P + HD):p * (P + HD) + HD],
                            bank[7][:, :].rearrange("p (t c h d) -> p t c h d", t=BT, c=KD, h=2)[:, :, :, p, :],
                            abv[:, :].rearrange("p (c h d) -> p c h d", c=KD, h=2)[:, :, p, :]
                            .unsqueeze(1).broadcast_to((P, BT, KD, HD)), ALU.add).then_inc(s["v"].sem, 1)

                def maxima(b, h):
                    n = HEADS * b + h
                    dve.wait_ge(*s["s_psum"](n + 1))
                    dve.tensor_reduce(mx[h % 2], bank[2 + h % 2][:, :].rearrange("p (q n) -> p q n", q=BT),
                                      AX.X, ALU.max).then_inc(s["mx"].sem, 1)
                    dve.wait_ge(*s["mx"](n + 1))
                    if after(b, 1) or h >= 2:
                        dve.wait_ge(*s["exp"](BT * (n - 1)))
                    dve.tensor_scalar(nm[h % 2], mx[h % 2], -SCORE_SCALE, None, ALU.mult).then_inc(s["nm"].sem, 1)

                def weights(b, h):
                    n = HEADS * b + h
                    dve.wait_ge(*s["exp"](BT * (n + 1)))
                    dve.reciprocal(ri[h % 2], sm[h % 2]).then_inc(s["ri"].sem, 1)
                    dve.wait_ge(*s["ri"](n + 1))
                    for q in range(BT):
                        dve.tensor_scalar(pm[h % 2][:, q, :], pm[h % 2][:, q, :], ri[h % 2][:, q:q + 1], None,
                                          ALU.mult).then_inc(s["pm"].sem, 1)

                def add_out(b):
                    dve.wait_ge(*s["o_psum"](b + 1))
                    dve.wait_ge(*s["bo"](NG))
                    for t in range(BT):
                        x = X[:, bass.ds(BT * b + t, 1), :].rearrange("p a d -> p (a d)")
                        dve.tensor_tensor(x, bank[7][:, t * D:(t + 1) * D], x, ALU.add).then_inc(s["x_new"].sem, 1)

                def step(b, side):
                    for h in range(HEADS):
                        if h == 3 and (not known(b) or b + 1 < B):
                            values(b + 1, 1 - side)
                        if not known(b) or b < B:
                            maxima(b, h)
                        pb, ph = back(b, h, 1)
                        if (after(b, 1) or h >= 1) and (not known(b) or pb < B):
                            weights(pb, ph)
                        if known(b) and (b, h) == (0, 0):
                            moments(s, 3)
                        if known(b) and (b, h) == (0, 1):
                            rest(s, 3)
                    if after(b, 1):
                        add_out(b - 1)

                moments(s, 0)
                moments(s, 1)
                rest(s, 0)
                rest(s, 1)
                moments(s, 2)
                dve.wait_ge(zero_q, 2)
                values(0, 0)
                rest(s, 2)
                sequences(dve, step)
                step(B, 0)

            for s in stages:
                if s["mixes"]:
                    mixture(s)
                elif s["kind"] == "h":
                    recurrence(s)
                else:
                    attention(s)
            for g in range(NG):
                combine(stages[-1], g)


def constants():
    k = np.arange(P)
    return {
        "ident": np.eye(P, dtype=np.float32),
        "ones": np.ones((P, P), np.float32),
        "ones16": np.ones((P, P), np.float16),
        "before16": (k[:, None] < k[None, :]).astype(np.float16),
        "iota": np.broadcast_to(k.astype(np.float32), (P, P)).copy(),
        "tokens16": (1 + k[:, None] + P * np.arange(NTT)[None, :]).astype(np.float16),
        "spare": (2 * T + 1 + k[:, None] + P * np.arange(MOE1.TILES)[None, :]).astype(np.float32),
    }


def kernel(**inputs):
    import concourse.bacc as _bacc
    from concourse.bass_utils import run_bass_kernel_spmd as _run

    v = {k: np.asarray(x) for k, x in inputs.items()}

    def on_partitions(w):
        return np.ascontiguousarray(np.moveaxis(w.reshape(-1, P, *w.shape[1:]), 0, 1))

    def rows(w):
        n = -(-w.shape[0] // P)
        full = np.zeros((n * P, w.shape[1]), w.dtype)
        full[:w.shape[0]] = w
        return on_partitions(full)

    arrays = dict(constants())
    arrays["x"] = np.ascontiguousarray(v["L0_attn_hidden_states"].reshape(T, D))
    f0, f1, h, at = "L0_ffn_", "L1_ffn_", "L0_attn_", "L1_attn_"
    arrays["f0_router"] = on_partitions(v[f0 + "gate_w"].T)
    arrays["f0_bias"] = np.broadcast_to(v[f0 + "router_bias"], (P, MOE0.E)).copy()
    arrays["f0_w13"] = on_partitions(np.concatenate([v[f0 + "W1"], v[f0 + "W3"]], axis=2).transpose(1, 0, 2))
    arrays["f0_w2"] = np.ascontiguousarray(v[f0 + "W2"].transpose(1, 0, 2))
    arrays["f0_s1"] = on_partitions(v[f0 + "sw1"].T)
    arrays["f0_s3"] = on_partitions(v[f0 + "sw3"].T)
    arrays["f0_s2"] = rows(v[f0 + "sw2"].T)
    arrays["f1_router"] = on_partitions(v[f1 + "gate_w"])
    arrays["f1_bias"] = np.broadcast_to(v[f1 + "expert_bias"], (P, MOE1.E)).copy()
    arrays["f1_w13"] = on_partitions(v[f1 + "experts_gate_up"].transpose(1, 0, 2))
    arrays["f1_w2"] = np.ascontiguousarray(v[f1 + "experts_down"].transpose(1, 0, 2))
    arrays["f1_s1"] = on_partitions(v[f1 + "shared_gate_w"])
    arrays["f1_s3"] = on_partitions(v[f1 + "shared_up_w"])
    arrays["f1_s2"] = rows(v[f1 + "shared_down_w"])
    for n, src in (("wf", "Wf"), ("wi", "Wi"), ("wg", "Wg"), ("wo", "Wo")):
        arrays["h_" + n] = on_partitions(v[h + src].T)
    arrays["h_norm"] = np.ascontiguousarray(v[h + "g_norm_weight"].reshape(KD, P).T)
    for n in ("q", "k", "v", "o"):
        arrays["a_w" + n] = on_partitions(v[at + "W" + n])
    arrays["a_bq"] = np.ascontiguousarray(v[at + "bq"].reshape(KD, P).T)
    arrays["a_bk"] = np.ascontiguousarray(v[at + "bk"].reshape(KD, P).T)
    arrays["a_bv"] = np.broadcast_to(v[at + "bv"], (P, D)).copy()
    arrays["a_bo"] = np.broadcast_to(v[at + "bo"], (P, D)).copy()

    nc = _bacc.Bacc("TRN2", target_bir_lowering=False, num_devices=1)
    args = {n: nc.dram_tensor("in_" + n, x.shape, mybir.dt.from_np(x.dtype), kind="ExternalInput").ap()
            for n, x in arrays.items()}
    out = nc.dram_tensor("out_x", (T, D), F32, kind="ExternalOutput").ap()
    macaron_kernel(nc, args, out)
    r = _run(nc, [{"in_" + n: x for n, x in arrays.items()}], core_ids=[0])
    return r.results[0]["out_x"].reshape(B, S, D)
```
